# Optimizing a Trainium2 kernel written in Bass

```python
import numpy as np
import jax
import jax.numpy as jnp

def _softmax(x, axis=-1):
    return jax.nn.softmax(x, axis=axis)

def _gelu(x):
    return jax.nn.gelu(x, approximate=True)

def _silu(x):
    return jax.nn.silu(x)

def _sigmoid(x):
    return jax.nn.sigmoid(x)

def _layernorm(x, axis=-1, eps=1e-05):
    m = jnp.mean(x, axis=axis, keepdims=True)
    v = jnp.var(x, axis=axis, keepdims=True)
    return (x - m) / jnp.sqrt(v + eps)

def _scatter_add(tgt, idx, src, axis=0):
    return tgt.at[idx].add(src)

def _segment_sum(src, seg, n):
    return jax.ops.segment_sum(src, seg, n)
kernel_name = 'mk_gnn_preln_d4_gnn_r32_a82b2b'

def setup_inputs(seed: int=0):
    np.random.seed(seed)
    _w = jnp.asarray

    def _rec_inputs():
        import jax
        import jax.numpy as jnp
        _gk = jax.random.key(seed)
        x = -0.0003713 + 1 * jax.random.normal(jax.random.fold_in(_gk, 1), (3125, 256), jnp.float32)
        _s = jax.random.randint(jax.random.fold_in(_gk, 2), (25000,), 0, 3125, jnp.int32)
        _d = jax.random.randint(jax.random.fold_in(_gk, 3), (25000,), 0, 3125, jnp.int32)
        _loop = jnp.arange(3125, dtype=jnp.int32)
        src = jnp.concatenate([_s, _d, _loop])
        dst = jnp.concatenate([_d, _s, _loop])
        _o = jnp.argsort(dst, stable=True)
        src = src[_o]
        dst = dst[_o]
        edge_weight = jax.random.uniform(jax.random.fold_in(_gk, 13), (53125,), jnp.float32, 0.0, 1)
        return (x, src, dst, edge_weight)
    x, src, dst, edge_weight = _rec_inputs()

    def _L0_gnn_setup():
        import jax, jax.numpy as jnp
        import numpy as np
        N_NODES = 50000
        N_EDGES = 25000
        F_IN = 256
        HEADS = 4
        C_OUT = 64
        NEG_SLOPE = 0.2
        key = jax.random.key(seed)
        k0, k1, k2, k3, k4, k5 = jax.random.split(key, 6)
        x = jax.random.normal(k0, (N_NODES, F_IN), dtype=jnp.float32)
        edge_index = jax.random.randint(k1, (2, N_EDGES), 0, N_NODES, dtype=jnp.int64)
        s = 1.0 / np.sqrt(F_IN)
        W = jax.random.uniform(k2, (HEADS * C_OUT, F_IN), minval=-s, maxval=s, dtype=jnp.float32)
        att_src = jax.random.normal(k3, (HEADS, C_OUT), dtype=jnp.float32) * 0.1
        att_dst = jax.random.normal(k4, (HEADS, C_OUT), dtype=jnp.float32) * 0.1
        bias = jnp.zeros((HEADS * C_OUT,), dtype=jnp.float32)
        return {'x': x, 'edge_index': edge_index, 'W': W, 'att_src': att_src, 'att_dst': att_dst, 'bias': bias}
    _L0_gnn_all = _L0_gnn_setup()
    _L0_gnn_in = {k: v for k, v in _L0_gnn_all.items() if k in ('W', 'att_src', 'att_dst', 'bias')}
    del _L0_gnn_all

    def _L1_gnn_setup():
        import jax, jax.numpy as jnp
        import numpy as np
        N = 50000
        IN_CH = 256
        HEADS = 8
        OUT_CH = 32
        E = 25000
        key = jax.random.key(seed)
        k1, k2, k3, k4, k5 = jax.random.split(key, 5)
        x = jax.random.normal(k1, (N, IN_CH), dtype=jnp.float32)
        edge_index = jax.random.randint(k2, (2, E), 0, N, dtype=jnp.int64)
        W = jax.random.normal(k3, (HEADS * OUT_CH, IN_CH), dtype=jnp.float32) / np.sqrt(IN_CH)
        bound = float(np.sqrt(6.0 / (HEADS + OUT_CH)))
        attn_l = jax.random.uniform(k4, (1, HEADS, OUT_CH), minval=-bound, maxval=bound, dtype=jnp.float32)
        attn_r = jax.random.uniform(k5, (1, HEADS, OUT_CH), minval=-bound, maxval=bound, dtype=jnp.float32)
        return {'x': x, 'edge_index': edge_index, 'W': W, 'attn_l': attn_l, 'attn_r': attn_r}
    _L1_gnn_all = _L1_gnn_setup()
    _L1_gnn_in = {k: v for k, v in _L1_gnn_all.items() if k in ('W', 'attn_l', 'attn_r')}
    del _L1_gnn_all

    def _L2_gnn_setup():
        import jax, jax.numpy as jnp
        import numpy as np
        N_NODES = 50000
        N_EDGES = 25000
        F_IN = 256
        F_OUT = 64
        HEADS = 4
        LEAKY_ALPHA = 0.2
        key = jax.random.key(seed)
        ks = jax.random.split(key, 8)
        x = jax.random.normal(ks[0], (N_NODES, F_IN), dtype=jnp.float32)
        W = jax.random.normal(ks[1], (HEADS, F_IN, F_OUT), dtype=jnp.float32) * 0.05
        a_self = jax.random.normal(ks[2], (HEADS, F_OUT), dtype=jnp.float32) * 0.05
        a_neigh = jax.random.normal(ks[3], (HEADS, F_OUT), dtype=jnp.float32) * 0.05
        bias = jnp.zeros((HEADS, F_OUT), dtype=jnp.float32)
        adj_val = jnp.ones((N_EDGES,), dtype=jnp.float32)
        edge_row = jax.random.randint(ks[4], (N_EDGES,), 0, N_NODES, dtype=jnp.int32)
        edge_col = jax.random.randint(ks[5], (N_EDGES,), 0, N_NODES, dtype=jnp.int32)
        return {'x': x, 'W': W, 'a_self': a_self, 'a_neigh': a_neigh, 'bias': bias, 'adj_val': adj_val, 'edge_row': edge_row, 'edge_col': edge_col}
    _L2_gnn_all = _L2_gnn_setup()
    _L2_gnn_in = {k: v for k, v in _L2_gnn_all.items() if k in ('W', 'a_self', 'a_neigh', 'bias')}
    del _L2_gnn_all

    def _L3_gnn_setup():
        import jax, jax.numpy as jnp
        import numpy as np
        N = 50000
        E = 15625
        CH = 256
        H1, C1 = (4, 64)
        H2, C2 = (8, 32)
        CONCAT = H1 * C1 + H2 * C2

        def _layer_norm(x, gamma, beta, eps=1e-05):
            mu = jnp.mean(x, axis=-1, keepdims=True)
            var = jnp.var(x, axis=-1, keepdims=True)
            return (x - mu) * jax.lax.rsqrt(var + eps) * gamma + beta

        def _gat_conv(x, src, dst, W, a_src, a_dst, bias, heads, out_ch, n_nodes):
            h = (x @ W).reshape(n_nodes, heads, out_ch)
            alpha_s = jnp.einsum('nhc,hc->nh', h, a_src)
            alpha_d = jnp.einsum('nhc,hc->nh', h, a_dst)
            e = jax.nn.leaky_relu(alpha_s[src] + alpha_d[dst], negative_slope=0.2)
            m = jax.ops.segment_max(e, dst, num_segments=n_nodes)
            ex = jnp.exp(e - m[dst])
            denom = jax.ops.segment_sum(ex, dst, num_segments=n_nodes)
            a = ex / (denom[dst] + 1e-16)
            msg = h[src] * a[:, :, None]
            out = jax.ops.segment_sum(msg, dst, num_segments=n_nodes)
            return out.reshape(n_nodes, heads * out_ch) + bias
        key = jax.random.key(seed)
        ks = jax.random.split(key, 16)
        s = 0.05
        x = jax.random.normal(ks[0], (N, CH), dtype=jnp.float32)
        edge_index = jax.random.randint(ks[1], (2, E), 0, N, dtype=jnp.int64)
        return {'x': x, 'edge_index': edge_index, 'gamma': jnp.ones((CH,), jnp.float32), 'beta': jnp.zeros((CH,), jnp.float32), 'W1': jax.random.normal(ks[2], (CH, H1 * C1), jnp.float32) * s, 'a_src1': jax.random.normal(ks[3], (H1, C1), jnp.float32) * s, 'a_dst1': jax.random.normal(ks[4], (H1, C1), jnp.float32) * s, 'b1': jnp.zeros((H1 * C1,), jnp.float32), 'W2': jax.random.normal(ks[5], (CH, H2 * C2), jnp.float32) * s, 'a_src2': jax.random.normal(ks[6], (H2, C2), jnp.float32) * s, 'a_dst2': jax.random.normal(ks[7], (H2, C2), jnp.float32) * s, 'b2': jnp.zeros((H2 * C2,), jnp.float32), 'Wu': jax.random.normal(ks[8], (CONCAT, CH), jnp.float32) * s, 'bu': jnp.zeros((CH,), jnp.float32)}
    _L3_gnn_all = _L3_gnn_setup()
    _L3_gnn_in = {k: v for k, v in _L3_gnn_all.items() if k in ('gamma', 'beta', 'W1', 'a_src1', 'a_dst1', 'b1', 'W2', 'a_src2', 'a_dst2', 'b2', 'Wu', 'bu')}
    del _L3_gnn_all
    return {'x': x, 'src': src, 'dst': dst, 'edge_weight': edge_weight, 'L0_gnn_W': _L0_gnn_in['W'], 'L0_gnn_att_src': _L0_gnn_in['att_src'], 'L0_gnn_att_dst': _L0_gnn_in['att_dst'], 'L0_gnn_bias': _L0_gnn_in['bias'], 'L1_gnn_W': _L1_gnn_in['W'], 'L1_gnn_attn_l': _L1_gnn_in['attn_l'], 'L1_gnn_attn_r': _L1_gnn_in['attn_r'], 'L2_gnn_W': _L2_gnn_in['W'], 'L2_gnn_a_self': _L2_gnn_in['a_self'], 'L2_gnn_a_neigh': _L2_gnn_in['a_neigh'], 'L2_gnn_bias': _L2_gnn_in['bias'], 'L3_gnn_gamma': _L3_gnn_in['gamma'], 'L3_gnn_beta': _L3_gnn_in['beta'], 'L3_gnn_W1': _L3_gnn_in['W1'], 'L3_gnn_a_src1': _L3_gnn_in['a_src1'], 'L3_gnn_a_dst1': _L3_gnn_in['a_dst1'], 'L3_gnn_b1': _L3_gnn_in['b1'], 'L3_gnn_W2': _L3_gnn_in['W2'], 'L3_gnn_a_src2': _L3_gnn_in['a_src2'], 'L3_gnn_a_dst2': _L3_gnn_in['a_dst2'], 'L3_gnn_b2': _L3_gnn_in['b2'], 'L3_gnn_Wu': _L3_gnn_in['Wu'], 'L3_gnn_bu': _L3_gnn_in['bu']}

def reference(x, src, dst, edge_weight, L0_gnn_W, L0_gnn_att_src, L0_gnn_att_dst, L0_gnn_bias, L1_gnn_W, L1_gnn_attn_l, L1_gnn_attn_r, L2_gnn_W, L2_gnn_a_self, L2_gnn_a_neigh, L2_gnn_bias, L3_gnn_gamma, L3_gnn_beta, L3_gnn_W1, L3_gnn_a_src1, L3_gnn_a_dst1, L3_gnn_b1, L3_gnn_W2, L3_gnn_a_src2, L3_gnn_a_dst2, L3_gnn_b2, L3_gnn_Wu, L3_gnn_bu):
    import jax
    import jax.numpy as jnp

    def _L0_gnn_ref(x, edge_index, W, att_src, att_dst, bias):
        import jax, jax.numpy as jnp
        import numpy as np
        N_NODES = 50000
        N_EDGES = 25000
        F_IN = 256
        HEADS = 4
        C_OUT = 64
        NEG_SLOPE = 0.2
        N = x.shape[0]
        H, C = att_src.shape
        loops = jnp.arange(N, dtype=edge_index.dtype)
        src = jnp.concatenate([edge_index[0], loops])
        dst = jnp.concatenate([edge_index[1], loops])
        h = (x @ W.T).reshape(N, H, C)
        a_s = jnp.einsum('nhc,hc->nh', h, att_src)
        a_d = jnp.einsum('nhc,hc->nh', h, att_dst)
        e = jax.nn.leaky_relu(a_s[src] + a_d[dst], NEG_SLOPE)
        m = jax.ops.segment_max(e, dst, num_segments=N)
        m = jnp.where(jnp.isfinite(m), m, 0.0)
        p = jnp.exp(e - m[dst])
        denom = jax.ops.segment_sum(p, dst, num_segments=N)
        alpha = p / (denom[dst] + 1e-16)
        msg = alpha[:, :, None] * h[src]
        out = jax.ops.segment_sum(msg, dst, num_segments=N)
        out = out.reshape(N, H * C) + bias
        out = jax.nn.elu(out) + x
        return out

    def _L1_gnn_ref(x, edge_index, W, attn_l, attn_r):
        import jax, jax.numpy as jnp
        import numpy as np
        N = 50000
        IN_CH = 256
        HEADS = 8
        OUT_CH = 32
        E = 25000
        num_nodes = x.shape[0]
        xp = (x @ W.T).reshape(num_nodes, HEADS, OUT_CH).astype(jnp.float32)
        loops = jnp.arange(num_nodes, dtype=edge_index.dtype)
        src = jnp.concatenate([edge_index[0], loops])
        dst = jnp.concatenate([edge_index[1], loops])
        alpha_l = (xp * attn_l).sum(-1)[src]
        alpha_r = (xp * attn_r).sum(-1)[dst]
        alpha = jax.nn.leaky_relu(alpha_l + alpha_r, negative_slope=0.2)
        alpha = jnp.exp(alpha - alpha.max(axis=0, keepdims=True))
        alpha_sum = jax.ops.segment_sum(alpha, dst, num_segments=num_nodes)
        alpha = alpha / jnp.maximum(alpha_sum[dst], 1e-06)
        msgs = alpha[:, :, None] * xp[src]
        out = jax.ops.segment_sum(msgs, dst, num_segments=num_nodes)
        return out.reshape(num_nodes, HEADS * OUT_CH)

    def _L2_gnn_ref(x, W, a_self, a_neigh, bias, adj_val, edge_row, edge_col):
        import jax, jax.numpy as jnp
        import numpy as np
        N_NODES = 50000
        N_EDGES = 25000
        F_IN = 256
        F_OUT = 64
        HEADS = 4
        LEAKY_ALPHA = 0.2
        N = x.shape[0]
        feats = jnp.einsum('nf,hfo->hno', x, W)
        s_self = jnp.einsum('hno,ho->hn', feats, a_self)
        s_neigh = jnp.einsum('hno,ho->hn', feats, a_neigh)
        z = s_self[:, edge_row] + s_neigh[:, edge_col]
        e = jnp.where(z > 0, z, LEAKY_ALPHA * z) * adj_val[None, :]

        def seg_softmax(e_h):
            m = jax.ops.segment_max(e_h, edge_row, num_segments=N)
            ex = jnp.exp(e_h - m[edge_row])
            s = jax.ops.segment_sum(ex, edge_row, num_segments=N)
            return ex / s[edge_row]
        alpha = jax.vmap(seg_softmax)(e)

        def aggregate(alpha_h, feat_h):
            return jax.ops.segment_sum(alpha_h[:, None] * feat_h[edge_col], edge_row, num_segments=N)
        out = jax.vmap(aggregate)(alpha, feats) + bias[:, None, :]
        out = jnp.transpose(out, (1, 0, 2)).reshape(N, -1)
        return jax.nn.relu(out)

    def _L3_gnn_ref(x, edge_index, gamma, beta, W1, a_src1, a_dst1, b1, W2, a_src2, a_dst2, b2, Wu, bu):
        import jax, jax.numpy as jnp
        import numpy as np
        N = 50000
        E = 15625
        CH = 256
        H1, C1 = (4, 64)
        H2, C2 = (8, 32)
        CONCAT = H1 * C1 + H2 * C2

        def _layer_norm(x, gamma, beta, eps=1e-05):
            mu = jnp.mean(x, axis=-1, keepdims=True)
            var = jnp.var(x, axis=-1, keepdims=True)
            return (x - mu) * jax.lax.rsqrt(var + eps) * gamma + beta

        def _gat_conv(x, src, dst, W, a_src, a_dst, bias, heads, out_ch, n_nodes):
            h = (x @ W).reshape(n_nodes, heads, out_ch)
            alpha_s = jnp.einsum('nhc,hc->nh', h, a_src)
            alpha_d = jnp.einsum('nhc,hc->nh', h, a_dst)
            e = jax.nn.leaky_relu(alpha_s[src] + alpha_d[dst], negative_slope=0.2)
            m = jax.ops.segment_max(e, dst, num_segments=n_nodes)
            ex = jnp.exp(e - m[dst])
            denom = jax.ops.segment_sum(ex, dst, num_segments=n_nodes)
            a = ex / (denom[dst] + 1e-16)
            msg = h[src] * a[:, :, None]
            out = jax.ops.segment_sum(msg, dst, num_segments=n_nodes)
            return out.reshape(n_nodes, heads * out_ch) + bias
        n = x.shape[0]
        loop = jnp.arange(n, dtype=edge_index.dtype)
        src = jnp.concatenate([edge_index[0], loop])
        dst = jnp.concatenate([edge_index[1], loop])
        residual = x
        x_norm = _layer_norm(x, gamma, beta)
        out1 = _gat_conv(x_norm, src, dst, W1, a_src1, a_dst1, b1, H1, C1, n)
        out2 = _gat_conv(x_norm, src, dst, W2, a_src2, a_dst2, b2, H2, C2, n)
        x_cat = jax.nn.elu(jnp.concatenate([out1, out2], axis=-1))
        unified = x_cat @ Wu + bu
        return residual + unified
    edge_index = jnp.stack([src, dst])
    h = jnp.maximum(_layernorm(x, axis=-1), 0.0)
    x = x + _L0_gnn_ref(h, edge_index, L0_gnn_W, L0_gnn_att_src, L0_gnn_att_dst, L0_gnn_bias)
    h = jnp.maximum(_layernorm(x, axis=-1), 0.0)
    x = x + _L1_gnn_ref(h, edge_index, L1_gnn_W, L1_gnn_attn_l, L1_gnn_attn_r)
    h = jnp.maximum(_layernorm(x, axis=-1), 0.0)
    x = x + _L2_gnn_ref(h, L2_gnn_W, L2_gnn_a_self, L2_gnn_a_neigh, L2_gnn_bias, edge_weight, src, dst)
    h = jnp.maximum(_layernorm(x, axis=-1), 0.0)
    x = x + _L3_gnn_ref(h, edge_index, L3_gnn_gamma, L3_gnn_beta, L3_gnn_W1, L3_gnn_a_src1, L3_gnn_a_dst1, L3_gnn_b1, L3_gnn_W2, L3_gnn_a_src2, L3_gnn_a_dst2, L3_gnn_b2, L3_gnn_Wu, L3_gnn_bu)
    return x

_drawn_inputs = setup_inputs


def setup_inputs(seed=0):
    import zlib

    import numpy as np

    out = dict(_drawn_inputs(seed))
    spreads = {'L0_gnn_bias': (0.0, 0.1),
     'L2_gnn_bias': (0.0, 0.1),
     'L3_gnn_gamma': (1.0, 0.6),
     'L3_gnn_beta': (0.0, 0.1),
     'L3_gnn_b1': (0.0, 0.268),
     'L3_gnn_b2': (0.0, 0.29),
     'L3_gnn_bu': (0.0, 0.1)}
    factors = {'edge_weight': 8.0,
     'L0_gnn_att_src': 8.0,
     'L0_gnn_att_dst': 8.0,
     'L2_gnn_a_self': 8.0,
     'L2_gnn_a_neigh': 8.0,
     'L3_gnn_a_src1': 3.967,
     'L3_gnn_a_dst1': 8.0,
     'L3_gnn_a_src2': 4.875,
     'L3_gnn_a_dst2': 8.0}
    for name, (base, spread) in spreads.items():
        noise = np.random.default_rng([zlib.crc32(name.encode()), seed]).standard_normal(out[name].shape)
        drawn = base * np.exp(spread * noise) if base else spread * noise
        out[name] = jnp.asarray(drawn.astype(out[name].dtype))
    for name, factor in factors.items():
        out[name] = (out[name] * factor).astype(out[name].dtype)
    return out
```

```python
from contextlib import ExitStack

import concourse.bass as bass
from concourse import mybir

F32 = mybir.dt.float32
BF16 = mybir.dt.bfloat16
I32 = mybir.dt.int32
ALU = mybir.AluOpType
ACT = mybir.ActivationFunctionType
X = mybir.AxisListType.X

P = 128
CH = 256
LO = 128
LOWEST = -3.0e38
PAD_KEY = 4095
FAR = float(1 << 23) * 1.5
EPS = 1e-5


class Signal:

    def __init__(self, sem):
        self.sem = sem
        self.base = 0

    def at(self, n):
        return self.base + n


class Graph:

    def __init__(self, name, edges, nodes, loops):
        self.name = name
        self.tiles = -(-nodes // P)
        self.edge_cols = -(-edges // P)
        self.loop_cols = self.tiles if loops else 0
        self.cols = -(-(self.edge_cols + self.loop_cols) // 8) * 8
        real = edges + (nodes if loops else 0)
        self.slots = -(-((real + self.tiles * (P - 1)) // P) // 8) * 8
        self.rows = self.slots // 4


def build(nc, A, out):
    x_in = A["x"]
    N = x_in.shape[0]
    E = A["src"].shape[0]
    T = -(-N // P)
    NT = T * P
    LAST = N - (T - 1) * P

    ctx = ExitStack()
    with ctx:
        signals = {}

        def sig(name):
            if name not in signals:
                signals[name] = Signal(ctx.enter_context(nc.semaphore(name)))
            return signals[name]

        used = {}

        def numbered(name):
            used[name] = used.get(name, 0) + 1
            return f"{name}.{used[name]}"

        def sb(name, shape, dt=F32, c=ctx):
            return c.enter_context(nc.sbuf_tensor(numbered(name), shape, dt))

        def ps(name, shape, dt, c):
            return c.enter_context(nc.psum_tensor(numbered(name), shape, dt))

        by_dst = Graph("by_dst", E, N, True)
        by_src = Graph("by_src", E, N, False)

        iota_row = sb("iota_row", [P, P])
        iota_col = sb("iota_col", [P, 1])
        ident = sb("ident", [P, P])
        identb = sb("identb", [P, P], BF16)
        ones = sb("ones", [P, P])
        onesb = sb("onesb", [P, P], BF16)
        n128b = sb("n128b", [P, P], BF16)
        before = sb("before", [P, P])
        notbefore = sb("notbefore", [P, 4, P], BF16)
        xres = sb("xres", [P, T, CH])
        hres = sb("hres", [P, T, CH])
        for g in (by_dst, by_src):
            g.klo = sb(f"{g.name}_klo", [P, g.slots])
            g.key = sb(f"{g.name}_key", [P, g.slots], I32)
            g.other = sb(f"{g.name}_other", [P, g.slots], I32)
            g.negfirst = sb(f"{g.name}_negfirst", [g.rows, 4 * P])
            g.neglast = sb(f"{g.name}_neglast", [g.rows, 4 * P])
            g.negnew = sb(f"{g.name}_negnew", [g.rows, 4 * P])
            g.negnewb = sb(f"{g.name}_negnewb", [g.rows, 4 * P])
            g.negcont = sb(f"{g.name}_negcont", [8, g.rows + 1])
            g.negthru = sb(f"{g.name}_negthru", [8, g.rows])
            g.negthrub = sb(f"{g.name}_negthrub", [8, g.rows])
            g.tile_of = sb(f"{g.name}_tile_of", [1, g.slots], I32)
        by_src.w = sb("edge_w", [P, by_src.slots])

        made, made2, loaded = sig("const_made"), sig("const_made2"), sig("x_loaded")
        with ExitStack() as c, nc.Block() as block:
            ii = sb("iota_i", [P, P], I32, c)
            ic = sb("iota_ci", [P, 1], I32, c)

            @block.gpsimd
            def _(pool):
                pool.iota(ii[:, :], [[1, P]], base=0, channel_multiplier=0).then_inc(made.sem, 1)
                pool.iota(ic[:, :], [[1, 1]], base=0, channel_multiplier=1).then_inc(made.sem, 1)

            @block.vector
            def _(dve):
                dve.memset(ones[:, :], 1.0)
                dve.memset(onesb[:, :], 1.0)
                dve.memset(n128b[:, :], 128.0)
                dve.memset(xres[:, T - 1, :], 0.0).then_inc(made2.sem, 1)
                dve.wait_ge(made.sem, 2)
                dve.tensor_copy(iota_row[:, :], ii[:, :]).then_inc(made2.sem, 1)
                dve.tensor_copy(iota_col[:, :], ic[:, :]).then_inc(made2.sem, 1)
                dve.wait_ge(made2.sem, 3)
                dve.tensor_scalar(ident[:, :], iota_row[:, :], iota_col[:, 0:1], None, ALU.is_equal)
                dve.tensor_scalar(identb[:, :], iota_row[:, :], iota_col[:, 0:1], None, ALU.is_equal)
                dve.tensor_scalar(before[:, :], iota_row[:, :], iota_col[:, 0:1], None, ALU.is_gt)
                for j in range(4):
                    dve.tensor_scalar(notbefore[:, j, :], iota_row[:, :], iota_col[:, 0:1], 4096.0,
                                      ALU.is_ge, ALU.mult)

            @block.sync
            def _(sp):
                sp.dma_start(xres[:, 0:T - 1, :], x_in[0:(T - 1) * P, :].rearrange("(t p) f -> p t f", p=P)).then_inc(loaded.sem, 16)
                sp.wait_ge(made2.sem, 1)
                sp.dma_start(xres[0:LAST, T - 1, :], x_in[(T - 1) * P:N, :]).then_inc(loaded.sem, 16)
                sp.wait_ge(loaded.sem, 32)
        made.base, made2.base, loaded.base = 2, 3, 32

        sort_edges(nc, sig, sb, ps, by_dst, A["dst"], A["src"], None, N, T, locals())
        sort_edges(nc, sig, sb, ps, by_src, A["src"], A["dst"], A["edge_weight"], N, T, locals())

        K = dict(iota_row=iota_row, ident=ident, ones=ones, xres=xres, hres=hres, N=N, T=T, NT=NT, LAST=LAST)

        gat_layer(nc, sig, sb, ps, A, K, 0, by_dst,
                  [("L0", 4, A["L0_gnn_W"], "out_in", A["L0_gnn_att_src"], A["L0_gnn_att_dst"])], out)
        gat_layer(nc, sig, sb, ps, A, K, 1, by_dst,
                  [("L1", 8, A["L1_gnn_W"], "out_in", A["L1_gnn_attn_l"].rearrange("a h c -> (a h) c"),
                    A["L1_gnn_attn_r"].rearrange("a h c -> (a h) c"))], out)
        gat_layer(nc, sig, sb, ps, A, K, 2, by_src,
                  [("L2", 4, A["L2_gnn_W"], "head_in_out", A["L2_gnn_a_neigh"], A["L2_gnn_a_self"])], out)
        gat_layer(nc, sig, sb, ps, A, K, 3, by_dst,
                  [("L3a", 4, A["L3_gnn_W1"], "in_out", A["L3_gnn_a_src1"], A["L3_gnn_a_dst1"]),
                   ("L3b", 8, A["L3_gnn_W2"], "in_out", A["L3_gnn_a_src2"], A["L3_gnn_a_dst2"])], out)


def sort_edges(nc, sig, sb, ps, g, key_in, other_in, w_in, N, T, C):
    E = key_in.shape[0]
    EC, COLS, SLOTS, R = g.edge_cols, g.cols, g.slots, g.rows
    FULL, REST = E // EC, E % EC
    B = 4
    iota_row, iota_col, ident, identb = C["iota_row"], C["iota_col"], C["ident"], C["identb"]
    ones, onesb, n128b, before, notbefore = C["ones"], C["onesb"], C["n128b"], C["before"], C["notbefore"]
    records = nc.dram_tensor(f"{g.name}_records", [SLOTS * P, 4], I32, kind="Internal").ap()

    with ExitStack() as c:
        key = sb("k_key", [P, COLS], I32, c)
        keylo_i = sb("k_lo_i", [P, COLS], I32, c)
        keyhi_i = sb("k_hi_i", [P, COLS], I32, c)
        klo = sb("k_lo", [P, COLS], F32, c)
        khi = sb("k_hi", [P, COLS], F32, c)
        keyf = sb("k_f", [P, COLS], F32, c)
        rec = sb("k_rec", [P, COLS, 4], I32, c)
        oth = sb("k_other", [P, COLS], I32, c)
        wts = sb("k_w", [P, COLS], F32, c) if w_in is not None else None
        pad_far = sb("k_far", [P, COLS], F32, c)
        blank = sb("k_blank", [P, SLOTS, 4], I32, c)
        ld, lds, prep = sig("sort_loaded"), sig("sort_stored"), sig("sort_prepared")
        init = sig("sort_init")

        with nc.Block() as block:
            @block.vector
            def _(dve):
                dve.memset(key[:, :], PAD_KEY).then_inc(init.sem, 1)
                dve.memset(rec[:, :, :], 0)
                if w_in is not None:
                    dve.memset(wts[:, :], 0.0)
                dve.memset(oth[:, :], 0).then_inc(init.sem, 1)
                dve.memset(blank[:, :, :], 0).then_inc(init.sem, 1)
                dve.wait_ge(init.sem, init.at(3))
                dve.memset(blank[:, :, 1:2].bitcast(F32), -1.0).then_inc(init.sem, 1)

            n_loads = 4 + (2 if w_in is not None else 0)

            @block.sync
            def _(sp):
                sp.wait_ge(init.sem, init.at(2))
                loads = [(key[:, 0:EC], key_in), (oth[:, 0:EC], other_in)]
                if w_in is not None:
                    loads.append((wts[:, 0:EC], w_in))
                for dst, src in loads:
                    sp.dma_start(dst[0:FULL, :], src[0:FULL * EC].rearrange("(p c) -> p c", c=EC)).then_inc(ld.sem, 16)
                    sp.dma_start(dst[FULL:FULL + 1, 0:REST], src[FULL * EC:E].rearrange("(p c) -> p c", p=1)).then_inc(ld.sem, 16)
                sp.wait_ge(init.sem, init.at(4))
                sp.dma_start(records.rearrange("(k s) f -> k s f", k=P), blank[:, :, :]).then_inc(lds.sem, 16)
                sp.wait_ge(ld.sem, ld.at(16 * n_loads))
                sp.wait_ge(lds.sem, lds.at(16))

            @block.gpsimd
            def _(pool):
                if g.loop_cols:
                    pool.wait_ge(init.sem, init.at(2))
                    pool.iota(key[:, EC:EC + T], [[P, T]], base=0, channel_multiplier=1)
                    pool.iota(oth[:, EC:EC + T], [[P, T]], base=0, channel_multiplier=1)
        init.base += 4
        ld.base += 16 * n_loads
        lds.base += 16

        with nc.Block() as block:
            @block.vector
            def _(dve):
                n = [0]

                def link(ins):
                    n[0] += 1
                    ins.then_inc(prep.sem, 1)
                    dve.wait_ge(prep.sem, prep.at(n[0]))

                link(dve.tensor_copy(keyf[:, :], key[:, :]))
                if g.loop_cols:
                    link(dve.tensor_scalar(pad_far[:, :], keyf[:, :], float(N), float(PAD_KEY + 1), ALU.is_ge, ALU.mult))
                    link(dve.tensor_tensor(keyf[:, :], keyf[:, :], pad_far[:, :], ALU.add))
                    link(dve.tensor_scalar(keyf[:, :], keyf[:, :], float(PAD_KEY), None, ALU.min))
                    link(dve.tensor_copy(key[:, :], keyf[:, :]))
                link(dve.tensor_scalar(keylo_i[:, :], key[:, :], 127, None, ALU.bitwise_and))
                link(dve.tensor_scalar(keyhi_i[:, :], key[:, :], 7, None, ALU.logical_shift_right))
                link(dve.tensor_copy(klo[:, :], keylo_i[:, :]))
                link(dve.tensor_copy(khi[:, :], keyhi_i[:, :]))
                link(dve.tensor_scalar(pad_far[:, :], khi[:, :], float(T), FAR, ALU.is_ge, ALU.mult))
                link(dve.tensor_copy(rec[:, :, 1].bitcast(F32), klo[:, :]))
                link(dve.tensor_copy(rec[:, :, 2], key[:, :]))
                link(dve.tensor_copy(rec[:, :, 0], oth[:, :]))
                if w_in is not None:
                    link(dve.tensor_copy(rec[:, :, 3].bitcast(F32), wts[:, :]))
                prep.base += n[0]

        table = sb("k_table", [P, 2, B + 1, T], F32, c)
        hot, hist, cnt = sig("hist_onehots"), sig("hist_counted"), sig("hist_steps")
        with ExitStack() as c2, nc.Block() as block:
            ohlo = sb("h_lo", [P, 2, B, P], BF16, c2)
            ohhi = sb("h_hi", [P, 2, B, T], BF16, c2)
            zero = sb("h_zero", [P, P], BF16, c2)
            counts = sb("h_counts", [P, T], F32, c2)
            tot = sb("h_tot", [P, T], F32, c2)
            toti = sb("h_toti", [P, T], I32, c2)
            nslot = sb("h_nslot", [P, T], F32, c2)
            end = sb("h_end", [P, T], F32, c2)
            zrow = sb("h_zrow", [P, T], F32, c2)
            start = sb("h_start", [P, T], F32, c2)
            slot_i = sb("h_sloti", [1, SLOTS], I32, c2)
            slot_f = sb("h_slotf", [1, SLOTS], F32, c2)
            ge = sb("h_ge", [1, SLOTS, T], F32, c2)
            tf = sb("h_tf", [1, SLOTS], F32, c2)
            pc = ps("h_ps", [P, 512], F32, c2)
            px = ps("h_px", [P, 2, 32], F32, c2)
            NB2 = COLS // (2 * B)
            zm = sig("hist_zero")

            @block.gpsimd
            def _(pool):
                pool.iota(slot_i[:, :], [[1, SLOTS]], base=0, channel_multiplier=0).then_inc(zm.sem, 1)

            @block.vector
            def _(dve):
                dve.memset(zero[:, :], 0.0).then_inc(zm.sem, 1)
                dve.memset(zrow[:, :], 0.0)
                with dve.Fori(0, NB2) as i:
                    for par in range(2):
                        dve.wait_ge(hist.sem, hist.at(1) + i * 2)
                        col = (i * 2 + par) * B
                        dve.tensor_tensor(ohlo[:, par, :, :], iota_row[:, :].unsqueeze(1).to_broadcast([P, B, P]),
                                          klo[:, bass.ds(col, B)].unsqueeze(2).to_broadcast([P, B, P]), ALU.is_equal).then_inc(hot.sem, 1)
                        dve.tensor_tensor(ohhi[:, par, :, :], iota_row[:, 0:T].unsqueeze(1).to_broadcast([P, B, T]),
                                          khi[:, bass.ds(col, B)].unsqueeze(2).to_broadcast([P, B, T]), ALU.is_equal).then_inc(hot.sem, 1)
                n = [0]

                def link(ins):
                    n[0] += 1
                    ins.then_inc(cnt.sem, 1)
                    dve.wait_ge(cnt.sem, cnt.at(n[0]))

                dve.wait_ge(hist.sem, hist.at(2 * NB2 + 2))
                link(dve.tensor_copy(counts[:, :], pc[:, 0:T]))
                dve.wait_ge(hist.sem, hist.at(2 * NB2 + 3))
                link(dve.tensor_scalar(tot[:, :], px[:, 1, 0:T], float(P - 1), None, ALU.add))
                link(dve.tensor_copy(toti[:, :], tot[:, :]))
                link(dve.tensor_scalar(toti[:, :], toti[:, :], 7, None, ALU.logical_shift_right))
                link(dve.tensor_copy(nslot[:, :], toti[:, :]))
                link(dve.tensor_tensor_scan(end[:, :], nslot[:, :], zrow[:, :], 0.0, ALU.add, ALU.add))
                link(dve.tensor_tensor(start[:, :], end[:, :], nslot[:, :], ALU.subtract))
                link(dve.scalar_tensor_tensor(table[:, 0, 0, :], start[:, :], float(P), px[:, 0, 0:T], ALU.mult, ALU.add))
                dve.wait_ge(zm.sem, zm.at(2))
                link(dve.tensor_copy(slot_f[:, :], slot_i[:, :]))
                link(dve.tensor_tensor(ge[:, :, :], slot_f[:, :].unsqueeze(2).to_broadcast([1, SLOTS, T]),
                                       end[0:1, :].unsqueeze(1).to_broadcast([1, SLOTS, T]), ALU.is_ge))
                link(dve.tensor_reduce(tf[:, :], ge[:, :, :], X, ALU.add))
                link(dve.tensor_scalar(tf[:, :], tf[:, :], float(T - 1), None, ALU.min))
                link(dve.tensor_copy(g.tile_of[:, :], tf[:, :]))

            @block.tensor
            def _(pe):
                pe.wait_ge(zm.sem, zm.at(2))
                pe.matmul(pc[:, 0:T], zero[:, :], zero[:, 0:T], start=True, stop=False).then_inc(hist.sem, 1)
                with pe.Fori(0, NB2) as i:
                    for par in range(2):
                        pe.wait_ge(hot.sem, hot.at(2 + 2 * par) + i * 4)
                        for j in range(B):
                            last = pe.matmul(pc[:, 0:T], ohlo[:, par, j, :], ohhi[:, par, j, :], start=False, stop=False)
                        last.then_inc(hist.sem, 1)
                pe.matmul(pc[:, 0:T], zero[:, :], zero[:, 0:T], start=False, stop=True).then_inc(hist.sem, 1)
                pe.wait_ge(cnt.sem, cnt.at(1))
                pe.matmul(px[:, 0, 0:T], before[:, :], counts[:, :], start=True, stop=True)
                pe.matmul(px[:, 1, 0:T], ones[:, :], counts[:, :], start=True, stop=True).then_inc(hist.sem, 1)
            hot.base += 4 * NB2
            hist.base += 2 * NB2 + 3
            cnt.base += 13
            zm.base += 2

        s_diag, s_rows = sig("rank_diag"), sig("rank_rows")
        s_oh, s_cnt, s_look, s_pos, s_step, s_sc = (sig("rank_onehots"), sig("rank_counts"), sig("rank_looked"),
                                                   sig("rank_positions"), sig("rank_steps"), sig("rank_stepped"))
        scat = [sig(f"scattered{j}") for j in range(2)]
        copied = sig("rank_gate")
        with ExitStack() as c2, nc.Block() as block:
            ohlo = sb("r_lo", [P, 2, B, P], BF16, c2)
            ohhi = sb("r_hi", [P, 2, B, T], BF16, c2)
            ohloT = sb("r_loT", [P, 2, B, P], F32, c2)
            dlo = sb("r_dlo", [P, 2, B, P], BF16, c2)
            dhi = sb("r_dhi", [P, 2, B, P], BF16, c2)
            same = sb("r_same", [P, B, P], F32, c2)
            sel = sb("r_sel", [P, B, T], F32, c2)
            inside = sb("r_in", [P, B], F32, c2)
            found = sb("r_found", [P, B], F32, c2)
            q = sb("r_q", [P, B], F32, c2)
            qi = sb("r_qi", [P, B], I32, c2)
            qs = sb("r_qs", [P, B], I32, c2)
            qk = sb("r_qk", [P, B], I32, c2)
            idx = sb("r_idx", [P, 2, B], I32, c2)
            out4 = sb("r_out", [P, 2, B, 4], I32, c2)
            p_lo = [ps(f"r_plo{j}", [P, 512], F32, c2) for j in range(2)]
            p_key = [ps(f"r_pkey{j}", [P, 512], F32, c2) for j in range(2)]
            p_cnt = [ps(f"r_pc{j}", [P, 4, P], F32, c2) for j in range(2)]
            p_look = [ps(f"r_pl{j}", [P, 4, P], F32, c2) for j in range(2)]
            NB2 = COLS // (2 * B)
            D = 13

            @block.scalar
            def _(act):
                with act.Fori(0, NB2) as i:
                    for par in range(2):
                        if par == 0:
                            pass
                        act.wait_ge(s_rows.sem, s_rows.at(0) + i * 2 + par + 1)
                        for j in range(B):
                            col = (i * 2 + par) * B + j
                            act.activation(dlo[:, par, j, :], ident[:, :], ACT.Copy, scale=klo[:, bass.ds(col, 1)])
                            ins = act.activation(dhi[:, par, j, :], ident[:, :], ACT.Copy, scale=khi[:, bass.ds(col, 1)])
                        ins.then_inc(s_diag.sem, 1)

            @block.tensor
            def _(pe):
                pe.matmul(p_look[0][:, 0, :], ident[:, :], ident[:, :], start=True, stop=True).then_inc(s_rows.sem, 1)
                pe.matmul(p_look[1][:, 0, :], ident[:, :], ident[:, :], start=True, stop=True).then_inc(s_rows.sem, 1)
                with pe.Fori(0, NB2) as i:
                    for par in range(2):
                        n = i * 2 + par
                        pe.wait_ge(s_diag.sem, s_diag.at(1) + n)
                        pe.wait_ge(s_pos.sem, s_pos.at(1) + n)
                        lo4 = dlo[:, par, :, :].rearrange("p b q -> p (b q)")
                        hi4 = dhi[:, par, :, :].rearrange("p b q -> p (b q)")
                        pe.matmul(p_lo[par][:, :], onesb[:, :], lo4, start=True, stop=True)
                        pe.matmul(p_key[par][:, :], onesb[:, :], lo4, start=True, stop=False)
                        pe.matmul(p_key[par][:, :], n128b[:, :], hi4, start=False, stop=False)
                        pe.matmul(p_key[par][:, :], identb[:, :], notbefore[:, :, :].rearrange("p b q -> p (b q)"),
                                  start=False, stop=True).then_inc(s_rows.sem, 1)
                        pe.wait_ge(s_oh.sem, s_oh.at(1) + n)
                        for j in range(B):
                            ins = pe.matmul(p_cnt[par][:, j, 0:T], ohlo[:, par, j, :], ohhi[:, par, j, :], start=True, stop=True)
                        ins.then_inc(s_cnt.sem, 1)
                        pe.wait_ge(s_sc.sem, s_sc.at(1) + n)
                        for j in range(B):
                            ins = pe.matmul(p_look[par][:, j, 0:T], ohloT[:, par, j, :], table[:, par, j, :], start=True, stop=True)
                        ins.then_inc(s_look.sem, 1)

            @block.vector
            def _(dve):
                dve.memset(idx[:, :, :], 0).then_inc(s_pos.sem, 1)
                dve.memset(qi[:, :], 0).then_inc(s_pos.sem, 1)
                def batches_of(i):
                    for par in range(2):
                        n = i * 2 + par
                        col = n * B
                        d0 = s_step.base + n * D
                        base = d0 if isinstance(i, int) else dve.snap(d0)

                        def step(ins):
                            ins.then_inc(s_step.sem, 1)

                        dve.wait_ge(s_rows.sem, s_rows.at(3) + n)
                        dve.tensor_tensor(ohlo[:, par, :, :], iota_row[:, :].unsqueeze(1).to_broadcast([P, B, P]),
                                          klo[:, bass.ds(col, B)].unsqueeze(2).to_broadcast([P, B, P]), ALU.is_equal)
                        dve.tensor_tensor(ohhi[:, par, :, :], iota_row[:, 0:T].unsqueeze(1).to_broadcast([P, B, T]),
                                          khi[:, bass.ds(col, B)].unsqueeze(2).to_broadcast([P, B, T]), ALU.is_equal).then_inc(s_oh.sem, 1)
                        step(dve.tensor_scalar(ohloT[:, par, :, :], p_lo[par][:, :].rearrange("p (b q) -> p b q", b=B),
                                               iota_col[:, 0:1], None, ALU.is_equal))
                        step(dve.tensor_tensor(same[:, :, :], p_key[par][:, :].rearrange("p (b q) -> p b q", b=B),
                                               keyf[:, bass.ds(col, B)].unsqueeze(2).to_broadcast([P, B, P]), ALU.is_equal))
                        dve.wait_ge(s_cnt.sem, s_cnt.at(1) + n)
                        for j in range(B):
                            if j:
                                dve.wait_ge(s_step.sem, base + 2 + j)
                            else:
                                dve.wait_ge(s_step.sem, base + 2)
                            dst = table[:, par, j + 1, :] if j < B - 1 else table[:, 1 - par, 0, :]
                            ins = dve.tensor_tensor(dst, table[:, par, j, :], p_cnt[par][:, j, 0:T], ALU.add)
                            step(ins)
                        dve.wait_ge(s_step.sem, base + 6)
                        dve.tensor_reduce(inside[:, :], same[:, :, :], X, ALU.add).then_inc(s_sc.sem, 1)
                        dve.wait_ge(s_look.sem, s_look.at(1) + n)
                        step(dve.tensor_tensor(sel[:, :, :], p_look[par][:, :, 0:T], ohhi[:, par, :, :], ALU.mult))
                        dve.wait_ge(s_step.sem, base + 7)
                        step(dve.tensor_reduce(found[:, :], sel[:, :, :], X, ALU.add))
                        dve.wait_ge(s_step.sem, base + 8)
                        dve.wait_ge(s_sc.sem, s_sc.at(1) + n)
                        step(dve.tensor_tensor(q[:, :], found[:, :], inside[:, :], ALU.add))
                        dve.wait_ge(s_step.sem, base + 9)
                        step(dve.tensor_tensor(qi[:, :], q[:, :], pad_far[:, bass.ds(col, B)], ALU.add))
                        dve.wait_ge(s_step.sem, base + 10)
                        step(dve.tensor_scalar(qs[:, :], qi[:, :], 7, None, ALU.logical_shift_right))
                        step(dve.tensor_scalar(qk[:, :], qi[:, :], 127, None, ALU.bitwise_and))
                        dve.wait_ge(s_step.sem, base + 12)
                        if not isinstance(i, int):
                            dve.wait_ge(scat[par].sem, scat[par].at(0) + i * (16 * B))
                        step(dve.tensor_copy(out4[:, par, :, :], rec[:, bass.ds(col, B), :]))
                        dve.wait_ge(s_step.sem, base + 13)
                        dve.scalar_tensor_tensor(idx[:, par, :], qk[:, :], float(SLOTS), qs[:, :], ALU.mult, ALU.add).then_inc(s_pos.sem, 1)

                batches_of(0)
                with dve.Fori(1, NB2) as i:
                    batches_of(i)

            @block.gpsimd
            def _(pool):
                limit = pool.to_reg(SLOTS * P - 1)
                with pool.Fori(0, NB2) as i:
                    for par in range(2):
                        n = i * 2 + par
                        pool.wait_ge(s_pos.sem, s_pos.at(3) + n)
                        pool.sem_inc(copied.sem, 1)
                        for j in range(B):
                            pool.indirect_dma_start(out=records, out_offset=bass.IndirectOffsetOnAxis(ap=idx[:, par, j:j + 1], axis=0),
                                                    in_=out4[:, par, j, :], in_offset=None, bounds_check=limit,
                                                    oob_is_err=False).then_inc(scat[par].sem, 16)
                for par in range(2):
                    pool.wait_ge(scat[par].sem, scat[par].at(NB2 * B * 16))
            s_diag.base += 2 * NB2
            s_rows.base += 2 * NB2 + 2
            s_oh.base += 2 * NB2
            s_cnt.base += 2 * NB2
            s_look.base += 2 * NB2
            s_pos.base += 2 * NB2 + 2
            s_sc.base += 2 * NB2
            s_step.base += 2 * NB2 * D
            copied.base += 2 * NB2
            for par in range(2):
                scat[par].base += NB2 * B * 16

    prep = sig("sort_prepared")
    ld = sig("sort_loaded")
    with ExitStack() as c, nc.Block() as block:
        recs = sb("s_recs", [P, SLOTS, 4], I32, c)
        keyf = sb("s_keyf", [P, SLOTS], F32, c)
        vld = sb("s_vld", [P, SLOTS], F32, c)
        KT = sb("s_KT", [R, 4 * P], F32, c)
        ends = sb("s_ends", [R, 2], F32, c)
        KE = sb("s_KE", [8, 2, R], F32, c)
        pk = ps("s_pk", [P, 512], F32, c)
        pe_ = ps("s_pe", [8, 2, 256], F32, c)
        tr = sig("sort_turned")

        @block.sync
        def _(sp):
            sp.dma_start(recs[:, :, :], records.rearrange("(k s) f -> k s f", k=P)).then_inc(ld.sem, 16)

        @block.tensor
        def _(pe):
            pe.wait_ge(prep.sem, prep.at(5 + (g.name == "by_src")))
            for b in range(4):
                ins = pe.transpose(pk[0:R, b * P:(b + 1) * P], keyf[:, b:SLOTS:4], ident[:, :])
            ins.then_inc(tr.sem, 1)
            nn = 7 + (g.name == "by_src")
            pe.wait_ge(prep.sem, prep.at(nn + 1))
            for k in range(2):
                ins = pe.matmul(pe_[:, k, 0:R], ends[:, k:k + 1].to_broadcast([R, 8]), ident[0:R, 0:R], start=True, stop=True)
            ins.then_inc(tr.sem, 1)

        @block.vector
        def _(dve):
            n = [0]

            def link(ins):
                n[0] += 1
                ins.then_inc(prep.sem, 1)
                dve.wait_ge(prep.sem, prep.at(n[0]))

            def lowered(dst):
                link(dve.tensor_scalar(dst, dst, 1.0, -LOWEST, ALU.subtract, ALU.mult))

            dve.wait_ge(ld.sem, ld.at(16))
            link(dve.tensor_copy(g.klo[:, :], recs[:, :, 1].bitcast(F32)))
            link(dve.tensor_copy(g.other[:, :], recs[:, :, 0]))
            link(dve.tensor_copy(g.key[:, :], recs[:, :, 2]))
            if g.name == "by_src":
                link(dve.tensor_copy(g.w[:, :], recs[:, :, 3].bitcast(F32)))
            link(dve.tensor_scalar(vld[:, :], g.klo[:, :], 0.0, -1.0e5, ALU.is_lt, ALU.mult))
            link(dve.tensor_tensor(keyf[:, :], g.key[:, :], vld[:, :], ALU.add))
            dve.wait_ge(tr.sem, tr.at(1))
            link(dve.tensor_copy(KT[:, :], pk[0:R, :]))
            link(dve.tensor_copy(ends[:, 0:1], KT[:, 0:1]))
            link(dve.tensor_copy(ends[:, 1:2], KT[:, 4 * P - 1:4 * P]))
            W = 4 * P
            link(dve.memset(g.negnew[:, 0:1], 0.0))
            link(dve.memset(g.negnewb[:, W - 1:W], 0.0))
            link(dve.tensor_tensor(g.negnew[:, 1:W], KT[:, 1:W], KT[:, 0:W - 1], ALU.is_equal))
            link(dve.tensor_tensor(g.negnewb[:, 0:W - 1], KT[:, 1:W], KT[:, 0:W - 1], ALU.is_equal))
            link(dve.tensor_scalar(g.negfirst[:, :], KT[:, :], ends[:, 0:1], None, ALU.is_equal))
            link(dve.tensor_scalar(g.neglast[:, :], KT[:, :], ends[:, 1:2], None, ALU.is_equal))
            for m in (g.negnew, g.negnewb, g.negfirst, g.neglast):
                lowered(m[:, :])
            dve.wait_ge(tr.sem, tr.at(2))
            link(dve.tensor_copy(KE[:, :, :], pe_[:, :, 0:R]))
            link(dve.memset(g.negcont[:, :], 0.0))
            link(dve.tensor_tensor(g.negcont[:, 1:R], KE[:, 0, 1:R], KE[:, 1, 0:R - 1], ALU.is_equal))
            link(dve.tensor_tensor(g.negthru[:, :], KE[:, 0, :], KE[:, 1, :], ALU.is_equal))
            link(dve.tensor_tensor(g.negthrub[:, :], g.negthru[:, :], g.negcont[:, 1:R + 1], ALU.mult))
            link(dve.tensor_tensor(g.negthru[:, :], g.negthru[:, :], g.negcont[:, 0:R], ALU.mult))
            for m in (g.negcont, g.negthru, g.negthrub):
                lowered(m[:, :])
            prep.base += n[0]
        tr.base += 2
        ld.base += 16


def gat_layer(nc, sig, sb, ps, A, K, n, g, convs, out):
    N, T, NT, LAST = K["N"], K["T"], K["NT"], K["LAST"]
    xres, hres, ident, ones, iota_row = K["xres"], K["hres"], K["ident"], K["ones"], K["iota_row"]
    SLOTS, R = g.slots, g.rows
    NC = len(convs)
    FEAT = NC * CH
    HS = sum(c[1] for c in convs)
    WALL = FEAT + 2 * HS
    ACC = FEAT + HS
    heads0 = [sum(c[1] for c in convs[:k]) for k in range(NC)]
    acc0 = [k * CH + heads0[k] for k in range(NC)]
    feats = nc.dram_tensor(f"feats{n}", [NT, FEAT], F32, kind="Internal").ap()
    from_scores = nc.dram_tensor(f"from_scores{n}", [NT, HS], F32, kind="Internal").ap()
    to_scores = nc.dram_tensor(f"to_scores{n}", [NT, HS], F32, kind="Internal").ap()

    def rows_of(ap):
        return ap.rearrange("(a f) -> a f", a=1)

    steps, roots = sig("norm_steps"), sig("norm_roots")
    wld, tr, trc = sig("weights_loaded"), sig("weights_turned"), sig("weights_copied")
    with ExitStack() as c:
        wall = sb("wall", [P, 2, WALL], F32, c)
        hin = hres
        if n == 3:
            hin = sb("hnorm", [P, T, CH], F32, c)
        with ExitStack() as c2, nc.Block() as block:
            sq = sb("n_sq", [P, T, CH], F32, c2)
            mean = sb("n_mean", [P, T], F32, c2)
            var = sb("n_var", [P, T], F32, c2)
            std = sb("n_std", [P, T], F32, c2)
            gb = sb("n_gb", [P, 2, CH], F32, c2)
            woi = sb("w_oi", [P, 2, CH], F32, c2)
            attb = sb("w_att", [P, 2, 2 * HS], F32, c2)
            pw = ps("w_ps", [P, 2, CH], F32, c2)
            pf = ps("w_pf", [P, 2, 256], F32, c2)
            n_sqrt = 2 if n == 3 else 1
            n_dma = [(4 if cv[3] == "head_in_out" else 1) + 2 * cv[1] for cv in convs]
            gbl = sig("gamma_loaded")
            wz, wfree = sig("weights_zeroed"), sig("weights_free")

            @block.sync
            def _(sp):
                if n == 3:
                    sp.dma_start(gb[:, 0, :], rows_of(A["L3_gnn_gamma"]).to_broadcast([P, CH])).then_inc(gbl.sem, 16)
                    sp.dma_start(gb[:, 1, :], rows_of(A["L3_gnn_beta"]).to_broadcast([P, CH])).then_inc(gbl.sem, 16)
                for k, (_, H, W, form, a_from, a_to) in enumerate(convs):
                    C = CH // H
                    sp.wait_ge(wz.sem, wz.at(k + 1))
                    if form == "out_in":
                        sp.dma_start(woi[:, :, :], W.rearrange("(k p) f -> p k f", p=P)).then_inc(wld.sem, 16)
                    elif form == "in_out":
                        sp.dma_start(wall[:, :, k * CH:(k + 1) * CH], W.rearrange("(k p) f -> p k f", p=P)).then_inc(wld.sem, 16)
                    else:
                        for h in range(H):
                            sp.dma_start(wall[:, :, h * C:(h + 1) * C], W[h].rearrange("(k p) o -> p k o", p=P)).then_inc(wld.sem, 16)
                    for h in range(H):
                        r0, kk = (h * C) % P, (h * C) // P
                        for side, a in enumerate((a_from, a_to)):
                            col = side * HS + heads0[k] + h
                            sp.dma_start(attb[r0:r0 + C, kk, col:col + 1], a[h].rearrange("(c a) -> c a", a=1)).then_inc(wld.sem, 16)
                sp.wait_ge(wld.sem, wld.at(16 * sum(n_dma)))
                if n == 3:
                    sp.wait_ge(gbl.sem, gbl.at(32))

            @block.tensor
            def _(pe):
                for k, (_, H, W, form, _, _) in enumerate(convs):
                    pe.wait_ge(wld.sem, wld.at(16 * sum(n_dma[:k + 1])))
                    for a in range(2):
                        for b in range(2):
                            src = woi[:, a, b * P:(b + 1) * P] if form == "out_in" else wall[:, a, k * CH + b * P:k * CH + (b + 1) * P]
                            ins = pe.transpose(pw[:, b, a * P:(a + 1) * P], src, ident[:, :])
                    ins.then_inc(tr.sem, 1)
                    pe.wait_ge(trc.sem, trc.at(2 * k + 1))
                    hs = slice(heads0[k], heads0[k] + H)
                    for m in range(2):
                        for side in range(2):
                            col = side * HS + heads0[k]
                            for kk in range(2):
                                ins = pe.matmul(pf[:, m, col:col + H], woi[:, kk, m * P:(m + 1) * P],
                                                attb[:, kk, col:col + H], start=kk == 0, stop=kk == 1)
                    ins.then_inc(tr.sem, 1)

            @block.scalar
            def _(act):
                act.activation(attb[:, :, :], ident[:, 0:4 * HS].rearrange("p (k h) -> p k h", k=2), ACT.Copy, scale=0.0).then_inc(wz.sem, 1)
                for k, (_, H, W, form, _, _) in enumerate(convs):
                    act.wait_ge(tr.sem, tr.at(2 * k + 1))
                    dst = wall[:, :, k * CH:(k + 1) * CH] if form == "out_in" else woi[:, :, :]
                    act.activation(dst, pw[:, :, :], ACT.Copy).then_inc(trc.sem, 1)
                    act.wait_ge(tr.sem, tr.at(2 * k + 2))
                    for side in range(2):
                        col = side * HS + heads0[k]
                        ins = act.activation(wall[:, :, FEAT + col:FEAT + col + H], pf[:, :, col:col + H], ACT.Copy)
                    ins.then_inc(trc.sem, 1)
                    if k + 1 < NC:
                        act.wait_ge(trc.sem, trc.at(2 * k + 2))
                        act.sem_inc(wz.sem, 1)
                for r in range(n_sqrt):
                    act.wait_ge(steps.sem, steps.at(7 * (r + 1) if r == 0 else 7 + 3 + 7))
                    act.activation(std[:, :], var[:, :], ACT.Sqrt).then_inc(roots.sem, 1)

            @block.vector
            def _(dve):
                m = [0]

                def link(ins):
                    m[0] += 1
                    ins.then_inc(steps.sem, 1)
                    dve.wait_ge(steps.sem, steps.at(m[0]))

                def center(dst, src, r):
                    link(dve.tensor_reduce(mean[:, :], src[:, :, :], X, ALU.add))
                    link(dve.tensor_scalar(mean[:, :], mean[:, :], 1.0 / CH, None, ALU.mult))
                    link(dve.tensor_tensor(dst[:, :, :], src[:, :, :], mean[:, :].unsqueeze(2).to_broadcast([P, T, CH]), ALU.subtract))
                    link(dve.tensor_tensor(sq[:, :, :], dst[:, :, :], dst[:, :, :], ALU.mult))
                    link(dve.tensor_reduce(var[:, :], sq[:, :, :], X, ALU.add))
                    link(dve.tensor_scalar(var[:, :], var[:, :], 1.0 / CH, None, ALU.mult))
                    link(dve.tensor_scalar(var[:, :], var[:, :], EPS, None, ALU.add))
                    dve.wait_ge(roots.sem, roots.at(r + 1))
                    link(dve.reciprocal(mean[:, :], std[:, :]))
                    link(dve.tensor_tensor(dst[:, :, :], dst[:, :, :], mean[:, :].unsqueeze(2).to_broadcast([P, T, CH]), ALU.mult))

                center(hres, xres, 0)
                link(dve.tensor_scalar(hres[:, :, :], hres[:, :, :], 0.0, None, ALU.max))
                if n == 3:
                    center(hin, hres, 1)
                    dve.wait_ge(gbl.sem, gbl.at(32))
                    for k, op in enumerate((ALU.mult, ALU.add)):
                        link(dve.tensor_tensor(hin[:, :, :], hin[:, :, :], gb[:, k, :].unsqueeze(1).to_broadcast([P, T, CH]), op))
                steps.base += m[0]
            wld.base += 16 * sum(n_dma)
            tr.base += 2 * NC
            trc.base += 2 * NC
            wz.base += NC
            roots.base += n_sqrt
            if n == 3:
                gbl.base += 32

        hs_, ht, hc, hm, he = sig("tile_staged"), sig("tile_turned"), sig("tile_copied"), sig("tile_product"), sig("tile_evacuated")
        st = [sig(f"tile_stored{j}") for j in range(2)]
        with ExitStack() as c2, nc.Block() as block:
            hst = sb("t_st", [P, 2, CH], F32, c2)
            hT = sb("t_T", [P, 2, 2, P], F32, c2)
            row = sb("t_row", [P, 2, WALL], F32, c2)
            pT = [ps(f"t_pT{j}", [P, 2, 256], F32, c2) for j in range(2)]
            pm = [ps(f"t_pm{j}", [P, 512], F32, c2) for j in range(2)]
            pn = [ps(f"t_pn{j}", [P, 512], F32, c2) for j in range(2)]
            MAIN = min(WALL, 512)

            def tiles(eng, body):
                for par in range(2):
                    body(par, 0, par)
                with eng.Fori(1, T // 2) as i:
                    for par in range(2):
                        body(i * 2 + par, i, par)
                if T % 2:
                    body(T - 1, T // 2, 0)

            @block.scalar
            def _(act):
                def body(t, i, par):
                    act.wait_ge(ht.sem, ht.at(1) + t)
                    act.activation(hst[:, par, :], hin[:, bass.ds(t, 1), :].rearrange("p a f -> p (a f)"), ACT.Copy).then_inc(hs_.sem, 1)
                    act.wait_ge(ht.sem, ht.at(3) + t)
                    act.wait_ge(hm.sem, hm.at(1) + t)
                    act.activation(hT[:, par, :, :], pT[par][:, :, 0:P], ACT.Copy).then_inc(hc.sem, 1)
                tiles(act, body)

            @block.tensor
            def _(pe):
                for j in range(2):
                    pe.matmul(pT[j][:, 0, 0:P], ident[:, :], ident[:, :], start=True, stop=True).then_inc(ht.sem, 1)
                for j in range(2):
                    pe.matmul(pm[j][:, 0:P], ident[:, :], ident[:, :], start=True, stop=True).then_inc(hm.sem, 1)

                def body(t, i, par):
                    pe.wait_ge(hs_.sem, hs_.at(1) + t)
                    for k in range(2):
                        ins = pe.transpose(pT[par][:, k, 0:P], hst[:, par, k * P:(k + 1) * P], ident[:, :])
                    ins.then_inc(ht.sem, 1)
                    pe.wait_ge(hc.sem, hc.at(1) + t)
                    pe.wait_ge(he.sem, he.at(1) + t)
                    for k in range(2):
                        ins = pe.matmul(pm[par][:, 0:MAIN], hT[:, par, k, :], wall[:, k, 0:MAIN], start=k == 0, stop=k == 1)
                    if WALL > MAIN:
                        for k in range(2):
                            ins = pe.matmul(pn[par][:, 0:WALL - MAIN], hT[:, par, k, :], wall[:, k, MAIN:WALL], start=k == 0, stop=k == 1)
                    ins.then_inc(hm.sem, 1)
                tiles(pe, body)

            @block.vector
            def _(dve):
                for j in range(2):
                    dve.memset(row[:, j, :], 0.0).then_inc(he.sem, 1)

                def body(t, i, par):
                    dve.wait_ge(hm.sem, hm.at(3) + t)
                    if not isinstance(i, int) or i > 0:
                        dve.wait_ge(st[par].sem, st[par].at(0) + i * 48)
                    ins = dve.tensor_copy(row[:, par, 0:MAIN], pm[par][:, 0:MAIN])
                    if WALL > MAIN:
                        ins = dve.tensor_copy(row[:, par, MAIN:WALL], pn[par][:, 0:WALL - MAIN])
                    ins.then_inc(he.sem, 1)
                tiles(dve, body)

            @block.sync
            def _(sp):
                def body(t, i, par):
                    sp.wait_ge(he.sem, he.at(3) + t)
                    for dst, a, b in ((feats, 0, FEAT), (from_scores, FEAT, FEAT + HS), (to_scores, FEAT + HS, WALL)):
                        sp.dma_start(dst[bass.ds(t * P, P), :], row[:, par, a:b]).then_inc(st[par].sem, 16)
                tiles(sp, body)
                for j in range(2):
                    sp.wait_ge(st[j].sem, st[j].at(48 * (T // 2 + (1 - j) * (T % 2))))
            hs_.base += T
            ht.base += T + 2
            hc.base += T
            hm.base += T + 2
            he.base += T + 2
            for j in range(2):
                st[j].base += 48 * (T // 2 + (1 - j) * (T % 2))

    with ExitStack() as c:
        prob = sb("prob", [P, SLOTS, HS], F32, c)
        gat = [sig(f"scores_in{j}") for j in range(2)]
        cp, gate, summed, lk = sig("score_index"), sig("score_gate"), sig("scores_summed"), sig("score_steps")
        B = 8
        with ExitStack() as c2, nc.Block() as block:
            idx = sb("g_idx", [P, 2, 2, B], I32, c2)
            got = sb("g_got", [P, 2, 2, B, HS], F32, c2)
            NB2 = SLOTS // (2 * B)
            NB = SLOTS // B

            def batches(eng, body):
                with eng.Fori(0, NB2) as i:
                    for par in range(2):
                        body(i * 2 + par, i, par)
                if NB % 2:
                    body(NB - 1, NB2, 0)

            @block.gpsimd
            def _(pool):
                limit = pool.to_reg(NT - 1)

                def body(nb, i, par):
                    pool.wait_ge(summed.sem, summed.at(1) + nb)
                    pool.sem_inc(gate.sem, 1)
                    pool.tensor_copy(idx[:, par, 0, :], g.other[:, bass.ds(nb * B, B)])
                    pool.tensor_copy(idx[:, par, 1, :], g.key[:, bass.ds(nb * B, B)]).then_inc(cp.sem, 1)
                    pool.wait_ge(cp.sem, cp.at(1) + nb)
                    pool.sem_inc(gate.sem, 1)
                    for side, tab in enumerate((from_scores, to_scores)):
                        for j in range(B):
                            pool.indirect_dma_start(out=got[:, par, side, j, :], out_offset=None, in_=tab,
                                                    in_offset=bass.IndirectOffsetOnAxis(ap=idx[:, par, side, j:j + 1], axis=0),
                                                    bounds_check=limit, oob_is_err=True).then_inc(gat[par].sem, 16)
                batches(pool, body)

            @block.vector
            def _(dve):
                for j in range(2):
                    dve.memset(got[:, j, 0, 0, :], 0.0).then_inc(summed.sem, 1)

                def body(nb, i, par):
                    dve.wait_ge(gat[par].sem, gat[par].at(32 * B) + i * (32 * B))
                    dve.tensor_tensor(prob[:, bass.ds(nb * B, B), :], got[:, par, 0, :, :], got[:, par, 1, :, :], ALU.add).then_inc(summed.sem, 1)
                batches(dve, body)
                m = [0]

                def link(ins):
                    m[0] += 1
                    ins.then_inc(lk.sem, 1)
                    dve.wait_ge(lk.sem, lk.at(m[0]))

                dve.wait_ge(summed.sem, summed.at(NB + 2))
                link(dve.scalar_tensor_tensor(prob[:, :, :], prob[:, :, :], 0.2, prob[:, :, :], ALU.mult, ALU.max))
                if n == 2:
                    link(dve.tensor_tensor(prob[:, :, :], prob[:, :, :], g.w[:, :].unsqueeze(2).to_broadcast([P, SLOTS, HS]), ALU.mult))
                lk.base += m[0]
            cp.base += NB
            gate.base += 2 * NB
            summed.base += NB + 2
            for j in range(2):
                gat[j].base += 32 * B * (NB2 + (1 - j) * (NB % 2))

        if n == 1:
            softmax_global(nc, sig, sb, ps, g, prob, HS, K)
        else:
            for k, (_, H, *_r) in enumerate(convs):
                softmax_runs(nc, sig, sb, ps, g, prob, heads0[k], H, K)

        acc = sb("acc", [P, T, ACC], F32, c)
        gin = [sig(f"rows_in{j}") for j in range(8)]
        cp, gate, msg_ok, pc_ok, mm, ac, zr = (sig("row_index"), sig("row_gate"), sig("messages_ready"), sig("probs_copied"),
                                               sig("slot_product"), sig("slot_added"), sig("acc_zeroed"))
        with ExitStack() as c2, nc.Block() as block:
            idx = sb("m_idx", [P, 2, 4], I32, c2)
            rows = sb("m_rows", [P, 8, FEAT], F32, c2)
            msg = sb("m_msg", [P, 4, ACC], F32, c2)
            oh = sb("m_oh", [P, 4, P], F32, c2)
            pp = [[ps(f"m_p{k}_{j}", [P, 512], F32, c2) for j in range(4)] for k in range(NC)]
            NI = SLOTS // 8

            @block.gpsimd
            def _(pool):
                limit = pool.to_reg(NT - 1)
                with pool.Fori(0, NI) as i:
                    for par in range(2):
                        nb = i * 2 + par
                        pool.wait_ge(msg_ok.sem, msg_ok.at(4) + nb * 4)
                        pool.sem_inc(gate.sem, 1)
                        pool.tensor_copy(idx[:, par, :], g.other[:, bass.ds(nb * 4, 4)]).then_inc(cp.sem, 1)
                        pool.wait_ge(cp.sem, cp.at(1) + nb)
                        pool.sem_inc(gate.sem, 1)
                        for j in range(4):
                            b = par * 4 + j
                            pool.indirect_dma_start(out=rows[:, b, :], out_offset=None, in_=feats,
                                                    in_offset=bass.IndirectOffsetOnAxis(ap=idx[:, par, j:j + 1], axis=0),
                                                    bounds_check=limit, oob_is_err=True).then_inc(gin[b].sem, 16)

            @block.scalar
            def _(act):
                with act.Fori(0, NI) as i:
                    for b in range(8):
                        s = i * 8 + b
                        act.wait_ge(mm.sem, mm.at(1) + s)
                        for k, cv in enumerate(convs):
                            a = acc0[k] + CH
                            ins = act.activation(msg[:, b % 4, a:a + cv[1]],
                                                 prob[:, bass.ds(s, 1), heads0[k]:heads0[k] + cv[1]].rearrange("p a h -> p (a h)"), ACT.Copy)
                        ins.then_inc(pc_ok.sem, 1)

            @block.tensor
            def _(pe):
                for j in range(4):
                    pe.matmul(pp[0][j][:, 0:P], ident[:, :], ident[:, :], start=True, stop=True).then_inc(mm.sem, 1)
                with pe.Fori(0, NI) as i:
                    for b in range(8):
                        s = i * 8 + b
                        j = b % 4
                        pe.wait_ge(msg_ok.sem, msg_ok.at(9) + s)
                        pe.wait_ge(pc_ok.sem, pc_ok.at(1) + s)
                        pe.wait_ge(ac.sem, ac.at(1) + s)
                        for k, cv in enumerate(convs):
                            w = CH + cv[1]
                            ins = pe.matmul(pp[k][j][:, 0:w], oh[:, j, :], msg[:, j, acc0[k]:acc0[k] + w], start=True, stop=True)
                        ins.then_inc(mm.sem, 1)

            @block.vector
            def _(dve):
                dve.memset(acc[:, :, :], 0.0).then_inc(ac.sem, 4)
                dve.memset(oh[:, :, :], 0.0).then_inc(msg_ok.sem, 8)
                dve.wait_ge(ac.sem, ac.at(4))
                dve.wait_ge(msg_ok.sem, msg_ok.at(8))
                with dve.Fori(0, NI) as i:
                    tiles = [dve.value_load(g.tile_of[0:1, bass.ds(i * 8 + b, 1)], min_val=0, max_val=T - 1) for b in range(8)]

                    def message(b):
                        s = i * 8 + b
                        j = b % 4
                        dve.wait_ge(mm.sem, mm.at(1) + s)
                        dve.tensor_scalar(oh[:, j, :], iota_row[:, :], g.klo[:, bass.ds(s, 1)], None, ALU.is_equal)
                        dve.wait_ge(gin[b].sem, gin[b].at(16) + i * 16)
                        for k, cv in enumerate(convs):
                            H = cv[1]
                            C = CH // H
                            ins = dve.tensor_tensor(msg[:, j, acc0[k]:acc0[k] + CH].rearrange("p (h c) -> p h c", h=H),
                                                    rows[:, b, k * CH:(k + 1) * CH].rearrange("p (h c) -> p h c", h=H),
                                                    prob[:, bass.ds(s, 1), heads0[k]:heads0[k] + H].rearrange("p a h -> p (a h)").unsqueeze(2).to_broadcast([P, H, C]),
                                                    ALU.mult)
                        ins.then_inc(msg_ok.sem, 1)

                    def add(b):
                        s = i * 8 + b
                        j = b % 4
                        dve.wait_ge(mm.sem, mm.at(5) + s)
                        dve.wait_ge(ac.sem, ac.at(4) + s)
                        for k, cv in enumerate(convs):
                            w = CH + cv[1]
                            a = acc[:, bass.ds(tiles[b], 1), acc0[k]:acc0[k] + w].rearrange("p a f -> p (a f)")
                            ins = dve.tensor_tensor(a, a, pp[k][j][:, 0:w], ALU.add)
                        ins.then_inc(ac.sem, 1)

                    for b in range(8):
                        message(b)
                        if b >= 2:
                            add(b - 2)
                    add(6)
                    add(7)
            cp.base += 2 * NI
            gate.base += 4 * NI
            msg_ok.base += SLOTS + 8
            pc_ok.base += SLOTS
            mm.base += SLOTS + 4
            ac.base += SLOTS + 4
            for j in range(8):
                gin[j].base += 16 * NI

        finish_layer(nc, sig, sb, ps, A, K, n, convs, acc, acc0, out)


def softmax_global(nc, sig, sb, ps, g, prob, H, K):
    SLOTS = g.slots
    ident, ones = K["ident"], K["ones"]
    lk, tr = sig("softmax_steps"), sig("softmax_turned")
    with ExitStack() as c, nc.Block() as block:
        low = sb("x_low", [P, SLOTS], F32, c)
        top = sb("x_top", [P, H], F32, c)
        top1 = sb("x_top1", [H, 1], F32, c)
        diag = sb("x_diag", [H, H], F32, c)
        pt = ps("x_pt", [H, 512], F32, c)
        pb = ps("x_pb", [P, 512], F32, c)

        @block.vector
        def _(dve):
            m = [0]

            def link(ins):
                m[0] += 1
                ins.then_inc(lk.sem, 1)
                dve.wait_ge(lk.sem, lk.at(m[0]))
            link(dve.tensor_scalar(low[:, :], g.klo[:, :], 0.0, LOWEST, ALU.is_lt, ALU.mult))
            link(dve.tensor_tensor(prob[:, :, :], prob[:, :, :], low[:, :].unsqueeze(2).to_broadcast([P, SLOTS, H]), ALU.add))
            link(dve.tensor_reduce(top[:, :], prob[:, :, :].rearrange("p s h -> p h s"), X, ALU.max))
            dve.wait_ge(tr.sem, tr.at(1))
            link(dve.tensor_reduce(top1[:, :], pt[:, 0:P], X, ALU.max))
            link(dve.tensor_scalar(diag[:, :], ident[0:H, 0:H], top1[:, 0:1], None, ALU.mult))
            dve.wait_ge(tr.sem, tr.at(2))
            link(dve.tensor_copy(top[:, :], pb[:, 0:H]))
            link(dve.tensor_tensor(prob[:, :, :], prob[:, :, :], top[:, :].unsqueeze(1).to_broadcast([P, SLOTS, H]), ALU.subtract))

        @block.tensor
        def _(pe):
            pe.wait_ge(lk.sem, lk.at(3))
            pe.transpose(pt[:, 0:P], top[:, :], ident[:, :]).then_inc(tr.sem, 1)
            pe.wait_ge(lk.sem, lk.at(5))
            pe.matmul(pb[:, 0:H], ones[0:H, :], diag[:, :], start=True, stop=True).then_inc(tr.sem, 1)

        @block.scalar
        def _(act):
            act.wait_ge(lk.sem, lk.at(7))
            act.activation(prob[:, :, :], prob[:, :, :], ACT.Exp)
        lk.base += 7
        tr.base += 2


def softmax_runs(nc, sig, sb, ps, g, prob, h0, H, K):
    SLOTS, R = g.slots, g.rows
    W = 4 * P
    ident = K["ident"]
    lk, tr, ev, ex, back, bk = (sig("softmax_steps"), sig("softmax_turned"), sig("softmax_copied"),
                                sig("softmax_exps"), sig("softmax_back"), sig("softmax_done"))
    with ExitStack() as c, nc.Block() as block:
        sc = sb("y_sc", [R, H, W], F32, c)
        top = sb("y_top", [R, H, W], F32, c)
        tmp = sb("y_tmp", [R, W], F32, c)
        ends = sb("y_ends", [R, 2, H], F32, c)
        endT = sb("y_endT", [H, 2, R], F32, c)
        run = sb("y_run", [H, 2, R], F32, c)
        carry = sb("y_carry", [H, 2, R], F32, c)
        carryT = sb("y_carryT", [R, 2, H], F32, c)
        pt = [ps(f"y_pt{j}", [P, W], F32, c) for j in range(2)]
        pe1 = ps("y_pe", [H, 2, 256], F32, c)
        pe2 = ps("y_pf", [R, 2, 256], F32, c)
        pb = [ps(f"y_pb{j}", [P, W], F32, c) for j in range(2)]

        @block.tensor
        def _(pe):
            for h in range(H):
                if h >= 2:
                    pe.wait_ge(ev.sem, ev.at(h - 1))
                for b in range(4):
                    ins = pe.transpose(pt[h % 2][0:R, b * P:(b + 1) * P], prob[:, b:SLOTS:4, h0 + h], ident[:, :])
                ins.then_inc(tr.sem, 1)
            pe.wait_ge(lk.sem, lk.at(3 * H + 2))
            for k in range(2):
                ins = pe.transpose(pe1[:, k, 0:R], ends[:, k, :], ident[0:R, 0:R])
            ins.then_inc(tr.sem, 1)
            pe.wait_ge(lk.sem, lk.at(3 * H + 9))
            for k in range(2):
                ins = pe.transpose(pe2[:, k, 0:H], carry[:, k, :], ident[0:H, 0:H])
            ins.then_inc(tr.sem, 1)
            for h in range(H):
                pe.wait_ge(ex.sem, ex.at(h + 1))
                if h >= 2:
                    pe.wait_ge(bk.sem, bk.at(h - 1))
                for b in range(4):
                    ins = pe.transpose(pb[h % 2][:, b * R:(b + 1) * R], sc[:, h, b * P:(b + 1) * P], ident[0:R, 0:R])
                ins.then_inc(back.sem, 1)

        @block.scalar
        def _(act):
            for h in range(H):
                act.wait_ge(tr.sem, tr.at(h + 1))
                act.activation(sc[:, h, :], pt[h % 2][0:R, :], ACT.Copy).then_inc(ev.sem, 1)

            def turn_back(h):
                act.wait_ge(back.sem, back.at(h + 1))
                act.activation(prob[:, :, h0 + h].rearrange("p (c b) -> p b c", b=4),
                               pb[h % 2][:, 0:4 * R].rearrange("p (b c) -> p b c", b=4), ACT.Copy).then_inc(bk.sem, 1)
            for h in range(H):
                act.wait_ge(lk.sem, lk.at(3 * H + 10 + 3 * (h + 1)))
                act.activation(sc[:, h, :], sc[:, h, :], ACT.Exp).then_inc(ex.sem, 1)
                if h >= 1:
                    turn_back(h - 1)
            turn_back(H - 1)

        @block.vector
        def _(dve):
            m = [0]

            def link(ins):
                m[0] += 1
                ins.then_inc(lk.sem, 1)
                dve.wait_ge(lk.sem, lk.at(m[0]))
            for h in range(H):
                dve.wait_ge(ev.sem, ev.at(h + 1))
                link(dve.tensor_tensor_scan(top[:, h, :], g.negnew[:, :], sc[:, h, :], LOWEST, ALU.add, ALU.max))
                link(dve.tensor_tensor_scan(tmp[:, ::-1], g.negnewb[:, ::-1], sc[:, h, ::-1], LOWEST, ALU.add, ALU.max))
                link(dve.tensor_tensor(top[:, h, :], top[:, h, :], tmp[:, :], ALU.max))
            link(dve.tensor_copy(ends[:, 0, :], top[:, :, W - 1]))
            link(dve.tensor_copy(ends[:, 1, :], top[:, :, 0]))
            dve.wait_ge(tr.sem, tr.at(H + 1))
            link(dve.tensor_copy(endT[:, :, :], pe1[:, :, 0:R]))
            link(dve.tensor_tensor_scan(run[:, 0, :], g.negthru[0:H, :], endT[:, 0, :], LOWEST, ALU.add, ALU.max))
            link(dve.tensor_tensor_scan(run[:, 1, ::-1], g.negthrub[0:H, ::-1], endT[:, 1, ::-1], LOWEST, ALU.add, ALU.max))
            link(dve.memset(carry[:, 0, 0:1], LOWEST))
            link(dve.memset(carry[:, 1, R - 1:R], LOWEST))
            link(dve.tensor_tensor(carry[:, 0, 1:R], run[:, 0, 0:R - 1], g.negcont[0:H, 1:R], ALU.add))
            link(dve.tensor_tensor(carry[:, 1, 0:R - 1], run[:, 1, 1:R], g.negcont[0:H, 1:R], ALU.add))
            dve.wait_ge(tr.sem, tr.at(H + 2))
            link(dve.tensor_copy(carryT[:, :, :], pe2[:, :, 0:H]))
            for h in range(H):
                link(dve.scalar_tensor_tensor(top[:, h, :], g.negfirst[:, :], carryT[:, 0, h:h + 1], top[:, h, :], ALU.add, ALU.max))
                link(dve.scalar_tensor_tensor(top[:, h, :], g.neglast[:, :], carryT[:, 1, h:h + 1], top[:, h, :], ALU.add, ALU.max))
                link(dve.tensor_tensor(sc[:, h, :], sc[:, h, :], top[:, h, :], ALU.subtract))
        lk.base += 3 * H + 10 + 3 * H
        tr.base += H + 2
        ev.base += H
        ex.base += H
        back.base += H
        bk.base += H


def finish_layer(nc, sig, sb, ps, A, K, n, convs, acc, acc0, out):
    N, T, LAST = K["N"], K["T"], K["LAST"]
    xres, hres, ident = K["xres"], K["hres"], K["ident"]
    NC = len(convs)
    lk, ld, ex = sig("finish_steps"), sig("finish_loaded"), sig("finish_exps")
    biases = {0: ["L0_gnn_bias"], 1: [], 2: ["L2_gnn_bias"], 3: ["L3_gnn_b1", "L3_gnn_b2"]}[n]
    with ExitStack() as c, nc.Block() as block:
        bias = sb("f_bias", [P, 3, CH], F32, c)
        tmp = sb("f_tmp", [P, T, CH], F32, c)
        rden = sb("f_rden", [P, T, 8], F32, c)
        wu = sb("f_wu", [P, 4, CH], F32, c) if n == 3 else None
        waits = len(biases) + (2 if n == 3 else 0)

        @block.sync
        def _(sp):
            for k, name in enumerate(biases):
                b = A[name]
                b = b.rearrange("(a f) -> a f", a=1) if n != 2 else b.rearrange("h c -> (h c)").rearrange("(a f) -> a f", a=1)
                sp.dma_start(bias[:, k, :], b.to_broadcast([P, CH])).then_inc(ld.sem, 16)
            if n == 3:
                sp.dma_start(bias[:, 2, :], A["L3_gnn_bu"].rearrange("(a f) -> a f", a=1).to_broadcast([P, CH])).then_inc(ld.sem, 16)
                sp.dma_start(wu[:, :, :], A["L3_gnn_Wu"].rearrange("(k p) f -> p k f", p=P)).then_inc(ld.sem, 16)
            if waits:
                sp.wait_ge(ld.sem, ld.at(16 * waits))

        count = [0]
        exps = []

        @block.vector
        def _(dve):
            def link(ins):
                count[0] += 1
                ins.then_inc(lk.sem, 1)
                dve.wait_ge(lk.sem, lk.at(count[0]))

            if waits:
                dve.wait_ge(ld.sem, ld.at(16 * waits))
            for k, cv in enumerate(convs):
                H = cv[1]
                z = acc[:, :, acc0[k]:acc0[k] + CH]
                den = acc[:, :, acc0[k] + CH:acc0[k] + CH + H]
                if n == 1:
                    link(dve.tensor_scalar(den, den, 1e-6, None, ALU.max))
                elif n == 2:
                    link(dve.tensor_scalar(den, den, 1e-30, None, ALU.max))
                else:
                    link(dve.tensor_scalar(den, den, 1e-16, None, ALU.add))
                link(dve.reciprocal(rden[:, :, 0:H], den))
                z4 = z.rearrange("p t (h c) -> p t h c", h=H)
                link(dve.tensor_tensor(z4, z4, rden[:, :, 0:H].unsqueeze(3).to_broadcast([P, T, H, CH // H]), ALU.mult))
                if biases:
                    link(dve.tensor_tensor(z, z, bias[:, k, :].unsqueeze(1).to_broadcast([P, T, CH]), ALU.add))
                if n in (0, 3):
                    link(dve.tensor_scalar(tmp[:, :, :], z, 0.0, None, ALU.min))
                    exps.append(count[0])
                    dve.wait_ge(ex.sem, ex.at(len(exps)))
                    link(dve.tensor_scalar(tmp[:, :, :], tmp[:, :, :], 1.0, None, ALU.subtract))
                    link(dve.scalar_tensor_tensor(z, z, 0.0, tmp[:, :, :], ALU.max, ALU.add))
                if n == 2:
                    link(dve.tensor_scalar(z, z, 0.0, None, ALU.max))
                if n != 3:
                    link(dve.tensor_tensor(xres[:, :, :], xres[:, :, :], z, ALU.add))
            if n in (0, 3):
                link(dve.tensor_tensor(xres[:, :, :], xres[:, :, :], hres[:, :, :], ALU.add))
            if n == 3:
                link(dve.tensor_tensor(xres[:, :, :], xres[:, :, :], bias[:, 2, :].unsqueeze(1).to_broadcast([P, T, CH]), ALU.add))

        @block.scalar
        def _(act):
            for k in range(NC if n in (0, 3) else 0):
                act.wait_ge(lk.sem, lk.at(5 + 7 * k))
                act.activation(tmp[:, :, :], tmp[:, :, :], ACT.Exp).then_inc(ex.sem, 1)

        if n != 3:
            lk.base += count[0]
            ld.base += 16 * waits
            ex.base += 1 if n == 0 else 0
            return

        hs_, ht, hc, hm, he, st = (sig("tile_staged"), sig("tile_turned"), sig("tile_copied"), sig("tile_product"),
                                   sig("tile_evacuated"), sig("stored"))
        cat = sb("f_cat", [P, 2, 2 * CH], F32, c)
        catT = sb("f_catT", [P, 2, 4, P], F32, c)
        pT = [ps(f"f_pT{j}", [P, 512], F32, c) for j in range(2)]
        pm = [ps(f"f_pm{j}", [P, 512], F32, c) for j in range(2)]
        total = count[0]

        def tiles(eng, body):
            with eng.Fori(0, T // 2) as i:
                for par in range(2):
                    body(i * 2 + par, par)
            if T % 2:
                body(T - 1, 0)

        @block.scalar
        def _(act):
            act.wait_ge(lk.sem, lk.at(total))

            def body(t, par):
                act.wait_ge(ht.sem, ht.at(1) + t)
                for k in range(2):
                    ins = act.activation(cat[:, par, k * CH:(k + 1) * CH],
                                         acc[:, bass.ds(t, 1), acc0[k]:acc0[k] + CH].rearrange("p a f -> p (a f)"), ACT.Copy)
                ins.then_inc(hs_.sem, 1)
                act.wait_ge(ht.sem, ht.at(3) + t)
                act.wait_ge(hm.sem, hm.at(1) + t)
                act.activation(catT[:, par, :, :], pT[par][:, :].rearrange("p (k q) -> p k q", k=4), ACT.Copy).then_inc(hc.sem, 1)
            tiles(act, body)

        @block.tensor
        def _(pe):
            pe.wait_ge(ld.sem, ld.at(16 * waits))
            for j in range(2):
                pe.matmul(pT[j][:, 0:P], ident[:, :], ident[:, :], start=True, stop=True).then_inc(ht.sem, 1)
            for j in range(2):
                pe.matmul(pm[j][:, 0:P], ident[:, :], ident[:, :], start=True, stop=True).then_inc(hm.sem, 1)

            def body(t, par):
                pe.wait_ge(hs_.sem, hs_.at(1) + t)
                for k in range(4):
                    ins = pe.transpose(pT[par][:, k * P:(k + 1) * P], cat[:, par, k * P:(k + 1) * P], ident[:, :])
                ins.then_inc(ht.sem, 1)
                pe.wait_ge(hc.sem, hc.at(1) + t)
                pe.wait_ge(he.sem, he.at(1) + t)
                for k in range(4):
                    ins = pe.matmul(pm[par][:, 0:CH], catT[:, par, k, :], wu[:, k, :], start=k == 0, stop=k == 3)
                ins.then_inc(hm.sem, 1)
            tiles(pe, body)

        @block.vector
        def _(dve):
            dve.memset(rden[:, :, :], 0.0).then_inc(he.sem, 2)

            def body(t, par):
                dve.wait_ge(hm.sem, hm.at(3) + t)
                xt = xres[:, bass.ds(t, 1), :].rearrange("p a f -> p (a f)")
                dve.tensor_tensor(xt, xt, pm[par][:, 0:CH], ALU.add).then_inc(he.sem, 1)
            tiles(dve, body)

        @block.sync
        def _(sp):
            sp.wait_ge(he.sem, he.at(T + 2))
            sp.dma_start(out[0:(T - 1) * P, :].rearrange("(t p) f -> p t f", p=P), xres[:, 0:T - 1, :]).then_inc(st.sem, 16)
            sp.dma_start(out[(T - 1) * P:N, :], xres[0:LAST, T - 1, :]).then_inc(st.sem, 16)
            sp.wait_ge(st.sem, st.at(32))


_INS = ['x', 'src', 'dst', 'edge_weight', 'L0_gnn_W', 'L0_gnn_att_src', 'L0_gnn_att_dst', 'L0_gnn_bias', 'L1_gnn_W',
        'L1_gnn_attn_l', 'L1_gnn_attn_r', 'L2_gnn_W', 'L2_gnn_a_self', 'L2_gnn_a_neigh', 'L2_gnn_bias', 'L3_gnn_gamma',
        'L3_gnn_beta', 'L3_gnn_W1', 'L3_gnn_a_src1', 'L3_gnn_a_dst1', 'L3_gnn_b1', 'L3_gnn_W2', 'L3_gnn_a_src2',
        'L3_gnn_a_dst2', 'L3_gnn_b2', 'L3_gnn_Wu', 'L3_gnn_bu']
_OUTS = [((3125, 256), 'float32')]


def kernel(**inputs):
    import numpy as _np
    import concourse.bacc as _bacc
    from concourse import mybir as _mybir
    from concourse.bass_utils import run_bass_kernel_spmd as _run

    nc = _bacc.Bacc("TRN2", target_bir_lowering=False, num_devices=1)
    arrays, args = {}, {}
    for name in _INS:
        a = _np.ascontiguousarray(inputs[name])
        arrays[f"in_{name}_dram"] = a
        args[name] = nc.dram_tensor(f"in_{name}_dram", a.shape, _mybir.dt.from_np(a.dtype), kind="ExternalInput").ap()
    outs = []
    for i, (shape, dtype) in enumerate(_OUTS):
        dt = _mybir.dt.from_np(_np.dtype(dtype))
        outs.append(nc.dram_tensor(f"out_{i}_dram", shape, dt, kind="ExternalOutput").ap())
    build(nc, args, *outs)
    r = _run(nc, [arrays], core_ids=[0])
    got = tuple(r.results[0][f"out_{i}_dram"] for i in range(len(_OUTS)))
    return got[0]
```

```python
from contextlib import ExitStack

import concourse.bass as bass
from concourse import mybir

F32 = mybir.dt.float32
BF16 = mybir.dt.bfloat16
I32 = mybir.dt.int32
ALU = mybir.AluOpType
ACT = mybir.ActivationFunctionType
X = mybir.AxisListType.X

P = 128
CH = 256
LO = 128
LOWEST = -3.0e38
PAD_KEY = 4095
FAR = float(1 << 23) * 1.5
EPS = 1e-5


class Signal:

    def __init__(self, sem):
        self.sem = sem
        self.base = 0

    def at(self, n):
        return self.base + n


class Graph:

    def __init__(self, name, edges, nodes, loops):
        self.name = name
        self.tiles = -(-nodes // P)
        self.edge_cols = -(-edges // P)
        self.loop_cols = self.tiles if loops else 0
        self.cols = -(-(self.edge_cols + self.loop_cols) // 8) * 8
        real = edges + (nodes if loops else 0)
        self.slots = -(-((real + self.tiles * (P - 1)) // P) // 8) * 8
        self.rows = self.slots // 4


def build(nc, A, out):
    x_in = A["x"]
    N = x_in.shape[0]
    E = A["src"].shape[0]
    T = -(-N // P)
    NT = T * P
    LAST = N - (T - 1) * P

    ctx = ExitStack()
    with ctx:
        signals = {}

        def sig(name):
            if name not in signals:
                signals[name] = Signal(ctx.enter_context(nc.semaphore(name)))
            return signals[name]

        used = {}

        def numbered(name):
            used[name] = used.get(name, 0) + 1
            return f"{name}.{used[name]}"

        def sb(name, shape, dt=F32, c=ctx):
            return c.enter_context(nc.sbuf_tensor(numbered(name), shape, dt))

        def ps(name, shape, dt, c):
            return c.enter_context(nc.psum_tensor(numbered(name), shape, dt))

        by_dst = Graph("by_dst", E, N, True)
        by_src = Graph("by_src", E, N, False)

        iota_row = sb("iota_row", [P, P])
        iota_col = sb("iota_col", [P, 1])
        ident = sb("ident", [P, P])
        identb = sb("identb", [P, P], BF16)
        ones = sb("ones", [P, P])
        onesb = sb("onesb", [P, P], BF16)
        n128b = sb("n128b", [P, P], BF16)
        before = sb("before", [P, P])
        notbefore = sb("notbefore", [P, 4, P], BF16)
        xres = sb("xres", [P, T, CH])
        hres = sb("hres", [P, T, CH])
        for g in (by_dst, by_src):
            g.klo = sb(f"{g.name}_klo", [P, g.slots])
            g.key = sb(f"{g.name}_key", [P, g.slots], I32)
            g.other = sb(f"{g.name}_other", [P, g.slots + 8], I32)
            g.negfirst = sb(f"{g.name}_negfirst", [g.rows, 4 * P])
            g.neglast = sb(f"{g.name}_neglast", [g.rows, 4 * P])
            g.negnew = sb(f"{g.name}_negnew", [g.rows, 4 * P])
            g.negnewb = sb(f"{g.name}_negnewb", [g.rows, 4 * P])
            g.negcont = sb(f"{g.name}_negcont", [8, g.rows + 1])
            g.negthru = sb(f"{g.name}_negthru", [8, g.rows])
            g.negthrub = sb(f"{g.name}_negthrub", [8, g.rows])
            g.tiles4 = sb(f"{g.name}_tiles4", [1, g.slots // 4], I32)
            g.lines = [nc.dram_tensor(f"{g.name}_{what}", [g.slots * P], BF16, kind="Internal").ap()
                       for what in ("other_row", "other_tile", "own_row")]
        by_src.w = sb("edge_w", [P, by_src.slots])

        made, made2, loaded = sig("const_made"), sig("const_made2"), sig("x_loaded")
        with ExitStack() as c, nc.Block() as block:
            ii = sb("iota_i", [P, P], I32, c)
            ic = sb("iota_ci", [P, 1], I32, c)

            @block.gpsimd
            def _(pool):
                pool.iota(ii[:, :], [[1, P]], base=0, channel_multiplier=0).then_inc(made.sem, 1)
                pool.iota(ic[:, :], [[1, 1]], base=0, channel_multiplier=1).then_inc(made.sem, 1)

            @block.vector
            def _(dve):
                dve.memset(ones[:, :], 1.0)
                dve.memset(onesb[:, :], 1.0)
                dve.memset(n128b[:, :], 128.0)
                dve.memset(xres[:, T - 1, :], 0.0).then_inc(made2.sem, 1)
                dve.wait_ge(made.sem, 2)
                dve.tensor_copy(iota_row[:, :], ii[:, :]).then_inc(made2.sem, 1)
                dve.tensor_copy(iota_col[:, :], ic[:, :]).then_inc(made2.sem, 1)
                dve.wait_ge(made2.sem, 3)
                dve.tensor_scalar(ident[:, :], iota_row[:, :], iota_col[:, 0:1], None, ALU.is_equal)
                dve.tensor_scalar(identb[:, :], iota_row[:, :], iota_col[:, 0:1], None, ALU.is_equal)
                dve.tensor_scalar(before[:, :], iota_row[:, :], iota_col[:, 0:1], None, ALU.is_gt)
                for j in range(4):
                    dve.tensor_scalar(notbefore[:, j, :], iota_row[:, :], iota_col[:, 0:1], 4096.0,
                                      ALU.is_ge, ALU.mult)

            @block.sync
            def _(sp):
                sp.dma_start(xres[:, 0:T - 1, :], x_in[0:(T - 1) * P, :].rearrange("(t p) f -> p t f", p=P)).then_inc(loaded.sem, 16)
                sp.wait_ge(made2.sem, 1)
                sp.dma_start(xres[0:LAST, T - 1, :], x_in[(T - 1) * P:N, :]).then_inc(loaded.sem, 16)
                sp.wait_ge(loaded.sem, 32)
        made.base, made2.base, loaded.base = 2, 3, 32

        sort_edges(nc, sig, sb, ps, [(by_dst, A["dst"], A["src"], None), (by_src, A["src"], A["dst"], A["edge_weight"])], N, T, locals())

        K = dict(iota_row=iota_row, iota_col=iota_col, ident=ident, ones=ones, xres=xres, hres=hres, N=N, T=T, NT=NT, LAST=LAST)

        gat_layer(nc, sig, sb, ps, A, K, 0, by_dst,
                  [("L0", 4, A["L0_gnn_W"], "out_in", A["L0_gnn_att_src"], A["L0_gnn_att_dst"])], out)
        gat_layer(nc, sig, sb, ps, A, K, 1, by_dst,
                  [("L1", 8, A["L1_gnn_W"], "out_in", A["L1_gnn_attn_l"].rearrange("a h c -> (a h) c"),
                    A["L1_gnn_attn_r"].rearrange("a h c -> (a h) c"))], out)
        gat_layer(nc, sig, sb, ps, A, K, 2, by_src,
                  [("L2", 4, A["L2_gnn_W"], "head_in_out", A["L2_gnn_a_neigh"], A["L2_gnn_a_self"])], out)
        gat_layer(nc, sig, sb, ps, A, K, 3, by_dst,
                  [("L3a", 4, A["L3_gnn_W1"], "in_out", A["L3_gnn_a_src1"], A["L3_gnn_a_dst1"]),
                   ("L3b", 8, A["L3_gnn_W2"], "in_out", A["L3_gnn_a_src2"], A["L3_gnn_a_dst2"])], out)


def sort_edges(nc, sig, sb, ps, sorts, N, T, C):
    B = 4
    iota_row, iota_col, ident, identb = C["iota_row"], C["iota_col"], C["ident"], C["identb"]
    ones, onesb, n128b, before, notbefore = C["ones"], C["onesb"], C["n128b"], C["before"], C["notbefore"]
    G = len(sorts)
    graphs = [s[0] for s in sorts]
    E = sorts[0][1].shape[0]
    EC = graphs[0].edge_cols
    FULL, REST = E // EC, E % EC

    with ExitStack() as c:
        for g, _, _, w_in in sorts:
            COLS, SLOTS = g.cols, g.slots
            g.records = nc.dram_tensor(f"{g.name}_records", [SLOTS * P, 4], I32, kind="Internal").ap()
            g.k_key = sb("k_key", [P, COLS], I32, c)
            g.k_i = sb("k_i", [P, COLS], I32, c)
            g.k_lo = sb("k_lo", [P, COLS], F32, c)
            g.k_hi = sb("k_hi", [P, COLS], F32, c)
            g.k_f = sb("k_f", [P, COLS], F32, c)
            g.k_rec = sb("k_rec", [P, COLS, 4], I32, c)
            g.k_other = sb("k_other", [P, COLS], I32, c)
            g.k_w = sb("k_w", [P, COLS], F32, c) if w_in is not None else None
            g.k_far = sb("k_far", [P, COLS], F32, c)
            g.k_table = sb("k_table", [P, 2, B + 1, T], F32, c)
        ld, lds, prep = sig("sort_loaded"), sig("sort_stored"), sig("sort_prepared")
        init = sig("sort_init")

        with ExitStack() as c2, nc.Block() as block:
            blanks = [sb("k_blank", [P, g.slots, 4], I32, c2) for g in graphs]
            n_loads = sum(4 + (2 if s[3] is not None else 0) for s in sorts)

            @block.vector
            def _(dve):
                for g in graphs:
                    dve.memset(g.k_key[:, :], PAD_KEY)
                    if g.k_w is not None:
                        dve.memset(g.k_w[:, :], 0.0)
                    dve.memset(g.k_other[:, :], 0).then_inc(init.sem, 1)
                for blank in blanks:
                    dve.memset(blank[:, :, :], 0).then_inc(init.sem, 1)
                dve.wait_ge(init.sem, init.at(2 * G))
                for blank in blanks:
                    dve.memset(blank[:, :, 1:2].bitcast(F32), -1.0).then_inc(init.sem, 1)

            @block.sync
            def _(sp):
                sp.wait_ge(init.sem, init.at(G))
                for g, key_in, other_in, w_in in sorts:
                    loads = [(g.k_key[:, 0:EC], key_in), (g.k_other[:, 0:EC], other_in)]
                    if w_in is not None:
                        loads.append((g.k_w[:, 0:EC], w_in))
                    for dst, src in loads:
                        sp.dma_start(dst[0:FULL, :], src[0:FULL * EC].rearrange("(p c) -> p c", c=EC)).then_inc(ld.sem, 16)
                        sp.dma_start(dst[FULL:FULL + 1, 0:REST], src[FULL * EC:E].rearrange("(p c) -> p c", p=1)).then_inc(ld.sem, 16)
                sp.wait_ge(init.sem, init.at(3 * G))
                for g, blank in zip(graphs, blanks):
                    sp.dma_start(g.records.rearrange("(k s) f -> k s f", k=P), blank[:, :, :]).then_inc(lds.sem, 16)
                sp.wait_ge(ld.sem, ld.at(16 * n_loads))
                sp.wait_ge(lds.sem, lds.at(16 * G))

            @block.gpsimd
            def _(pool):
                pool.wait_ge(init.sem, init.at(G))
                for g in graphs:
                    if g.loop_cols:
                        pool.iota(g.k_key[:, EC:EC + T], [[P, T]], base=0, channel_multiplier=1)
                        pool.iota(g.k_other[:, EC:EC + T], [[P, T]], base=0, channel_multiplier=1)
        init.base += 3 * G
        ld.base += 16 * n_loads
        lds.base += 16 * G

        with nc.Block() as block:
            @block.vector
            def _(dve):
                n = [0]

                def link(ins):
                    n[0] += 1
                    ins.then_inc(prep.sem, 1)
                    dve.wait_ge(prep.sem, prep.at(n[0]))

                for g in graphs:
                    link(dve.tensor_copy(g.k_f[:, :], g.k_key[:, :]))
                    if g.loop_cols:
                        link(dve.tensor_scalar(g.k_far[:, :], g.k_f[:, :], float(N), float(PAD_KEY + 1), ALU.is_ge, ALU.mult))
                        link(dve.tensor_tensor(g.k_f[:, :], g.k_f[:, :], g.k_far[:, :], ALU.add))
                        link(dve.tensor_scalar(g.k_f[:, :], g.k_f[:, :], float(PAD_KEY), None, ALU.min))
                        link(dve.tensor_copy(g.k_key[:, :], g.k_f[:, :]))
                    link(dve.tensor_scalar(g.k_i[:, :], g.k_key[:, :], P - 1, None, ALU.bitwise_and))
                    link(dve.tensor_copy(g.k_lo[:, :], g.k_i[:, :]))
                    link(dve.tensor_scalar(g.k_i[:, :], g.k_key[:, :], 7, None, ALU.logical_shift_right))
                    link(dve.tensor_copy(g.k_hi[:, :], g.k_i[:, :]))
                    link(dve.tensor_scalar(g.k_far[:, :], g.k_hi[:, :], float(T), FAR, ALU.is_ge, ALU.mult))
                    link(dve.tensor_copy(g.k_rec[:, :, 0], g.k_other[:, :]))
                    link(dve.tensor_copy(g.k_rec[:, :, 1].bitcast(F32), g.k_lo[:, :]))
                    link(dve.tensor_copy(g.k_rec[:, :, 2], g.k_key[:, :]))
                    if g.k_w is not None:
                        link(dve.tensor_copy(g.k_rec[:, :, 3].bitcast(F32), g.k_w[:, :]))
                    else:
                        link(dve.memset(g.k_rec[:, :, 3], 0))
                prep.base += n[0]

        hot, hist, cnt, zm = sig("hist_onehots"), sig("hist_counted"), sig("hist_steps"), sig("hist_zero")
        with ExitStack() as c2, nc.Block() as block:
            ohlo = sb("h_lo", [P, 2, B, P], BF16, c2)
            ohhi = sb("h_hi", [P, 2, B, T], BF16, c2)
            zero = sb("h_zero", [P, P], BF16, c2)
            counts = sb("h_counts", [P, T], F32, c2)
            tot = sb("h_tot", [P, T], F32, c2)
            toti = sb("h_toti", [P, T], I32, c2)
            nslot = sb("h_nslot", [P, T], F32, c2)
            end = sb("h_end", [P, T], F32, c2)
            zrow = sb("h_zrow", [P, T], F32, c2)
            start = sb("h_start", [P, T], F32, c2)
            most = max(g.slots for g in graphs)
            slot_i = sb("h_sloti", [1, most], I32, c2)
            slot_f = sb("h_slotf", [1, most], F32, c2)
            ge = sb("h_ge", [1, most, T], F32, c2)
            tf = sb("h_tf", [1, most], F32, c2)
            tp = sb("h_tp", [1, most // 4], F32, c2)
            pcs = [ps("h_ps", [P, 512], F32, c2) for _ in graphs]
            pxs = [ps("h_px", [P, 2, 32], F32, c2) for _ in graphs]
            STEPS = 15

            @block.gpsimd
            def _(pool):
                pool.iota(slot_i[:, :], [[1, most]], base=0, channel_multiplier=0).then_inc(zm.sem, 1)

            @block.vector
            def _(dve):
                dve.memset(zero[:, :], 0.0).then_inc(zm.sem, 1)
                dve.memset(zrow[:, :], 0.0)
                made, opened = 0, 0
                for g in graphs:
                    opened += 1
                    NB2 = g.cols // (2 * B)
                    with dve.Fori(0, NB2) as i:
                        for par in range(2):
                            dve.wait_ge(hist.sem, hist.at(made + opened) + i * 2)
                            col = (i * 2 + par) * B
                            dve.tensor_tensor(ohlo[:, par, :, :], iota_row[:, :].unsqueeze(1).to_broadcast([P, B, P]),
                                              g.k_lo[:, bass.ds(col, B)].unsqueeze(2).to_broadcast([P, B, P]), ALU.is_equal).then_inc(hot.sem, 1)
                            dve.tensor_tensor(ohhi[:, par, :, :], iota_row[:, 0:T].unsqueeze(1).to_broadcast([P, B, T]),
                                              g.k_hi[:, bass.ds(col, B)].unsqueeze(2).to_broadcast([P, B, T]), ALU.is_equal).then_inc(hot.sem, 1)
                    made += 2 * NB2
                n = [0]

                def link(ins):
                    n[0] += 1
                    ins.then_inc(cnt.sem, 1)
                    dve.wait_ge(cnt.sem, cnt.at(n[0]))

                dve.wait_ge(hist.sem, hist.at(made + 2 * G))
                dve.wait_ge(zm.sem, zm.at(2))
                for k, g in enumerate(graphs):
                    SLOTS = g.slots
                    link(dve.tensor_copy(counts[:, :], pcs[k][:, 0:T]))
                    dve.wait_ge(hist.sem, hist.at(made + 2 * G + k + 1))
                    link(dve.tensor_scalar(tot[:, :], pxs[k][:, 1, 0:T], float(P - 1), None, ALU.add))
                    link(dve.tensor_copy(toti[:, :], tot[:, :]))
                    link(dve.tensor_scalar(toti[:, :], toti[:, :], 7, None, ALU.logical_shift_right))
                    link(dve.tensor_copy(nslot[:, :], toti[:, :]))
                    link(dve.tensor_tensor_scan(end[:, :], nslot[:, :], zrow[:, :], 0.0, ALU.add, ALU.add))
                    link(dve.tensor_tensor(start[:, :], end[:, :], nslot[:, :], ALU.subtract))
                    link(dve.scalar_tensor_tensor(g.k_table[:, 0, 0, :], start[:, :], float(P), pxs[k][:, 0, 0:T], ALU.mult, ALU.add))
                    link(dve.tensor_copy(slot_f[:, :], slot_i[:, :]))
                    link(dve.tensor_tensor(ge[:, 0:SLOTS, :], slot_f[:, 0:SLOTS].unsqueeze(2).to_broadcast([1, SLOTS, T]),
                                           end[0:1, :].unsqueeze(1).to_broadcast([1, SLOTS, T]), ALU.is_ge))
                    link(dve.tensor_reduce(tf[:, 0:SLOTS], ge[:, 0:SLOTS, :], X, ALU.add))
                    link(dve.tensor_scalar(tf[:, 0:SLOTS], tf[:, 0:SLOTS], float(T - 1), None, ALU.min))
                    four = tf[:, 0:SLOTS].rearrange("a (n b) -> a n b", b=4)
                    link(dve.scalar_tensor_tensor(tp[:, 0:SLOTS // 4], four[:, :, 3], float(T), four[:, :, 2], ALU.mult, ALU.add))
                    link(dve.scalar_tensor_tensor(tp[:, 0:SLOTS // 4], tp[:, 0:SLOTS // 4], float(T), four[:, :, 1], ALU.mult, ALU.add))
                    link(dve.scalar_tensor_tensor(g.tiles4[:, :], tp[:, 0:SLOTS // 4], float(T), four[:, :, 0], ALU.mult, ALU.add))

            @block.tensor
            def _(pe):
                pe.wait_ge(zm.sem, zm.at(2))
                made = 0
                for k, g in enumerate(graphs):
                    NB2 = g.cols // (2 * B)
                    pe.matmul(pcs[k][:, 0:T], zero[:, :], zero[:, 0:T], start=True, stop=False).then_inc(hist.sem, 1)
                    with pe.Fori(0, NB2) as i:
                        for par in range(2):
                            pe.wait_ge(hot.sem, hot.at(2 * made + 2 + 2 * par) + i * 4)
                            for j in range(B):
                                last = pe.matmul(pcs[k][:, 0:T], ohlo[:, par, j, :], ohhi[:, par, j, :], start=False, stop=False)
                            last.then_inc(hist.sem, 1)
                    made += 2 * NB2
                for k, g in enumerate(graphs):
                    pe.matmul(pcs[k][:, 0:T], zero[:, :], zero[:, 0:T], start=False, stop=True).then_inc(hist.sem, 1)
                for k, g in enumerate(graphs):
                    pe.wait_ge(cnt.sem, cnt.at(STEPS * k + 1))
                    pe.matmul(pxs[k][:, 0, 0:T], before[:, :], counts[:, :], start=True, stop=True)
                    pe.matmul(pxs[k][:, 1, 0:T], ones[:, :], counts[:, :], start=True, stop=True).then_inc(hist.sem, 1)
            made = sum(g.cols // B for g in graphs)
            hot.base += 2 * made
            hist.base += made + 3 * G
            cnt.base += STEPS * G
            zm.base += 2

        D = 13
        S = [{name: sig(f"{name}_{g.name}") for name in ("diag", "rows", "onehots", "counts", "looked", "placed", "steps", "ready")}
             for g in graphs]
        scat = [[sig(f"scattered{h}_{g.name}") for h in range(2)] for g in graphs]
        gate = sig("scatter_gate")
        with ExitStack() as c2, nc.Block() as block:
            def each(name, shape, dt):
                return [sb(name, shape, dt, c2) for _ in graphs]

            ohlo = each("r_lo", [P, B, P], BF16)
            ohhi = each("r_hi", [P, B, T], BF16)
            ohloT = each("r_loT", [P, B, P], F32)
            dlo = each("r_dlo", [P, 2, B, P], BF16)
            dhi = each("r_dhi", [P, 2, B, P], BF16)
            same = each("r_same", [P, B, P], F32)
            sel = each("r_sel", [P, B, T], F32)
            inside = each("r_in", [P, B], F32)
            found = each("r_found", [P, B], F32)
            q = each("r_q", [P, B], F32)
            qi = each("r_qi", [P, B], I32)
            qs = each("r_qs", [P, B], I32)
            qk = each("r_qk", [P, B], I32)
            idx = each("r_idx", [P, 2, B], I32)
            out4 = each("r_out", [P, 2, B, 4], I32)
            p_lo = [ps("r_plo", [P, 512], F32, c2) for _ in graphs]
            p_key = [ps("r_pkey", [P, 512], F32, c2) for _ in graphs]
            p_cnt = [ps("r_pc", [P, 4, P], F32, c2) for _ in graphs]
            p_look = [ps("r_pl", [P, 4, P], F32, c2) for _ in graphs]
            trips = [g.cols // (2 * B) for g in graphs]
            least = min(trips)

            def turns(eng, parts):
                def both(i, ks):
                    for half in range(2):
                        for part in parts:
                            for k in ks:
                                part(k, i * 2 + half, half, isinstance(i, int))
                both(0, range(G))
                with eng.Fori(1, least) as i:
                    both(i, range(G))
                for k in range(G):
                    if trips[k] > least:
                        with eng.Fori(least, trips[k]) as i:
                            both(i, [k])

            @block.scalar
            def _(act):
                def diagonals(k, n, half, first):
                    act.wait_ge(S[k]["rows"].sem, S[k]["rows"].at(1) + n)
                    for j in range(B):
                        col = n * B + j
                        act.activation(dlo[k][:, half, j, :], ident[:, :], ACT.Copy, scale=graphs[k].k_lo[:, bass.ds(col, 1)])
                        ins = act.activation(dhi[k][:, half, j, :], ident[:, :], ACT.Copy, scale=graphs[k].k_hi[:, bass.ds(col, 1)])
                    ins.then_inc(S[k]["diag"].sem, 1)
                turns(act, [diagonals])

            @block.tensor
            def _(pe):
                for k in range(G):
                    for _ in range(2):
                        pe.matmul(p_look[k][:, 0, :], ident[:, :], ident[:, :], start=True, stop=True).then_inc(S[k]["rows"].sem, 1)

                def spread(k, n, half, first):
                    pe.wait_ge(S[k]["diag"].sem, S[k]["diag"].at(1) + n)
                    pe.wait_ge(S[k]["ready"].sem, S[k]["ready"].at(1) + n)
                    lo4 = dlo[k][:, half, :, :].rearrange("p b q -> p (b q)")
                    hi4 = dhi[k][:, half, :, :].rearrange("p b q -> p (b q)")
                    pe.matmul(p_lo[k][:, :], onesb[:, :], lo4, start=True, stop=True)
                    pe.matmul(p_key[k][:, :], onesb[:, :], lo4, start=True, stop=False)
                    pe.matmul(p_key[k][:, :], n128b[:, :], hi4, start=False, stop=False)
                    pe.matmul(p_key[k][:, :], identb[:, :], notbefore[:, :, :].rearrange("p b q -> p (b q)"),
                              start=False, stop=True).then_inc(S[k]["rows"].sem, 1)

                def count(k, n, half, first):
                    pe.wait_ge(S[k]["onehots"].sem, S[k]["onehots"].at(1) + n)
                    for j in range(B):
                        ins = pe.matmul(p_cnt[k][:, j, 0:T], ohlo[k][:, j, :], ohhi[k][:, j, :], start=True, stop=True)
                    ins.then_inc(S[k]["counts"].sem, 1)

                def look(k, n, half, first):
                    pe.wait_ge(S[k]["ready"].sem, S[k]["ready"].at(2) + n)
                    for j in range(B):
                        ins = pe.matmul(p_look[k][:, j, 0:T], ohloT[k][:, j, :], graphs[k].k_table[:, half, j, :], start=True, stop=True)
                    ins.then_inc(S[k]["looked"].sem, 1)
                turns(pe, [spread, count, look])

            @block.vector
            def _(dve):
                for k in range(G):
                    dve.memset(qi[k][:, :], 0).then_inc(S[k]["ready"].sem, 1)

                def onehots(k, n, half, first):
                    g, s = graphs[k], S[k]
                    col = n * B
                    dve.tensor_tensor(ohlo[k][:, :, :], iota_row[:, :].unsqueeze(1).to_broadcast([P, B, P]),
                                      g.k_lo[:, bass.ds(col, B)].unsqueeze(2).to_broadcast([P, B, P]), ALU.is_equal)
                    dve.tensor_tensor(ohhi[k][:, :, :], iota_row[:, 0:T].unsqueeze(1).to_broadcast([P, B, T]),
                                      g.k_hi[:, bass.ds(col, B)].unsqueeze(2).to_broadcast([P, B, T]), ALU.is_equal).then_inc(s["onehots"].sem, 1)

                def count(k, n, half, first):
                    g, s = graphs[k], S[k]
                    col = n * B
                    base = s["steps"].at(0) + n * D
                    dve.wait_ge(s["rows"].sem, s["rows"].at(3) + n)
                    dve.tensor_scalar(ohloT[k][:, :, :], p_lo[k][:, :].rearrange("p (b q) -> p b q", b=B),
                                      iota_col[:, 0:1], None, ALU.is_equal).then_inc(s["steps"].sem, 1)
                    dve.tensor_tensor(same[k][:, :, :], p_key[k][:, :].rearrange("p (b q) -> p b q", b=B),
                                      g.k_f[:, bass.ds(col, B)].unsqueeze(2).to_broadcast([P, B, P]), ALU.is_equal).then_inc(s["steps"].sem, 1)
                    dve.wait_ge(s["counts"].sem, s["counts"].at(1) + n)
                    for j in range(B):
                        dve.wait_ge(s["steps"].sem, base + 2 + j)
                        dst = g.k_table[:, half, j + 1, :] if j < B - 1 else g.k_table[:, 1 - half, 0, :]
                        dve.tensor_tensor(dst, g.k_table[:, half, j, :], p_cnt[k][:, j, 0:T], ALU.add).then_inc(s["steps"].sem, 1)
                    dve.wait_ge(s["steps"].sem, base + 6)
                    dve.tensor_reduce(inside[k][:, :], same[k][:, :, :], X, ALU.add).then_inc(s["ready"].sem, 1)

                def place(k, n, half, first):
                    g, s = graphs[k], S[k]
                    col = n * B
                    base = s["steps"].at(0) + n * D
                    dve.wait_ge(s["looked"].sem, s["looked"].at(1) + n)
                    dve.tensor_tensor(sel[k][:, :, :], p_look[k][:, :, 0:T], ohhi[k][:, :, :], ALU.mult).then_inc(s["steps"].sem, 1)
                    dve.wait_ge(s["steps"].sem, base + 7)
                    dve.tensor_reduce(found[k][:, :], sel[k][:, :, :], X, ALU.add).then_inc(s["steps"].sem, 1)
                    dve.wait_ge(s["steps"].sem, base + 8)
                    dve.wait_ge(s["ready"].sem, s["ready"].at(2) + n)
                    dve.tensor_tensor(q[k][:, :], found[k][:, :], inside[k][:, :], ALU.add).then_inc(s["steps"].sem, 1)
                    dve.wait_ge(s["steps"].sem, base + 9)
                    dve.tensor_tensor(qi[k][:, :], q[k][:, :], g.k_far[:, bass.ds(col, B)], ALU.add).then_inc(s["steps"].sem, 1)
                    dve.wait_ge(s["steps"].sem, base + 10)
                    dve.tensor_scalar(qs[k][:, :], qi[k][:, :], 7, None, ALU.logical_shift_right).then_inc(s["steps"].sem, 1)
                    dve.tensor_scalar(qk[k][:, :], qi[k][:, :], P - 1, None, ALU.bitwise_and).then_inc(s["steps"].sem, 1)
                    if not first:
                        dve.wait_ge(scat[k][half].sem, scat[k][half].at(-half * 8 * B) + n * (8 * B))
                    dve.wait_ge(s["steps"].sem, base + 12)
                    dve.tensor_copy(out4[k][:, half, :, :], g.k_rec[:, bass.ds(col, B), :]).then_inc(s["steps"].sem, 1)
                    dve.wait_ge(s["steps"].sem, base + 13)
                    dve.scalar_tensor_tensor(idx[k][:, half, :], qk[k][:, :], float(g.slots), qs[k][:, :], ALU.mult, ALU.add).then_inc(s["placed"].sem, 1)
                turns(dve, [onehots, count, place])

            @block.gpsimd
            def _(pool):
                limits = [pool.to_reg(g.slots * P - 1) for g in graphs]

                def scatter(k, n, half, first):
                    pool.wait_ge(S[k]["placed"].sem, S[k]["placed"].at(1) + n)
                    pool.sem_inc(gate.sem, 1)
                    for j in range(B):
                        pool.indirect_dma_start(out=graphs[k].records, out_offset=bass.IndirectOffsetOnAxis(ap=idx[k][:, half, j:j + 1], axis=0),
                                                in_=out4[k][:, half, j, :], in_offset=None, bounds_check=limits[k],
                                                oob_is_err=False).then_inc(scat[k][half].sem, 16)
                turns(pool, [scatter])
                for k in range(G):
                    for half in range(2):
                        pool.wait_ge(scat[k][half].sem, scat[k][half].at(trips[k] * B * 16))
            for k in range(G):
                NB = 2 * trips[k]
                for name, more in (("diag", 0), ("rows", 2), ("onehots", 0), ("counts", 0), ("looked", 0), ("placed", 0), ("ready", 1)):
                    S[k][name].base += NB + more
                S[k]["steps"].base += NB * D
                for half in range(2):
                    scat[k][half].base += trips[k] * B * 16
                gate.base += NB
    for g in graphs:
        read_sorted(nc, sig, sb, ps, g, C)


def read_sorted(nc, sig, sb, ps, g, C):
    ident = C["ident"]
    records, SLOTS, R = g.records, g.slots, g.rows
    prep = sig("sort_prepared")
    ld = sig("sort_loaded")
    with ExitStack() as c, nc.Block() as block:
        recs = sb("s_recs", [P, SLOTS, 4], I32, c)
        keyf = sb("s_keyf", [P, SLOTS], F32, c)
        vld = sb("s_vld", [P, SLOTS], F32, c)
        KT = sb("s_KT", [R, 4 * P], F32, c)
        ends = sb("s_ends", [R, 2], F32, c)
        KE = sb("s_KE", [8, 2, R], F32, c)
        pk = ps("s_pk", [P, 512], F32, c)
        pe_ = ps("s_pe", [8, 2, 256], F32, c)
        tr = sig("sort_turned")
        oi = sb("s_oi", [P, SLOTS], I32, c)
        others = sb("s_others", [P, 2, SLOTS], F32, c)
        line = sb("s_line", [R, 3, 4 * P], BF16, c)
        pl = [ps("s_pl", [P, 512], F32, c) for _ in range(3)]
        lst, lin = sig("lines_stored"), sig("lines_made")

        @block.sync
        def _(sp):
            sp.dma_start(recs[:, :, :], records.rearrange("(k s) f -> k s f", k=P)).then_inc(ld.sem, 16)
            sp.wait_ge(tr.sem, tr.at(4))
            for k in range(3):
                sp.dma_start(g.lines[k].rearrange("(c q) -> c q", q=4 * P), line[:, k, :]).then_inc(lst.sem, 16)
            sp.wait_ge(lst.sem, lst.at(48))

        @block.scalar
        def _(act):
            act.wait_ge(tr.sem, tr.at(3))
            for k in range(3):
                ins = act.activation(line[:, k, :], pl[k][0:R, :], ACT.Copy)
            ins.then_inc(tr.sem, 1)

        @block.tensor
        def _(pe):
            pe.wait_ge(prep.sem, prep.at(5 + (g.name == "by_src")))
            for b in range(4):
                ins = pe.transpose(pk[0:R, b * P:(b + 1) * P], keyf[:, b:SLOTS:4], ident[:, :])
            ins.then_inc(tr.sem, 1)
            nn = 7 + (g.name == "by_src")
            pe.wait_ge(prep.sem, prep.at(nn + 1))
            for k in range(2):
                ins = pe.matmul(pe_[:, k, 0:R], ends[:, k:k + 1].to_broadcast([R, 8]), ident[0:R, 0:R], start=True, stop=True)
            ins.then_inc(tr.sem, 1)
            pe.wait_ge(lin.sem, lin.at(4))
            for k, src in enumerate((others[:, 0, :], others[:, 1, :], g.klo[:, :])):
                for b in range(4):
                    ins = pe.transpose(pl[k][0:R, b * P:(b + 1) * P], src[:, b:SLOTS:4], ident[:, :])
            ins.then_inc(tr.sem, 1)

        @block.vector
        def _(dve):
            n = [0]

            def link(ins):
                n[0] += 1
                ins.then_inc(prep.sem, 1)
                dve.wait_ge(prep.sem, prep.at(n[0]))

            def lowered(dst):
                link(dve.tensor_scalar(dst, dst, 1.0, -LOWEST, ALU.subtract, ALU.mult))

            dve.wait_ge(ld.sem, ld.at(16))
            link(dve.tensor_copy(g.klo[:, :], recs[:, :, 1].bitcast(F32)))
            dve.memset(g.other[:, SLOTS:SLOTS + 8], 0)
            link(dve.tensor_copy(g.other[:, 0:SLOTS], recs[:, :, 0]))
            link(dve.tensor_copy(g.key[:, :], recs[:, :, 2]))
            if g.name == "by_src":
                link(dve.tensor_copy(g.w[:, :], recs[:, :, 3].bitcast(F32)))
            link(dve.tensor_scalar(vld[:, :], g.klo[:, :], 0.0, -1.0e5, ALU.is_lt, ALU.mult))
            link(dve.tensor_tensor(keyf[:, :], g.key[:, :], vld[:, :], ALU.add))
            dve.wait_ge(tr.sem, tr.at(1))
            link(dve.tensor_copy(KT[:, :], pk[0:R, :]))
            link(dve.tensor_copy(ends[:, 0:1], KT[:, 0:1]))
            link(dve.tensor_copy(ends[:, 1:2], KT[:, 4 * P - 1:4 * P]))
            W = 4 * P
            link(dve.memset(g.negnew[:, 0:1], 0.0))
            link(dve.memset(g.negnewb[:, W - 1:W], 0.0))
            link(dve.tensor_tensor(g.negnew[:, 1:W], KT[:, 1:W], KT[:, 0:W - 1], ALU.is_equal))
            link(dve.tensor_tensor(g.negnewb[:, 0:W - 1], KT[:, 1:W], KT[:, 0:W - 1], ALU.is_equal))
            link(dve.tensor_scalar(g.negfirst[:, :], KT[:, :], ends[:, 0:1], None, ALU.is_equal))
            link(dve.tensor_scalar(g.neglast[:, :], KT[:, :], ends[:, 1:2], None, ALU.is_equal))
            for m in (g.negnew, g.negnewb, g.negfirst, g.neglast):
                lowered(m[:, :])
            dve.wait_ge(tr.sem, tr.at(2))
            link(dve.tensor_copy(KE[:, :, :], pe_[:, :, 0:R]))
            link(dve.memset(g.negcont[:, :], 0.0))
            link(dve.tensor_tensor(g.negcont[:, 1:R], KE[:, 0, 1:R], KE[:, 1, 0:R - 1], ALU.is_equal))
            link(dve.tensor_tensor(g.negthru[:, :], KE[:, 0, :], KE[:, 1, :], ALU.is_equal))
            link(dve.tensor_tensor(g.negthrub[:, :], g.negthru[:, :], g.negcont[:, 1:R + 1], ALU.mult))
            link(dve.tensor_tensor(g.negthru[:, :], g.negthru[:, :], g.negcont[:, 0:R], ALU.mult))
            for m in (g.negcont, g.negthru, g.negthrub):
                lowered(m[:, :])
            prep.base += n[0]
            dve.wait_ge(tr.sem, tr.at(2))
            for k, (amount, op) in enumerate(((P - 1, ALU.bitwise_and), (7, ALU.logical_shift_right))):
                dve.tensor_scalar(oi[:, :], g.other[:, 0:SLOTS], amount, None, op).then_inc(lin.sem, 1)
                dve.wait_ge(lin.sem, lin.at(2 * k + 1))
                dve.tensor_copy(others[:, k, :], oi[:, :]).then_inc(lin.sem, 1)
                dve.wait_ge(lin.sem, lin.at(2 * k + 2))
        tr.base += 4
        lin.base += 4
        lst.base += 48
        ld.base += 16


def gat_layer(nc, sig, sb, ps, A, K, n, g, convs, out):
    with ExitStack() as c:
        gat_layer_in(c, nc, sig, sb, ps, A, K, n, g, convs, out)


def gat_layer_in(lc, nc, sig, sb, ps, A, K, n, g, convs, out):
    N, T, NT, LAST = K["N"], K["T"], K["NT"], K["LAST"]
    xres, hres, ident, ones, iota_row = K["xres"], K["hres"], K["ident"], K["ones"], K["iota_row"]
    SLOTS, R = g.slots, g.rows
    NC = len(convs)
    FEAT = NC * CH
    HS = sum(c[1] for c in convs)
    WALL = FEAT + 2 * HS
    nodes = sb('node_scores', [P, T, 2 * HS], F32, lc)
    heads0 = [sum(c[1] for c in convs[:k]) for k in range(NC)]
    AW = CH + max(c[1] for c in convs)
    acc0 = [k * AW for k in range(NC)]
    feats = nc.dram_tensor(f"feats{n}", [NT, FEAT], F32, kind="Internal").ap()

    def rows_of(ap):
        return ap.rearrange("(a f) -> a f", a=1)

    steps, roots = sig("norm_steps"), sig("norm_roots")
    wld, tr, trc = sig("weights_loaded"), sig("weights_turned"), sig("weights_copied")
    with ExitStack() as c:
        wall = sb("wall", [P, 2, WALL], F32, c)
        hin = hres
        if n == 3:
            hin = sb("hnorm", [P, T, CH], F32, c)
        with ExitStack() as c2, nc.Block() as block:
            sq = sb("n_sq", [P, T, CH], F32, c2)
            mean = sb("n_mean", [P, T], F32, c2)
            var = sb("n_var", [P, T], F32, c2)
            std = sb("n_std", [P, T], F32, c2)
            gb = sb("n_gb", [P, 2, CH], F32, c2)
            woi = sb("w_oi", [P, 2, CH], F32, c2)
            attb = sb("w_att", [P, 2, 2 * HS], F32, c2)
            pw = ps("w_ps", [P, 2, CH], F32, c2)
            pf = ps("w_pf", [P, 2, 256], F32, c2)
            n_sqrt = 2 if n == 3 else 1
            n_dma = [(4 if cv[3] == "head_in_out" else 1) + 2 * cv[1] for cv in convs]
            gbl = sig("gamma_loaded")
            wz, wfree = sig("weights_zeroed"), sig("weights_free")

            @block.sync
            def _(sp):
                if n == 3:
                    sp.dma_start(gb[:, 0, :], rows_of(A["L3_gnn_gamma"]).to_broadcast([P, CH])).then_inc(gbl.sem, 16)
                    sp.dma_start(gb[:, 1, :], rows_of(A["L3_gnn_beta"]).to_broadcast([P, CH])).then_inc(gbl.sem, 16)
                for k, (_, H, W, form, a_from, a_to) in enumerate(convs):
                    C = CH // H
                    sp.wait_ge(wz.sem, wz.at(k + 1))
                    if form == "out_in":
                        sp.dma_start(woi[:, :, :], W.rearrange("(k p) f -> p k f", p=P)).then_inc(wld.sem, 16)
                    elif form == "in_out":
                        sp.dma_start(wall[:, :, k * CH:(k + 1) * CH], W.rearrange("(k p) f -> p k f", p=P)).then_inc(wld.sem, 16)
                    else:
                        for h in range(H):
                            sp.dma_start(wall[:, :, h * C:(h + 1) * C], W[h].rearrange("(k p) o -> p k o", p=P)).then_inc(wld.sem, 16)
                    for h in range(H):
                        r0, kk = (h * C) % P, (h * C) // P
                        for side, a in enumerate((a_from, a_to)):
                            col = side * HS + heads0[k] + h
                            sp.dma_start(attb[r0:r0 + C, kk, col:col + 1], a[h].rearrange("(c a) -> c a", a=1)).then_inc(wld.sem, 16)
                sp.wait_ge(wld.sem, wld.at(16 * sum(n_dma)))
                if n == 3:
                    sp.wait_ge(gbl.sem, gbl.at(32))

            @block.tensor
            def _(pe):
                for k, (_, H, W, form, _, _) in enumerate(convs):
                    pe.wait_ge(wld.sem, wld.at(16 * sum(n_dma[:k + 1])))
                    for a in range(2):
                        for b in range(2):
                            src = woi[:, a, b * P:(b + 1) * P] if form == "out_in" else wall[:, a, k * CH + b * P:k * CH + (b + 1) * P]
                            ins = pe.transpose(pw[:, b, a * P:(a + 1) * P], src, ident[:, :])
                    ins.then_inc(tr.sem, 1)
                    pe.wait_ge(trc.sem, trc.at(2 * k + 1))
                    hs = slice(heads0[k], heads0[k] + H)
                    for m in range(2):
                        for side in range(2):
                            col = side * HS + heads0[k]
                            for kk in range(2):
                                ins = pe.matmul(pf[:, m, col:col + H], woi[:, kk, m * P:(m + 1) * P],
                                                attb[:, kk, col:col + H], start=kk == 0, stop=kk == 1)
                    ins.then_inc(tr.sem, 1)

            @block.scalar
            def _(act):
                act.activation(attb[:, :, :], ident[:, 0:4 * HS].rearrange("p (k h) -> p k h", k=2), ACT.Copy, scale=0.0).then_inc(wz.sem, 1)
                for k, (_, H, W, form, _, _) in enumerate(convs):
                    act.wait_ge(tr.sem, tr.at(2 * k + 1))
                    dst = wall[:, :, k * CH:(k + 1) * CH] if form == "out_in" else woi[:, :, :]
                    act.activation(dst, pw[:, :, :], ACT.Copy).then_inc(trc.sem, 1)
                    act.wait_ge(tr.sem, tr.at(2 * k + 2))
                    for side in range(2):
                        col = side * HS + heads0[k]
                        ins = act.activation(wall[:, :, FEAT + col:FEAT + col + H], pf[:, :, col:col + H], ACT.Copy)
                    ins.then_inc(trc.sem, 1)
                    if k + 1 < NC:
                        act.wait_ge(trc.sem, trc.at(2 * k + 2))
                        act.sem_inc(wz.sem, 1)
                for r in range(n_sqrt):
                    act.wait_ge(steps.sem, steps.at(7 * (r + 1) if r == 0 else 7 + 3 + 7))
                    act.activation(std[:, :], var[:, :], ACT.Sqrt).then_inc(roots.sem, 1)

            @block.vector
            def _(dve):
                m = [0]

                def link(ins):
                    m[0] += 1
                    ins.then_inc(steps.sem, 1)
                    dve.wait_ge(steps.sem, steps.at(m[0]))

                def center(dst, src, r):
                    link(dve.tensor_reduce(mean[:, :], src[:, :, :], X, ALU.add))
                    link(dve.tensor_scalar(mean[:, :], mean[:, :], 1.0 / CH, None, ALU.mult))
                    link(dve.tensor_tensor(dst[:, :, :], src[:, :, :], mean[:, :].unsqueeze(2).to_broadcast([P, T, CH]), ALU.subtract))
                    link(dve.tensor_tensor(sq[:, :, :], dst[:, :, :], dst[:, :, :], ALU.mult))
                    link(dve.tensor_reduce(var[:, :], sq[:, :, :], X, ALU.add))
                    link(dve.tensor_scalar(var[:, :], var[:, :], 1.0 / CH, None, ALU.mult))
                    link(dve.tensor_scalar(var[:, :], var[:, :], EPS, None, ALU.add))
                    dve.wait_ge(roots.sem, roots.at(r + 1))
                    link(dve.reciprocal(mean[:, :], std[:, :]))
                    link(dve.tensor_tensor(dst[:, :, :], dst[:, :, :], mean[:, :].unsqueeze(2).to_broadcast([P, T, CH]), ALU.mult))

                center(hres, xres, 0)
                link(dve.tensor_scalar(hres[:, :, :], hres[:, :, :], 0.0, None, ALU.max))
                if n == 3:
                    center(hin, hres, 1)
                    dve.wait_ge(gbl.sem, gbl.at(32))
                    for k, op in enumerate((ALU.mult, ALU.add)):
                        link(dve.tensor_tensor(hin[:, :, :], hin[:, :, :], gb[:, k, :].unsqueeze(1).to_broadcast([P, T, CH]), op))
                steps.base += m[0]
            wld.base += 16 * sum(n_dma)
            tr.base += 2 * NC
            trc.base += 2 * NC
            wz.base += NC
            roots.base += n_sqrt
            if n == 3:
                gbl.base += 32

        hs_, ht, hc, hm, he = sig("tile_staged"), sig("tile_turned"), sig("tile_copied"), sig("tile_product"), sig("tile_evacuated")
        st = [sig(f"tile_stored{j}") for j in range(2)]
        with ExitStack() as c2, nc.Block() as block:
            hst = sb("t_st", [P, 2, CH], F32, c2)
            hT = sb("t_T", [P, 2, 2, P], F32, c2)
            row = sb("t_row", [P, 2, FEAT], F32, c2)
            pT = [ps(f"t_pT{j}", [P, 2, 256], F32, c2) for j in range(2)]
            pm = [ps(f"t_pm{j}", [P, 512], F32, c2) for j in range(2)]
            pn = [ps(f"t_pn{j}", [P, 512], F32, c2) for j in range(2)]
            MAIN = min(WALL, 512)

            def tiles(eng, body):
                for par in range(2):
                    body(par, 0, par)
                with eng.Fori(1, T // 2) as i:
                    for par in range(2):
                        body(i * 2 + par, i, par)
                if T % 2:
                    body(T - 1, T // 2, 0)

            @block.scalar
            def _(act):
                def body(t, i, par):
                    act.wait_ge(ht.sem, ht.at(1) + t)
                    act.activation(hst[:, par, :], hin[:, bass.ds(t, 1), :].rearrange("p a f -> p (a f)"), ACT.Copy).then_inc(hs_.sem, 1)
                    act.wait_ge(ht.sem, ht.at(3) + t)
                    act.wait_ge(hm.sem, hm.at(1) + t)
                    act.activation(hT[:, par, :, :], pT[par][:, :, 0:P], ACT.Copy).then_inc(hc.sem, 1)
                tiles(act, body)

            @block.tensor
            def _(pe):
                for j in range(2):
                    pe.matmul(pT[j][:, 0, 0:P], ident[:, :], ident[:, :], start=True, stop=True).then_inc(ht.sem, 1)
                for j in range(2):
                    pe.matmul(pm[j][:, 0:P], ident[:, :], ident[:, :], start=True, stop=True).then_inc(hm.sem, 1)

                def body(t, i, par):
                    pe.wait_ge(hs_.sem, hs_.at(1) + t)
                    for k in range(2):
                        ins = pe.transpose(pT[par][:, k, 0:P], hst[:, par, k * P:(k + 1) * P], ident[:, :])
                    ins.then_inc(ht.sem, 1)
                    pe.wait_ge(hc.sem, hc.at(1) + t)
                    pe.wait_ge(he.sem, he.at(1) + t)
                    for k in range(2):
                        ins = pe.matmul(pm[par][:, 0:MAIN], hT[:, par, k, :], wall[:, k, 0:MAIN], start=k == 0, stop=k == 1)
                    if WALL > MAIN:
                        for k in range(2):
                            ins = pe.matmul(pn[par][:, 0:WALL - MAIN], hT[:, par, k, :], wall[:, k, MAIN:WALL], start=k == 0, stop=k == 1)
                    ins.then_inc(hm.sem, 1)
                tiles(pe, body)

            @block.vector
            def _(dve):
                for j in range(2):
                    dve.memset(row[:, j, :], 0.0).then_inc(he.sem, 1)

                def body(t, i, par):
                    dve.wait_ge(hm.sem, hm.at(3) + t)
                    if not isinstance(i, int) or i > 0:
                        dve.wait_ge(st[par].sem, st[par].at(0) + i * 16)
                    dve.tensor_copy(row[:, par, :], pm[par][:, 0:FEAT])
                    scores = pn[par][:, 0:WALL - MAIN] if WALL > MAIN else pm[par][:, FEAT:WALL]
                    dve.tensor_copy(nodes[:, bass.ds(t, 1), :].rearrange("p a f -> p (a f)"), scores).then_inc(he.sem, 1)
                tiles(dve, body)

            @block.sync
            def _(sp):
                def body(t, i, par):
                    sp.wait_ge(he.sem, he.at(3) + t)
                    sp.dma_start(feats[bass.ds(t * P, P), :], row[:, par, :]).then_inc(st[par].sem, 16)
                tiles(sp, body)
                for j in range(2):
                    sp.wait_ge(st[j].sem, st[j].at(16 * (T // 2 + (1 - j) * (T % 2))))
            hs_.base += T
            ht.base += T + 2
            hc.base += T
            hm.base += T + 2
            he.base += T + 2
            for j in range(2):
                st[j].base += 16 * (T // 2 + (1 - j) * (T % 2))

    with ExitStack() as c:
        prob = sb("prob", [P, SLOTS, HS], F32, c)
        edge_scores(nc, sig, sb, ps, K, n, g, nodes, prob, HS)
        if n == 1:
            softmax_global(nc, sig, sb, ps, g, prob, HS, K)
        else:
            for k, (_, H, *_r) in enumerate(convs):
                softmax_runs(nc, sig, sb, ps, g, prob, heads0[k], H, K)

        acc = sb("acc", [P, T, NC * AW], F32, c)
        gin = [sig(f"rows_in{j}") for j in range(8)]
        cp, gate, msg_ok, act_ok, mm, ac = (sig("row_index"), sig("row_gate"), sig("messages_ready"), sig("messages_ready_too"),
                                            sig("slot_product"), sig("slot_added"))
        with ExitStack() as c2, nc.Block() as block:
            idx = sb("m_idx", [P, 2, 4], I32, c2)
            rows = sb("m_rows", [P, 8, FEAT], F32, c2)
            msg = sb("m_msg", [P, 4, NC * AW], F32, c2)
            oh = sb("m_oh", [P, 4, P], F32, c2)
            opened = sb("m_opened", [P, 1], F32, c2)
            pp = [ps("m_p", [P, NC, 512], F32, c2) for j in range(4)]
            NI = SLOTS // 8
            NB = SLOTS // 4

            @block.gpsimd
            def _(pool):
                limit = pool.to_reg(NT - 1)
                with pool.Fori(0, NI) as i:
                    for par in range(2):
                        nb = i * 2 + par
                        pool.wait_ge(cp.sem, cp.at(1) + nb)
                        pool.wait_ge(msg_ok.sem, msg_ok.at(4) + nb * 4)
                        pool.wait_ge(act_ok.sem, act_ok.at(4) + nb * 4)
                        pool.sem_inc(gate.sem, 1)
                        for j in range(4):
                            b = par * 4 + j
                            pool.indirect_dma_start(out=rows[:, b, :], out_offset=None, in_=feats,
                                                    in_offset=bass.IndirectOffsetOnAxis(ap=idx[:, par, j:j + 1], axis=0),
                                                    bounds_check=limit, oob_is_err=True).then_inc(gin[b].sem, 16)

            @block.scalar
            def _(act):
                act.wait_ge(ac.sem, ac.at(5))

                def indices(nb, par):
                    act.activation(idx[:, par, :], g.other[:, bass.ds(nb * 4, 4)], ACT.Copy).then_inc(cp.sem, 1)

                indices(0, 0)
                indices(1, 1)
                with act.Fori(0, NI) as i:
                    for b in range(8):
                        s = i * 8 + b
                        act.wait_ge(mm.sem, mm.at(1) + s)
                        act.wait_ge(gin[b].sem, gin[b].at(16) + i * 16)
                        for k, cv in enumerate(convs):
                            H = cv[1]
                            a = acc0[k] + CH
                            ins = act.activation(msg[:, b % 4, a:a + H],
                                                 prob[:, bass.ds(s, 1), heads0[k]:heads0[k] + H].rearrange("p a h -> p (a h)"), ACT.Copy)
                            if H == 4:
                                for h in range(H):
                                    C = CH // H
                                    ins = act.activation(msg[:, b % 4, acc0[k] + h * C:acc0[k] + (h + 1) * C],
                                                         rows[:, b, k * CH + h * C:k * CH + (h + 1) * C], ACT.Copy,
                                                         scale=prob[:, bass.ds(s, 1), heads0[k] + h:heads0[k] + h + 1].rearrange("p a h -> p (a h)"))
                        ins.then_inc(act_ok.sem, 1)
                        if b % 4 == 3:
                            act.wait_ge(msg_ok.sem, msg_ok.at(9) + s)
                            act.wait_ge(act_ok.sem, act_ok.at(9) + s)
                            indices(i * 2 + b // 4 + 2, b // 4)

            @block.tensor
            def _(pe):
                for j in range(4):
                    pe.matmul(pp[j][:, 0, 0:P], ident[:, :], ident[:, :], start=True, stop=True).then_inc(mm.sem, 1)
                with pe.Fori(0, NI) as i:
                    for b in range(8):
                        s = i * 8 + b
                        j = b % 4
                        pe.wait_ge(msg_ok.sem, msg_ok.at(9) + s)
                        pe.wait_ge(act_ok.sem, act_ok.at(9) + s)
                        pe.wait_ge(ac.sem, ac.at(2) + s)
                        for k in range(NC):
                            ins = pe.matmul(pp[j][:, k, 0:AW], oh[:, j, :], msg[:, j, acc0[k]:acc0[k] + AW], start=True, stop=True)
                        ins.then_inc(mm.sem, 1)

            @block.vector
            def _(dve):
                dve.memset(acc[:, :, :], 0.0).then_inc(ac.sem, 4)
                dve.memset(msg[:, :, :], 0.0).then_inc(ac.sem, 1)
                dve.memset(oh[:, :, :], 0.0).then_inc(msg_ok.sem, 8)
                dve.wait_ge(ac.sem, ac.at(5))
                dve.memset(opened[:, :], 0.0).then_inc(act_ok.sem, 8)
                dve.wait_ge(msg_ok.sem, msg_ok.at(8))

                def tile_ids(word):
                    v = dve.value_load(g.tiles4[0:1, bass.ds(word, 1)], min_val=0, max_val=T ** 4 - 1)
                    return [dve.snap((v // T ** b) % T) for b in range(4)]

                def message(i, b):
                    s = i * 8 + b
                    j = b % 4
                    dve.wait_ge(mm.sem, mm.at(1) + s)
                    ins = dve.tensor_scalar(oh[:, j, :], iota_row[:, :], g.klo[:, bass.ds(s, 1)], None, ALU.is_equal)
                    for k, cv in enumerate(convs):
                        H = cv[1]
                        C = CH // H
                        if H == 4:
                            continue
                        dve.wait_ge(gin[b].sem, gin[b].at(16) + i * 16)
                        ins = dve.tensor_tensor(msg[:, j, acc0[k]:acc0[k] + CH].rearrange("p (h c) -> p h c", h=H),
                                                rows[:, b, k * CH:(k + 1) * CH].rearrange("p (h c) -> p h c", h=H),
                                                prob[:, bass.ds(s, 1), heads0[k]:heads0[k] + H].rearrange("p a h -> p (a h)").unsqueeze(2).to_broadcast([P, H, C]),
                                                ALU.mult)
                    ins.then_inc(msg_ok.sem, 1)

                def add(s, j, tile):
                    dve.wait_ge(mm.sem, mm.at(5) + s)
                    dve.wait_ge(ac.sem, ac.at(5) + s)
                    a = acc[:, bass.ds(tile, 1), :].rearrange("p a (k f) -> p (a k) f", k=NC)
                    dve.tensor_tensor(a, a, pp[j][:, :, 0:AW], ALU.add).then_inc(ac.sem, 1)

                for b in range(4):
                    message(0, b)
                ids = tile_ids(0)
                for b in range(4):
                    message(0, 4 + b)
                    add(b, b, ids[b])
                with dve.Fori(1, NI) as i:
                    ids = tile_ids(i * 2 - 1)
                    for b in range(4):
                        message(i, b)
                        add(i * 8 + b - 4, b, ids[b])
                    ids = tile_ids(i * 2)
                    for b in range(4):
                        message(i, 4 + b)
                        add(i * 8 + b, b, ids[b])
                ids = tile_ids(NB - 1)
                for b in range(4):
                    add(SLOTS - 4 + b, b, ids[b])
            cp.base += NB + 2
            gate.base += NB
            msg_ok.base += SLOTS + 8
            act_ok.base += SLOTS + 8
            mm.base += SLOTS + 4
            ac.base += SLOTS + 5
            for j in range(8):
                gin[j].base += 16 * NI

        finish_layer(nc, sig, sb, ps, A, K, n, convs, acc, acc0, out)


def edge_scores(nc, sig, sb, ps, K, n, g, nodes, prob, H):
    SLOTS, T = g.slots, K["T"]
    iota_row, iota_col = K["iota_row"], K["iota_col"]
    B = 8
    NB = SLOTS // B
    PER = max(1, 512 // ((T + 1) * H))
    PER = 4 if PER >= 4 else PER
    BANKS = B // PER
    RING = min(8, 2 * BANKS)
    W = (T + 1) * H
    ldl = [sig(f"lines_in{j}") for j in range(2)]
    hot, picked, used, lk = sig("score_onehots"), sig("scores_picked"), sig("scores_used"), sig("score_steps")
    with ExitStack() as c, nc.Block() as block:
        line = sb("e_line", [P, 2, 2, B * P], BF16, c)
        lineh = sb("e_lineh", [T, 2, B * P], BF16, c)
        oh = sb("e_oh", [P, 2, 2, B * P], BF16, c)
        ohh = sb("e_ohh", [T, 2, B * P], BF16, c)
        parts = [sb("e_parts", [P, 3, T, H], BF16, c) for _ in range(2)]
        rest = sb("e_rest", [P, T, H], F32, c)
        low1 = sb("e_low1", [T, T], F32, c)
        low = sb("e_low", [T, T, H], BF16, c)
        best = sb("e_best", [P, 2, PER, H], F32, c)
        pb = [ps("e_pb", [P, 512], F32, c) for _ in range(RING)]

        def batches(eng, body, last=True):
            count = NB if last else NB - 1
            with eng.Fori(0, count // 2) as i:
                for par in range(2):
                    body(i * 2 + par, i, par)
            if count % 2:
                body(count - 1, count // 2, 0)

        @block.sync
        def _(sp):
            def body(nb, i, par):
                if par or not isinstance(nb, int):
                    pass
                sp.wait_ge(hot.sem, hot.at(1) + nb)
                for k, src in ((0, g.lines[0]), (1, g.lines[2])):
                    sp.dma_start(line[:, par, k, :], src[bass.ds(nb * (B * P), B * P)].rearrange("(a f) -> a f", a=1).to_broadcast([P, B * P])).then_inc(ldl[par].sem, 16)
                sp.dma_start(lineh[:, par, :], g.lines[1][bass.ds(nb * (B * P), B * P)].rearrange("(a f) -> a f", a=1).to_broadcast([T, B * P])).then_inc(ldl[par].sem, 16)
            batches(sp, body)

        @block.tensor
        def _(pe):
            def body(nb, i, par):
                pe.wait_ge(hot.sem, hot.at(3) + nb)
                for j in range(B):
                    if j % 4 == 0:
                        v = pe.value_load(g.tiles4[0:1, bass.ds(nb * 2 + j // 4, 1)], min_val=0, max_val=T ** 4 - 1)
                        ids = [pe.snap((v // T ** b) % T) for b in range(4)]
                    bank = (par * BANKS + j // PER) % RING
                    if j % PER == 0:
                        pe.wait_ge(used.sem, used.at(1) + nb * BANKS + j // PER)
                    a = (j % PER) * W
                    cols = slice(j * P, (j + 1) * P)
                    for k in range(3):
                        pe.matmul(pb[bank][:, a:a + T * H], oh[:, par, 0, cols], parts[0][:, k, :, :].rearrange("p t h -> p (t h)"),
                                  start=k == 0, stop=False)
                    pe.matmul(pb[bank][:, a:a + T * H], ohh[:, par, cols], low[:, :, :].rearrange("p t h -> p (t h)"),
                              start=False, stop=True)
                    for k in range(3):
                        ins = pe.matmul(pb[bank][:, a + T * H:a + W], oh[:, par, 1, cols],
                                        parts[1][:, k, bass.ds(ids[j % 4], 1), :].rearrange("p t h -> p (t h)"), start=k == 0, stop=k == 2)
                    if j % PER == PER - 1:
                        ins.then_inc(picked.sem, 1)
            batches(pe, body)

        @block.vector
        def _(dve):
            m = [0]

            def link(ins):
                m[0] += 1
                ins.then_inc(lk.sem, 1)
                dve.wait_ge(lk.sem, lk.at(m[0]))

            for side in range(2):
                src = nodes[:, :, side * H:(side + 1) * H]
                link(dve.tensor_copy(parts[side][:, 0, :, :], src))
                link(dve.tensor_tensor(rest[:, :, :], src, parts[side][:, 0, :, :], ALU.subtract))
                link(dve.tensor_copy(parts[side][:, 1, :, :], rest[:, :, :]))
                link(dve.tensor_tensor(rest[:, :, :], rest[:, :, :], parts[side][:, 1, :, :], ALU.subtract))
                link(dve.tensor_copy(parts[side][:, 2, :, :], rest[:, :, :]))
            link(dve.tensor_scalar(low1[:, :], iota_row[0:T, 0:T], iota_col[0:T, 0:1], LOWEST, ALU.not_equal, ALU.mult))
            link(dve.tensor_copy(low[:, :, :], low1[:, :].unsqueeze(2).to_broadcast([T, T, H])))
            link(dve.memset(best[:, :, :, :], 0.0))
            dve.memset(rest[:, 0, :], 0.0).then_inc(hot.sem, 2)
            dve.memset(rest[:, 1, :], 0.0).then_inc(used.sem, RING)
            dve.memset(rest[:, 2, :], 0.0).then_inc(picked.sem, 2 * BANKS)

            def onehots(nb, i, par):
                dve.wait_ge(ldl[par].sem, ldl[par].at(48) + i * 48)
                dve.wait_ge(picked.sem, picked.at(BANKS) + nb * BANKS)
                dve.tensor_scalar(oh[:, par, :, :], line[:, par, :, :], iota_col[:, 0:1], None, ALU.is_equal)
                dve.tensor_scalar(ohh[:, par, :], lineh[:, par, :], iota_col[0:T, 0:1], None, ALU.is_equal).then_inc(hot.sem, 1)

            def pick(nb, i, par):
                for r in range(BANKS):
                    bank = (par * BANKS + r) % RING
                    at = nb * BANKS + r
                    dve.wait_ge(picked.sem, picked.at(2 * BANKS + 1) + at)
                    v = pb[bank][:, 0:PER * W].rearrange("p (s w) -> p s w", s=PER)
                    dve.wait_ge(used.sem, used.at(RING) + at)
                    dve.tensor_reduce(best[:, r % 2, :, :], v[:, :, 0:T * H].rearrange("p s (t h) -> p s h t", h=H), X, ALU.max).then_inc(lk.sem, 1)
                    dve.wait_ge(lk.sem, lk.at(m[0] + 1) + at)
                    dve.tensor_tensor(prob[:, bass.ds(nb * B + r * PER, PER), :], best[:, r % 2, :, :], v[:, :, T * H:W], ALU.add).then_inc(used.sem, 1)

            onehots(0, 0, 0)

            def body(nb, i, par):
                onehots(nb + 1, i + par, 1 - par)
                pick(nb, i, par)
            batches(dve, body, last=False)
            pick(NB - 1, 0, (NB - 1) % 2)
            total = m[0] + NB * BANKS
            m[0] = total
            dve.wait_ge(used.sem, used.at(RING + NB * BANKS))
            link(dve.scalar_tensor_tensor(prob[:, :, :], prob[:, :, :], 0.2, prob[:, :, :], ALU.mult, ALU.max))
            if n == 2:
                link(dve.tensor_tensor(prob[:, :, :], prob[:, :, :], g.w[:, :].unsqueeze(2).to_broadcast([P, SLOTS, H]), ALU.mult))
            lk.base += m[0]
        hot.base += NB + 2
        picked.base += NB * BANKS + 2 * BANKS
        used.base += NB * BANKS + RING
        for j in range(2):
            ldl[j].base += 48 * (NB // 2 + (1 - j) * (NB % 2))


def softmax_global(nc, sig, sb, ps, g, prob, H, K):
    SLOTS = g.slots
    ident, ones = K["ident"], K["ones"]
    lk, tr = sig("softmax_steps"), sig("softmax_turned")
    with ExitStack() as c, nc.Block() as block:
        low = sb("x_low", [P, SLOTS], F32, c)
        top = sb("x_top", [P, H], F32, c)
        top1 = sb("x_top1", [H, 1], F32, c)
        diag = sb("x_diag", [H, H], F32, c)
        pt = ps("x_pt", [H, 512], F32, c)
        pb = ps("x_pb", [P, 512], F32, c)

        @block.vector
        def _(dve):
            m = [0]

            def link(ins):
                m[0] += 1
                ins.then_inc(lk.sem, 1)
                dve.wait_ge(lk.sem, lk.at(m[0]))
            link(dve.tensor_scalar(low[:, :], g.klo[:, :], 0.0, LOWEST, ALU.is_lt, ALU.mult))
            link(dve.tensor_tensor(prob[:, :, :], prob[:, :, :], low[:, :].unsqueeze(2).to_broadcast([P, SLOTS, H]), ALU.add))
            link(dve.tensor_reduce(top[:, :], prob[:, :, :].rearrange("p s h -> p h s"), X, ALU.max))
            dve.wait_ge(tr.sem, tr.at(1))
            link(dve.tensor_reduce(top1[:, :], pt[:, 0:P], X, ALU.max))
            link(dve.tensor_scalar(diag[:, :], ident[0:H, 0:H], top1[:, 0:1], None, ALU.mult))
            dve.wait_ge(tr.sem, tr.at(2))
            link(dve.tensor_copy(top[:, :], pb[:, 0:H]))
            link(dve.tensor_tensor(prob[:, :, :], prob[:, :, :], top[:, :].unsqueeze(1).to_broadcast([P, SLOTS, H]), ALU.subtract))

        @block.tensor
        def _(pe):
            pe.wait_ge(lk.sem, lk.at(3))
            pe.transpose(pt[:, 0:P], top[:, :], ident[:, :]).then_inc(tr.sem, 1)
            pe.wait_ge(lk.sem, lk.at(5))
            pe.matmul(pb[:, 0:H], ones[0:H, :], diag[:, :], start=True, stop=True).then_inc(tr.sem, 1)

        @block.scalar
        def _(act):
            act.wait_ge(lk.sem, lk.at(7))
            act.activation(prob[:, :, :], prob[:, :, :], ACT.Exp)
        lk.base += 7
        tr.base += 2


def softmax_runs(nc, sig, sb, ps, g, prob, h0, H, K):
    SLOTS, R = g.slots, g.rows
    W = 4 * P
    ident = K["ident"]
    lk, tr, ev, ex, back, bk = (sig("softmax_steps"), sig("softmax_turned"), sig("softmax_copied"),
                                sig("softmax_exps"), sig("softmax_back"), sig("softmax_done"))
    with ExitStack() as c, nc.Block() as block:
        sc = sb("y_sc", [R, H, W], F32, c)
        top = sb("y_top", [R, H, W], F32, c)
        tmp = sb("y_tmp", [R, W], F32, c)
        ends = sb("y_ends", [R, 2, H], F32, c)
        endT = sb("y_endT", [H, 2, R], F32, c)
        run = sb("y_run", [H, 2, R], F32, c)
        carry = sb("y_carry", [H, 2, R], F32, c)
        carryT = sb("y_carryT", [R, 2, H], F32, c)
        pt = [ps(f"y_pt{j}", [P, W], F32, c) for j in range(2)]
        pe1 = ps("y_pe", [H, 2, 256], F32, c)
        pe2 = ps("y_pf", [R, 2, 256], F32, c)
        pb = [ps(f"y_pb{j}", [P, W], F32, c) for j in range(2)]

        @block.tensor
        def _(pe):
            for h in range(H):
                if h >= 2:
                    pe.wait_ge(ev.sem, ev.at(h - 1))
                for b in range(4):
                    ins = pe.transpose(pt[h % 2][0:R, b * P:(b + 1) * P], prob[:, b:SLOTS:4, h0 + h], ident[:, :])
                ins.then_inc(tr.sem, 1)
            pe.wait_ge(lk.sem, lk.at(3 * H + 2))
            for k in range(2):
                ins = pe.transpose(pe1[:, k, 0:R], ends[:, k, :], ident[0:R, 0:R])
            ins.then_inc(tr.sem, 1)
            pe.wait_ge(lk.sem, lk.at(3 * H + 9))
            for k in range(2):
                ins = pe.transpose(pe2[:, k, 0:H], carry[:, k, :], ident[0:H, 0:H])
            ins.then_inc(tr.sem, 1)
            for h in range(H):
                pe.wait_ge(ex.sem, ex.at(h + 1))
                if h >= 2:
                    pe.wait_ge(bk.sem, bk.at(h - 1))
                for b in range(4):
                    ins = pe.transpose(pb[h % 2][:, b * R:(b + 1) * R], sc[:, h, b * P:(b + 1) * P], ident[0:R, 0:R])
                ins.then_inc(back.sem, 1)

        @block.scalar
        def _(act):
            for h in range(H):
                act.wait_ge(tr.sem, tr.at(h + 1))
                act.activation(sc[:, h, :], pt[h % 2][0:R, :], ACT.Copy).then_inc(ev.sem, 1)

            def turn_back(h):
                act.wait_ge(back.sem, back.at(h + 1))
                act.activation(prob[:, :, h0 + h].rearrange("p (c b) -> p b c", b=4),
                               pb[h % 2][:, 0:4 * R].rearrange("p (b c) -> p b c", b=4), ACT.Copy).then_inc(bk.sem, 1)
            for h in range(H):
                act.wait_ge(lk.sem, lk.at(3 * H + 10 + 3 * (h + 1)))
                act.activation(sc[:, h, :], sc[:, h, :], ACT.Exp).then_inc(ex.sem, 1)
                if h >= 1:
                    turn_back(h - 1)
            turn_back(H - 1)

        @block.vector
        def _(dve):
            m = [0]

            def link(ins):
                m[0] += 1
                ins.then_inc(lk.sem, 1)
                dve.wait_ge(lk.sem, lk.at(m[0]))
            for h in range(H):
                dve.wait_ge(ev.sem, ev.at(h + 1))
                link(dve.tensor_tensor_scan(top[:, h, :], g.negnew[:, :], sc[:, h, :], LOWEST, ALU.add, ALU.max))
                link(dve.tensor_tensor_scan(tmp[:, ::-1], g.negnewb[:, ::-1], sc[:, h, ::-1], LOWEST, ALU.add, ALU.max))
                link(dve.tensor_tensor(top[:, h, :], top[:, h, :], tmp[:, :], ALU.max))
            link(dve.tensor_copy(ends[:, 0, :], top[:, :, W - 1]))
            link(dve.tensor_copy(ends[:, 1, :], top[:, :, 0]))
            dve.wait_ge(tr.sem, tr.at(H + 1))
            link(dve.tensor_copy(endT[:, :, :], pe1[:, :, 0:R]))
            link(dve.tensor_tensor_scan(run[:, 0, :], g.negthru[0:H, :], endT[:, 0, :], LOWEST, ALU.add, ALU.max))
            link(dve.tensor_tensor_scan(run[:, 1, ::-1], g.negthrub[0:H, ::-1], endT[:, 1, ::-1], LOWEST, ALU.add, ALU.max))
            link(dve.memset(carry[:, 0, 0:1], LOWEST))
            link(dve.memset(carry[:, 1, R - 1:R], LOWEST))
            link(dve.tensor_tensor(carry[:, 0, 1:R], run[:, 0, 0:R - 1], g.negcont[0:H, 1:R], ALU.add))
            link(dve.tensor_tensor(carry[:, 1, 0:R - 1], run[:, 1, 1:R], g.negcont[0:H, 1:R], ALU.add))
            dve.wait_ge(tr.sem, tr.at(H + 2))
            link(dve.tensor_copy(carryT[:, :, :], pe2[:, :, 0:H]))
            for h in range(H):
                link(dve.scalar_tensor_tensor(top[:, h, :], g.negfirst[:, :], carryT[:, 0, h:h + 1], top[:, h, :], ALU.add, ALU.max))
                link(dve.scalar_tensor_tensor(top[:, h, :], g.neglast[:, :], carryT[:, 1, h:h + 1], top[:, h, :], ALU.add, ALU.max))
                link(dve.tensor_tensor(sc[:, h, :], sc[:, h, :], top[:, h, :], ALU.subtract))
        lk.base += 3 * H + 10 + 3 * H
        tr.base += H + 2
        ev.base += H
        ex.base += H
        back.base += H
        bk.base += H


def finish_layer(nc, sig, sb, ps, A, K, n, convs, acc, acc0, out):
    N, T, LAST = K["N"], K["T"], K["LAST"]
    xres, hres, ident = K["xres"], K["hres"], K["ident"]
    NC = len(convs)
    lk, ld, ex = sig("finish_steps"), sig("finish_loaded"), sig("finish_exps")
    biases = {0: ["L0_gnn_bias"], 1: [], 2: ["L2_gnn_bias"], 3: ["L3_gnn_b1", "L3_gnn_b2"]}[n]
    with ExitStack() as c, nc.Block() as block:
        bias = sb("f_bias", [P, 3, CH], F32, c)
        tmp = sb("f_tmp", [P, T, CH], F32, c)
        rden = sb("f_rden", [P, T, 8], F32, c)
        wu = sb("f_wu", [P, 4, CH], F32, c) if n == 3 else None
        waits = len(biases) + (2 if n == 3 else 0)

        @block.sync
        def _(sp):
            for k, name in enumerate(biases):
                b = A[name]
                b = b.rearrange("(a f) -> a f", a=1) if n != 2 else b.rearrange("h c -> (h c)").rearrange("(a f) -> a f", a=1)
                sp.dma_start(bias[:, k, :], b.to_broadcast([P, CH])).then_inc(ld.sem, 16)
            if n == 3:
                sp.dma_start(bias[:, 2, :], A["L3_gnn_bu"].rearrange("(a f) -> a f", a=1).to_broadcast([P, CH])).then_inc(ld.sem, 16)
                sp.dma_start(wu[:, :, :], A["L3_gnn_Wu"].rearrange("(k p) f -> p k f", p=P)).then_inc(ld.sem, 16)
            if waits:
                sp.wait_ge(ld.sem, ld.at(16 * waits))

        count = [0]
        exps = []

        @block.vector
        def _(dve):
            def link(ins):
                count[0] += 1
                ins.then_inc(lk.sem, 1)
                dve.wait_ge(lk.sem, lk.at(count[0]))

            if waits:
                dve.wait_ge(ld.sem, ld.at(16 * waits))
            for k, cv in enumerate(convs):
                H = cv[1]
                z = acc[:, :, acc0[k]:acc0[k] + CH]
                den = acc[:, :, acc0[k] + CH:acc0[k] + CH + H]
                if n == 1:
                    link(dve.tensor_scalar(den, den, 1e-6, None, ALU.max))
                elif n == 2:
                    link(dve.tensor_scalar(den, den, 1e-30, None, ALU.max))
                else:
                    link(dve.tensor_scalar(den, den, 1e-16, None, ALU.add))
                link(dve.reciprocal(rden[:, :, 0:H], den))
                z4 = z.rearrange("p t (h c) -> p t h c", h=H)
                link(dve.tensor_tensor(z4, z4, rden[:, :, 0:H].unsqueeze(3).to_broadcast([P, T, H, CH // H]), ALU.mult))
                if biases:
                    link(dve.tensor_tensor(z, z, bias[:, k, :].unsqueeze(1).to_broadcast([P, T, CH]), ALU.add))
                if n in (0, 3):
                    link(dve.tensor_scalar(tmp[:, :, :], z, 0.0, None, ALU.min))
                    exps.append(count[0])
                    dve.wait_ge(ex.sem, ex.at(len(exps)))
                    link(dve.tensor_scalar(tmp[:, :, :], tmp[:, :, :], 1.0, None, ALU.subtract))
                    link(dve.scalar_tensor_tensor(z, z, 0.0, tmp[:, :, :], ALU.max, ALU.add))
                if n == 2:
                    link(dve.tensor_scalar(z, z, 0.0, None, ALU.max))
                if n != 3:
                    link(dve.tensor_tensor(xres[:, :, :], xres[:, :, :], z, ALU.add))
            if n in (0, 3):
                link(dve.tensor_tensor(xres[:, :, :], xres[:, :, :], hres[:, :, :], ALU.add))
            if n == 3:
                link(dve.tensor_tensor(xres[:, :, :], xres[:, :, :], bias[:, 2, :].unsqueeze(1).to_broadcast([P, T, CH]), ALU.add))

        @block.scalar
        def _(act):
            for k in range(NC if n in (0, 3) else 0):
                act.wait_ge(lk.sem, lk.at(5 + 7 * k))
                act.activation(tmp[:, :, :], tmp[:, :, :], ACT.Exp).then_inc(ex.sem, 1)

        if n != 3:
            lk.base += count[0]
            ld.base += 16 * waits
            ex.base += 1 if n == 0 else 0
            return

        hs_, ht, hc, hm, he, st = (sig("tile_staged"), sig("tile_turned"), sig("tile_copied"), sig("tile_product"),
                                   sig("tile_evacuated"), sig("stored"))
        cat = sb("f_cat", [P, 2, 2 * CH], F32, c)
        catT = sb("f_catT", [P, 2, 4, P], F32, c)
        pT = [ps(f"f_pT{j}", [P, 512], F32, c) for j in range(2)]
        pm = [ps(f"f_pm{j}", [P, 512], F32, c) for j in range(2)]
        total = count[0]

        def tiles(eng, body):
            with eng.Fori(0, T // 2) as i:
                for par in range(2):
                    body(i * 2 + par, par)
            if T % 2:
                body(T - 1, 0)

        @block.scalar
        def _(act):
            act.wait_ge(lk.sem, lk.at(total))

            def body(t, par):
                act.wait_ge(ht.sem, ht.at(1) + t)
                for k in range(2):
                    ins = act.activation(cat[:, par, k * CH:(k + 1) * CH],
                                         acc[:, bass.ds(t, 1), acc0[k]:acc0[k] + CH].rearrange("p a f -> p (a f)"), ACT.Copy)
                ins.then_inc(hs_.sem, 1)
                act.wait_ge(ht.sem, ht.at(3) + t)
                act.wait_ge(hm.sem, hm.at(1) + t)
                act.activation(catT[:, par, :, :], pT[par][:, :].rearrange("p (k q) -> p k q", k=4), ACT.Copy).then_inc(hc.sem, 1)
            tiles(act, body)

        @block.tensor
        def _(pe):
            pe.wait_ge(ld.sem, ld.at(16 * waits))
            for j in range(2):
                pe.matmul(pT[j][:, 0:P], ident[:, :], ident[:, :], start=True, stop=True).then_inc(ht.sem, 1)
            for j in range(2):
                pe.matmul(pm[j][:, 0:P], ident[:, :], ident[:, :], start=True, stop=True).then_inc(hm.sem, 1)

            def body(t, par):
                pe.wait_ge(hs_.sem, hs_.at(1) + t)
                for k in range(4):
                    ins = pe.transpose(pT[par][:, k * P:(k + 1) * P], cat[:, par, k * P:(k + 1) * P], ident[:, :])
                ins.then_inc(ht.sem, 1)
                pe.wait_ge(hc.sem, hc.at(1) + t)
                pe.wait_ge(he.sem, he.at(1) + t)
                for k in range(4):
                    ins = pe.matmul(pm[par][:, 0:CH], catT[:, par, k, :], wu[:, k, :], start=k == 0, stop=k == 3)
                ins.then_inc(hm.sem, 1)
            tiles(pe, body)

        @block.vector
        def _(dve):
            dve.memset(rden[:, :, :], 0.0).then_inc(he.sem, 2)

            def body(t, par):
                dve.wait_ge(hm.sem, hm.at(3) + t)
                xt = xres[:, bass.ds(t, 1), :].rearrange("p a f -> p (a f)")
                dve.tensor_tensor(xt, xt, pm[par][:, 0:CH], ALU.add).then_inc(he.sem, 1)
            tiles(dve, body)

        @block.sync
        def _(sp):
            sp.wait_ge(he.sem, he.at(T + 2))
            sp.dma_start(out[0:(T - 1) * P, :].rearrange("(t p) f -> p t f", p=P), xres[:, 0:T - 1, :]).then_inc(st.sem, 16)
            sp.dma_start(out[(T - 1) * P:N, :], xres[0:LAST, T - 1, :]).then_inc(st.sem, 16)
            sp.wait_ge(st.sem, st.at(32))


_INS = ['x', 'src', 'dst', 'edge_weight', 'L0_gnn_W', 'L0_gnn_att_src', 'L0_gnn_att_dst', 'L0_gnn_bias', 'L1_gnn_W',
        'L1_gnn_attn_l', 'L1_gnn_attn_r', 'L2_gnn_W', 'L2_gnn_a_self', 'L2_gnn_a_neigh', 'L2_gnn_bias', 'L3_gnn_gamma',
        'L3_gnn_beta', 'L3_gnn_W1', 'L3_gnn_a_src1', 'L3_gnn_a_dst1', 'L3_gnn_b1', 'L3_gnn_W2', 'L3_gnn_a_src2',
        'L3_gnn_a_dst2', 'L3_gnn_b2', 'L3_gnn_Wu', 'L3_gnn_bu']
_OUTS = [((3125, 256), 'float32')]


def kernel(**inputs):
    import numpy as _np
    import concourse.bacc as _bacc
    from concourse import mybir as _mybir
    from concourse.bass_utils import run_bass_kernel_spmd as _run

    nc = _bacc.Bacc("TRN2", target_bir_lowering=False, num_devices=1)
    arrays, args = {}, {}
    for name in _INS:
        a = _np.ascontiguousarray(inputs[name])
        arrays[f"in_{name}_dram"] = a
        args[name] = nc.dram_tensor(f"in_{name}_dram", a.shape, _mybir.dt.from_np(a.dtype), kind="ExternalInput").ap()
    outs = []
    for i, (shape, dtype) in enumerate(_OUTS):
        dt = _mybir.dt.from_np(_np.dtype(dtype))
        outs.append(nc.dram_tensor(f"out_{i}_dram", shape, dt, kind="ExternalOutput").ap())
    build(nc, args, *outs)
    r = _run(nc, [arrays], core_ids=[0])
    got = tuple(r.results[0][f"out_{i}_dram"] for i in range(len(_OUTS)))
    return got[0]
```

```python
from contextlib import ExitStack

import concourse.bass as bass
from concourse import mybir

F32 = mybir.dt.float32
BF16 = mybir.dt.bfloat16
I32 = mybir.dt.int32
ALU = mybir.AluOpType
ACT = mybir.ActivationFunctionType
X = mybir.AxisListType.X

P = 128
CH = 256
LO = 128
LOWEST = -3.0e38
PAD_KEY = 4095
FAR = float(1 << 23) * 1.5
EPS = 1e-5


class Signal:

    def __init__(self, sem):
        self.sem = sem
        self.base = 0

    def at(self, n):
        return self.base + n


class Graph:

    def __init__(self, name, edges, nodes, loops):
        self.name = name
        self.tiles = -(-nodes // P)
        self.edge_cols = -(-edges // P)
        self.loop_cols = self.tiles if loops else 0
        self.cols = -(-(self.edge_cols + self.loop_cols) // 16) * 16
        real = edges + (nodes if loops else 0)
        self.slots = -(-((real + self.tiles * (P - 1)) // P) // 16) * 16
        self.rows = self.slots // 4


def later(t, least):
    return not isinstance(t, int) or t >= least


def staggered(eng, T, parts):
    ahead, behind = max(o for o, _ in parts), min(o for o, _ in parts)

    def step(t, par):
        for offset, body in parts:
            if isinstance(t, int) and not 0 <= t + offset < T:
                continue
            body(t + offset, (par + offset) % 2)

    first = -(-(2 - behind) // 2)
    last = (T - ahead) // 2
    for t in range(-ahead, 2 * first):
        step(t, t % 2)
    with eng.Fori(first, last) as i:
        for par in range(2):
            step(i * 2 + par, par)
    for t in range(2 * last, T - behind):
        step(t, t % 2)


def four_tiles(eng, g, word, T):
    v = eng.value_load(g.tiles4[0:1, bass.ds(word, 1)], min_val=0, max_val=T ** 4 - 1)
    return [eng.snap(v % T), eng.snap((v // T) % T), eng.snap((v // T ** 2) % T), eng.snap(v // T ** 3)]


def build(nc, A, out):
    x_in = A["x"]
    N = x_in.shape[0]
    E = A["src"].shape[0]
    T = -(-N // P)
    NT = T * P
    LAST = N - (T - 1) * P

    ctx = ExitStack()
    with ctx:
        signals = {}

        def sig(name):
            if name not in signals:
                signals[name] = Signal(ctx.enter_context(nc.semaphore(name)))
            return signals[name]

        used = {}

        def numbered(name):
            used[name] = used.get(name, 0) + 1
            return f"{name}.{used[name]}"

        def sb(name, shape, dt=F32, c=ctx):
            return c.enter_context(nc.sbuf_tensor(numbered(name), shape, dt))

        def ps(name, shape, dt, c):
            return c.enter_context(nc.psum_tensor(numbered(name), shape, dt))

        by_dst = Graph("by_dst", E, N, True)
        by_src = Graph("by_src", E, N, False)

        iota_row = sb("iota_row", [P, P])
        iota_col = sb("iota_col", [P, 1])
        iotab = sb("iotab", [P, P], BF16)
        ident = sb("ident", [P, P])
        identb = sb("identb", [P, P], BF16)
        ones = sb("ones", [P, P])
        onesb = sb("onesb", [P, P], BF16)
        n128b = sb("n128b", [P, P], BF16)
        before = sb("before", [P, P])
        notbefore = sb("notbefore", [P, 4, P], BF16)
        xres = sb("xres", [P, T, CH])
        hres = sb("hres", [P, T, CH])
        for g in (by_dst, by_src):
            g.klo = sb(f"{g.name}_klo", [P, g.slots])
            g.other = sb(f"{g.name}_other", [P, g.slots + 16], I32)
            g.negfirst = sb(f"{g.name}_negfirst", [g.rows, 4 * P])
            g.neglast = sb(f"{g.name}_neglast", [g.rows, 4 * P])
            g.negnew = sb(f"{g.name}_negnew", [g.rows, 4 * P])
            g.negnewb = sb(f"{g.name}_negnewb", [g.rows, 4 * P])
            g.negcont = sb(f"{g.name}_negcont", [8, g.rows + 1])
            g.negthru = sb(f"{g.name}_negthru", [8, g.rows])
            g.negthrub = sb(f"{g.name}_negthrub", [8, g.rows])
            g.tiles4 = sb(f"{g.name}_tiles4", [1, g.slots // 4], I32)
            g.lines = [nc.dram_tensor(f"{g.name}_{what}", [g.slots * P], BF16, kind="Internal").ap()
                       for what in ("other_row", "other_tile", "own_row")]
        by_src.w = sb("edge_w", [P, by_src.slots])

        made, made2, loaded = sig("const_made"), sig("const_made2"), sig("x_loaded")
        with ExitStack() as c, nc.Block() as block:
            ii = sb("iota_i", [P, P], I32, c)
            ic = sb("iota_ci", [P, 1], I32, c)

            @block.gpsimd
            def _(pool):
                pool.iota(ii[:, :], [[1, P]], base=0, channel_multiplier=0).then_inc(made.sem, 1)
                pool.iota(ic[:, :], [[1, 1]], base=0, channel_multiplier=1).then_inc(made.sem, 1)

            @block.vector
            def _(dve):
                dve.memset(ones[:, :], 1.0)
                dve.memset(onesb[:, :], 1.0)
                dve.memset(n128b[:, :], 128.0)
                dve.memset(xres[:, T - 1, :], 0.0).then_inc(made2.sem, 1)
                dve.wait_ge(made.sem, 2)
                dve.tensor_copy(iotab[:, :], ii[:, :])
                dve.tensor_copy(iota_row[:, :], ii[:, :]).then_inc(made2.sem, 1)
                dve.tensor_copy(iota_col[:, :], ic[:, :]).then_inc(made2.sem, 1)
                dve.wait_ge(made2.sem, 3)
                dve.tensor_scalar(ident[:, :], iota_row[:, :], iota_col[:, 0:1], None, ALU.is_equal)
                dve.tensor_scalar(identb[:, :], iota_row[:, :], iota_col[:, 0:1], None, ALU.is_equal)
                dve.tensor_scalar(before[:, :], iota_row[:, :], iota_col[:, 0:1], None, ALU.is_gt)
                for j in range(4):
                    dve.tensor_scalar(notbefore[:, j, :], iota_row[:, :], iota_col[:, 0:1], 4096.0,
                                      ALU.is_ge, ALU.mult)

            @block.sync
            def _(sp):
                sp.dma_start(xres[:, 0:T - 1, :], x_in[0:(T - 1) * P, :].rearrange("(t p) f -> p t f", p=P)).then_inc(loaded.sem, 16)
                sp.wait_ge(made2.sem, 1)
                sp.dma_start(xres[0:LAST, T - 1, :], x_in[(T - 1) * P:N, :]).then_inc(loaded.sem, 16)
        made.base, made2.base = 2, 3

        sort_edges(nc, sig, sb, ps, [(by_dst, A["dst"], A["src"], None), (by_src, A["src"], A["dst"], A["edge_weight"])], N, T, locals())

        K = dict(iota_row=iota_row, iota_col=iota_col, ident=ident, ones=ones, xres=xres, hres=hres, N=N, T=T, NT=NT, LAST=LAST)

        gat_layer(nc, sig, sb, ps, A, K, 0, by_dst,
                  [("L0", 4, A["L0_gnn_W"], "out_in", A["L0_gnn_att_src"], A["L0_gnn_att_dst"])], out)
        gat_layer(nc, sig, sb, ps, A, K, 1, by_dst,
                  [("L1", 8, A["L1_gnn_W"], "out_in", A["L1_gnn_attn_l"].rearrange("a h c -> (a h) c"),
                    A["L1_gnn_attn_r"].rearrange("a h c -> (a h) c"))], out)
        gat_layer(nc, sig, sb, ps, A, K, 2, by_src,
                  [("L2", 4, A["L2_gnn_W"], "head_in_out", A["L2_gnn_a_neigh"], A["L2_gnn_a_self"])], out)
        gat_layer(nc, sig, sb, ps, A, K, 3, by_dst,
                  [("L3a", 4, A["L3_gnn_W1"], "in_out", A["L3_gnn_a_src1"], A["L3_gnn_a_dst1"]),
                   ("L3b", 8, A["L3_gnn_W2"], "in_out", A["L3_gnn_a_src2"], A["L3_gnn_a_dst2"])], out)


def sort_edges(nc, sig, sb, ps, sorts, N, T, C):
    B = 4
    G = len(sorts)
    graphs = [s[0] for s in sorts]
    E = sorts[0][1].shape[0]
    EC = graphs[0].edge_cols
    FULL, REST = E // EC, E % EC

    with ExitStack() as c:
        for g, _, _, w_in in sorts:
            COLS, SLOTS = g.cols, g.slots
            g.records = nc.dram_tensor(f"{g.name}_records", [SLOTS * P, 4], F32, kind="Internal").ap()
            g.k_key = sb("k_key", [P, COLS], I32, c)
            g.k_i = sb("k_i", [P, COLS], I32, c)
            g.k_lo = sb("k_lo", [P, COLS + 2 * B], F32, c)
            g.k_hi = sb("k_hi", [P, COLS + 2 * B], F32, c)
            g.k_f = sb("k_f", [P, COLS], F32, c)
            g.k_rec = sb("k_rec", [P, COLS, 4], F32, c)
            g.k_other = sb("k_other", [P, COLS], I32, c)
            g.k_w = sb("k_w", [P, COLS], F32, c) if w_in is not None else None
            g.k_far = sb("k_far", [P, COLS], F32, c)
            g.k_table = sb("k_table", [P, 2, B + 1, T], F32, c)
        ld, lds, prep = sig("sort_loaded"), sig("sort_stored"), sig("sort_prepared")
        init = sig("sort_init")

        blanks = [sb("k_blank", [g.rows, 4 * P, 4], F32, c) for g in graphs]
        with ExitStack() as c2, nc.Block() as block:
            n_loads = sum(4 + (2 if s[3] is not None else 0) for s in sorts)

            @block.vector
            def _(dve):
                for g in graphs:
                    dve.memset(g.k_key[:, :], PAD_KEY)
                    if g.k_w is not None:
                        dve.memset(g.k_w[:, :], 0.0)
                    dve.memset(g.k_other[:, :], 0).then_inc(init.sem, 1)
                for blank in blanks:
                    dve.memset(blank[:, :, :], 0.0).then_inc(init.sem, 1)
                dve.wait_ge(init.sem, init.at(2 * G))
                for blank in blanks:
                    dve.memset(blank[:, :, 1:2], -1.0).then_inc(init.sem, 1)

            @block.sync
            def _(sp):
                sp.wait_ge(init.sem, init.at(G))
                for g, key_in, other_in, w_in in sorts:
                    loads = [(g.k_key[:, 0:EC], key_in), (g.k_other[:, 0:EC], other_in)]
                    if w_in is not None:
                        loads.append((g.k_w[:, 0:EC], w_in))
                    for dst, src in loads:
                        sp.dma_start(dst[0:FULL, :], src[0:FULL * EC].rearrange("(p c) -> p c", c=EC)).then_inc(ld.sem, 16)
                        sp.dma_start(dst[FULL:FULL + 1, 0:REST], src[FULL * EC:E].rearrange("(p c) -> p c", p=1)).then_inc(ld.sem, 16)
                sp.wait_ge(init.sem, init.at(3 * G))
                for g, blank in zip(graphs, blanks):
                    sp.dma_start(g.records.rearrange("(c q) f -> c q f", q=4 * P), blank[:, :, :]).then_inc(lds.sem, 16)
                sp.wait_ge(ld.sem, ld.at(16 * n_loads))

            @block.gpsimd
            def _(pool):
                pool.wait_ge(init.sem, init.at(G))
                for g in graphs:
                    if g.loop_cols:
                        pool.iota(g.k_key[:, EC:EC + T], [[P, T]], base=0, channel_multiplier=1)
                        pool.iota(g.k_other[:, EC:EC + T], [[P, T]], base=0, channel_multiplier=1)
        init.base += 3 * G
        ld.base += 16 * n_loads
        lds.base += 16 * G

        with nc.Block() as block:
            @block.vector
            def _(dve):
                n = [0]

                def link(ins):
                    n[0] += 1
                    ins.then_inc(prep.sem, 1)
                    dve.wait_ge(prep.sem, prep.at(n[0]))

                for g in graphs:
                    COLS = g.cols
                    link(dve.tensor_copy(g.k_f[:, :], g.k_key[:, :]))
                    if g.loop_cols:
                        link(dve.tensor_scalar(g.k_far[:, :], g.k_f[:, :], float(N), float(PAD_KEY + 1), ALU.is_ge, ALU.mult))
                        link(dve.tensor_tensor(g.k_f[:, :], g.k_f[:, :], g.k_far[:, :], ALU.add))
                        link(dve.tensor_scalar(g.k_f[:, :], g.k_f[:, :], float(PAD_KEY), None, ALU.min))
                        link(dve.tensor_copy(g.k_key[:, :], g.k_f[:, :]))
                    link(dve.tensor_scalar(g.k_i[:, :], g.k_key[:, :], P - 1, None, ALU.bitwise_and))
                    link(dve.tensor_copy(g.k_lo[:, 0:COLS], g.k_i[:, :]))
                    link(dve.tensor_scalar(g.k_i[:, :], g.k_key[:, :], 7, None, ALU.logical_shift_right))
                    link(dve.tensor_copy(g.k_hi[:, 0:COLS], g.k_i[:, :]))
                    link(dve.tensor_scalar(g.k_far[:, :], g.k_hi[:, 0:COLS], float(T), FAR, ALU.is_ge, ALU.mult))
                    link(dve.tensor_copy(g.k_rec[:, :, 0], g.k_other[:, :]))
                    link(dve.tensor_copy(g.k_rec[:, :, 1], g.k_lo[:, 0:COLS]))
                    link(dve.tensor_copy(g.k_rec[:, :, 2], g.k_key[:, :]))
                    if g.k_w is not None:
                        link(dve.tensor_copy(g.k_rec[:, :, 3], g.k_w[:, :]))
                    else:
                        link(dve.memset(g.k_rec[:, :, 3], 0.0))
                    link(dve.memset(g.k_lo[:, COLS:COLS + 2 * B], 0.0))
                    link(dve.memset(g.k_hi[:, COLS:COLS + 2 * B], 0.0))
                prep.base += n[0]

        hist = {g: Histogram(nc, sig, sb, ps, c, g, C, B, T) for g in graphs}
        first, second = graphs
        assert first.cols >= second.cols
        with nc.Block() as block:
            @block.vector
            def _(dve):
                hist[first].start(dve)
                with dve.Fori(0, first.cols // (4 * B)) as i:
                    for b in range(4):
                        hist[first].onehots(dve, i * 4 + b, b % 2)

            @block.tensor
            def _(pe):
                hist[first].open(pe)
                with pe.Fori(0, first.cols // (2 * B)) as i:
                    for par in range(2):
                        hist[first].count(pe, i * 2 + par, par)
        next_places(nc, sig, sb, ps, hist[first], C, B, T)
        place_edges(nc, sig, sb, ps, first, C, B, T, hist[second])
        next_places(nc, sig, sb, ps, hist[second], C, B, T)
        place_edges(nc, sig, sb, ps, second, C, B, T, None)
    for g in graphs:
        read_sorted(nc, sig, sb, ps, g, C)


class Histogram:

    def __init__(self, nc, sig, sb, ps, c, g, C, B, T):
        self.g, self.C, self.B, self.T = g, C, B, T
        self.ohlo = sb("h_lo", [P, 2, B, P], BF16, c)
        self.ohhi = sb("h_hi", [P, 2, B, T], BF16, c)
        self.zero = sb("h_zero", [P, P], BF16, c)
        self.sums = ps("h_ps", [P, 512], F32, c)
        self.zeroed, self.made, self.counted = [sig(f"hist_{what}_{g.name}") for what in ("zeroed", "onehots", "counted")]

    def start(self, dve):
        dve.memset(self.zero[:, :], 0.0).then_inc(self.zeroed.sem, 1)

    def onehots(self, dve, n, par):
        g, B, T, iotab, iota_row = self.g, self.B, self.T, self.C["iotab"], self.C["iota_row"]
        if later(n, 2):
            dve.wait_ge(self.counted.sem, self.counted.at(0) + n)
        for j in range(B):
            dve.tensor_scalar(self.ohlo[:, par, j, :], iotab[:, :], g.k_lo[:, bass.ds(n * B + j, 1)], None, ALU.is_equal)
        dve.tensor_tensor(self.ohhi[:, par, :, :], iota_row[:, 0:T].unsqueeze(1).to_broadcast([P, B, T]),
                          g.k_hi[:, bass.ds(n * B, B)].unsqueeze(2).to_broadcast([P, B, T]), ALU.is_equal).then_inc(self.made.sem, 1)

    def open(self, pe):
        pe.wait_ge(self.zeroed.sem, self.zeroed.at(1))
        pe.matmul(self.sums[:, 0:self.T], self.zero[:, :], self.zero[:, 0:self.T], start=True, stop=False).then_inc(self.counted.sem, 1)

    def count(self, pe, n, par):
        pe.wait_ge(self.made.sem, self.made.at(1) + n)
        for j in range(self.B):
            last = pe.matmul(self.sums[:, 0:self.T], self.ohlo[:, par, j, :], self.ohhi[:, par, j, :], start=False, stop=False)
        last.then_inc(self.counted.sem, 1)


def next_places(nc, sig, sb, ps, hist, C, B, T):
    g, ident, ones, before = hist.g, C["ident"], C["ones"], C["before"]
    SLOTS = g.slots
    cnt, closed, totals, made = sig("places_steps"), sig("places_closed"), sig("places_totals"), sig("places_iota")
    with ExitStack() as c, nc.Block() as block:
        counts = sb("h_counts", [P, T], F32, c)
        tot = sb("h_tot", [P, T], F32, c)
        toti = sb("h_toti", [P, T], I32, c)
        nslot = sb("h_nslot", [P, T], F32, c)
        end = sb("h_end", [P, T], F32, c)
        zrow = sb("h_zrow", [P, T], F32, c)
        start = sb("h_start", [P, T], F32, c)
        slot_i = sb("h_sloti", [T, SLOTS], I32, c)
        slot_f = sb("h_slotf", [T, SLOTS], F32, c)
        ends = sb("h_ends", [T, T], F32, c)
        end_col = sb("h_endcol", [T, 1], F32, c)
        ge = sb("h_ge", [T, SLOTS], F32, c)
        tf = sb("h_tf", [1, SLOTS], F32, c)
        tp = sb("h_tp", [1, SLOTS // 4], F32, c)
        px = ps("h_px", [P, 2, 32], F32, c)
        pt = ps("h_pt", [1, 512], F32, c)
        n = [0]

        @block.gpsimd
        def _(pool):
            pool.iota(slot_i[:, :], [[1, SLOTS]], base=0, channel_multiplier=0).then_inc(made.sem, 1)

        @block.tensor
        def _(pe):
            pe.matmul(hist.sums[:, 0:T], hist.zero[:, :], hist.zero[:, 0:T], start=False, stop=True).then_inc(closed.sem, 1)
            pe.wait_ge(cnt.sem, cnt.at(1))
            pe.matmul(px[:, 0, 0:T], before[:, :], counts[:, :], start=True, stop=True)
            pe.matmul(px[:, 1, 0:T], ones[:, :], counts[:, :], start=True, stop=True).then_inc(totals.sem, 1)
            pe.wait_ge(cnt.sem, cnt.at(13))
            pe.matmul(pt[:, 0:SLOTS], ones[0:T, 0:1], ge[:, :], start=True, stop=True).then_inc(totals.sem, 1)

        @block.vector
        def _(dve):
            def link(ins):
                n[0] += 1
                ins.then_inc(cnt.sem, 1)
                dve.wait_ge(cnt.sem, cnt.at(n[0]))

            dve.wait_ge(closed.sem, closed.at(1))
            link(dve.tensor_copy(counts[:, :], hist.sums[:, 0:T]))
            link(dve.memset(zrow[:, :], 0.0))
            dve.wait_ge(totals.sem, totals.at(1))
            link(dve.tensor_scalar(tot[:, :], px[:, 1, 0:T], float(P - 1), None, ALU.add))
            link(dve.tensor_copy(toti[:, :], tot[:, :]))
            link(dve.tensor_scalar(toti[:, :], toti[:, :], 7, None, ALU.logical_shift_right))
            link(dve.tensor_copy(nslot[:, :], toti[:, :]))
            link(dve.tensor_tensor_scan(end[:, :], nslot[:, :], zrow[:, :], 0.0, ALU.add, ALU.add))
            link(dve.tensor_tensor(start[:, :], end[:, :], nslot[:, :], ALU.subtract))
            link(dve.scalar_tensor_tensor(g.k_table[:, 1, B, :], start[:, :], float(P), px[:, 0, 0:T], ALU.mult, ALU.add))
            dve.wait_ge(made.sem, made.at(1))
            link(dve.tensor_copy(slot_f[:, :], slot_i[:, :]))
            link(dve.tensor_tensor(ends[:, :], end[0:T, :], ident[0:T, 0:T], ALU.mult))
            link(dve.tensor_reduce(end_col[:, :], ends[:, :], X, ALU.add))
            link(dve.tensor_scalar(ge[:, :], slot_f[:, :], end_col[:, 0:1], None, ALU.is_ge))
            dve.wait_ge(totals.sem, totals.at(2))
            link(dve.tensor_scalar(tf[:, :], pt[:, 0:SLOTS], float(T - 1), None, ALU.min))
            four = tf[:, :].rearrange("a (n b) -> a n b", b=4)
            link(dve.scalar_tensor_tensor(tp[:, :], four[:, :, 3], float(T), four[:, :, 2], ALU.mult, ALU.add))
            link(dve.scalar_tensor_tensor(tp[:, :], tp[:, :], float(T), four[:, :, 1], ALU.mult, ALU.add))
            link(dve.scalar_tensor_tensor(g.tiles4[:, :], tp[:, :], float(T), four[:, :, 0], ALU.mult, ALU.add))
        cnt.base += n[0]
        closed.base += 1
        totals.base += 2
        made.base += 1


def place_edges(nc, sig, sb, ps, g, C, B, T, other):
    iota_row, iotab, iota_col, ident, identb = C["iota_row"], C["iotab"], C["iota_col"], C["ident"], C["identb"]
    ones, onesb, n128b, notbefore = C["ones"], C["onesb"], C["n128b"], C["notbefore"]
    Q = 4
    D = 2
    S = {name: sig(f"sort_{name}") for name in ("diag", "rows", "rows_used", "onehots", "counts", "tables", "turned",
                                                "looked", "found", "records", "steps")}
    scat = [sig(f"scattered{h}") for h in range(Q)]
    gate, blank = sig("scatter_gate"), sig("sort_stored")
    with ExitStack() as c2, nc.Block() as block:
        ohlo = sb("r_lo", [P, 2, B, P], BF16, c2)
        ohhi = sb("r_hi", [P, 2, B, T], BF16, c2)
        ohloT = sb("r_loT", [P, B, P], F32, c2)
        dlo = sb("r_dlo", [P, 2, B, P], BF16, c2)
        dhi = sb("r_dhi", [P, 2, B, P], BF16, c2)
        same = sb("r_same", [P, B, P], F32, c2)
        sel = sb("r_sel", [P, 2, B, T + 2], F32, c2)
        found = sb("r_found", [P, Q, B], F32, c2)
        idx = sb("r_idx", [P, Q, B], I32, c2)
        rec = sb("r_rec", [P, Q, B, 4], F32, c2)
        p_lo = [ps("r_plo", [P, 512], F32, c2) for _ in range(2)]
        p_key = [ps("r_pkey", [P, 512], F32, c2) for _ in range(2)]
        p_tab = ps("r_pt", [P, B + 1, T], F32, c2)
        p_look = ps("r_pl", [P, 4, P], F32, c2)
        trips = g.cols // (Q * B)

        def turns(eng, parts, beside):
            def batches(i, ps):
                for quarter in range(Q):
                    for part in ps:
                        part(i * Q + quarter, quarter, i)

            shared = trips if other is None else other.g.cols // (Q * B)
            both = parts if other is None else parts[:-1] + beside + parts[-1:]
            batches(0, both)
            with eng.Fori(1, shared) as i:
                batches(i, both)
            if trips > shared:
                with eng.Fori(shared, trips) as i:
                    batches(i, parts)

        def ahead(part, by):
            return lambda n, quarter, i: part(n + by, quarter + by, i)

        @block.scalar
        def _(act):
            def diagonals(n, quarter, i):
                if later(n, 2):
                    act.wait_ge(S["rows"].sem, S["rows"].at(-1) + n)
                half = quarter % 2
                for j in range(B):
                    col = n * B + j
                    act.activation(dlo[:, half, j, :], ident[:, :], ACT.Copy, scale=g.k_lo[:, bass.ds(col, 1)])
                    ins = act.activation(dhi[:, half, j, :], ident[:, :], ACT.Copy, scale=g.k_hi[:, bass.ds(col, 1)])
                ins.then_inc(S["diag"].sem, 1)

            def table(n, quarter, i):
                act.wait_ge(S["counts"].sem, S["counts"].at(1) + n)
                act.activation(g.k_table[:, quarter % 2, :, :], p_tab[:, :, :], ACT.Copy).then_inc(S["tables"].sem, 1)

            def records(n, quarter, i):
                if later(i, 1):
                    act.wait_ge(scat[quarter].sem, scat[quarter].at(0) + i * (16 * B))
                act.activation(rec[:, quarter, :, :], g.k_rec[:, bass.ds(n * B, B), :], ACT.Copy)
                act.wait_ge(S["found"].sem, S["found"].at(1) + n)
                act.activation(idx[:, quarter, :], found[:, quarter, :], ACT.Copy).then_inc(S["records"].sem, 1)

            diagonals(0, 0, 0)
            diagonals(1, 1, 0)
            table(0, 0, 0)
            turns(act, [ahead(diagonals, 2), ahead(table, 1), records], [])

        @block.tensor
        def _(pe):
            def spread(n, quarter, i):
                half = quarter % 2
                pe.wait_ge(S["diag"].sem, S["diag"].at(1) + n)
                if later(n, 2):
                    pe.wait_ge(S["rows_used"].sem, S["rows_used"].at(-1) + n)
                lo4 = dlo[:, half, :, :].rearrange("p b q -> p (b q)")
                hi4 = dhi[:, half, :, :].rearrange("p b q -> p (b q)")
                pe.matmul(p_lo[half][:, :], onesb[:, :], lo4, start=True, stop=True)
                pe.matmul(p_key[half][:, :], onesb[:, :], lo4, start=True, stop=False)
                pe.matmul(p_key[half][:, :], n128b[:, :], hi4, start=False, stop=False)
                pe.matmul(p_key[half][:, :], identb[:, :], notbefore[:, :, :].rearrange("p b q -> p (b q)"),
                          start=False, stop=True).then_inc(S["rows"].sem, 1)

            def count(n, quarter, i):
                pe.wait_ge(S["onehots"].sem, S["onehots"].at(1) + n)
                if later(n, 1):
                    pe.wait_ge(S["tables"].sem, S["tables"].at(0) + n)
                pe.matmul(p_tab[:, :, :], ident[:, :], g.k_table[:, 1 - quarter % 2, B:B + 1, :].to_broadcast([P, B + 1, T]),
                          start=True, stop=False)
                for j in range(B):
                    ins = pe.matmul(p_tab[:, j + 1:B + 1, :], ohlo[:, quarter % 2, j, :],
                                    ohhi[:, quarter % 2, j:j + 1, :].to_broadcast([P, B - j, T]), start=False, stop=j == B - 1)
                ins.then_inc(S["counts"].sem, 1)

            def look(n, quarter, i):
                pe.wait_ge(S["turned"].sem, S["turned"].at(1) + n)
                pe.wait_ge(S["tables"].sem, S["tables"].at(1) + n)
                for j in range(B):
                    ins = pe.matmul(p_look[:, j, 0:T], ohloT[:, j, :], g.k_table[:, quarter % 2, j, :], start=True, stop=True)
                ins.then_inc(S["looked"].sem, 1)
            if other is not None:
                other.open(pe)
            spread(0, 0, 0)
            count(0, 0, 0)
            turns(pe, [ahead(spread, 1), look, ahead(count, 1)], [lambda n, quarter, i: other.count(pe, n, quarter % 2)])

        @block.vector
        def _(dve):
            def onehots(n, quarter, i):
                if later(n, 2):
                    dve.wait_ge(S["counts"].sem, S["counts"].at(-1) + n)
                for j in range(B):
                    dve.tensor_scalar(ohlo[:, quarter % 2, j, :], iotab[:, :], g.k_lo[:, bass.ds(n * B + j, 1)], None, ALU.is_equal)
                dve.tensor_tensor(ohhi[:, quarter % 2, :, :], iota_row[:, 0:T].unsqueeze(1).to_broadcast([P, B, T]),
                                  g.k_hi[:, bass.ds(n * B, B)].unsqueeze(2).to_broadcast([P, B, T]), ALU.is_equal).then_inc(S["onehots"].sem, 1)

            def before_in_column(n, quarter, i):
                if later(n, 2):
                    dve.wait_ge(S["found"].sem, S["found"].at(-1) + n)
                dve.tensor_copy(sel[:, quarter % 2, :, T + 1], g.k_far[:, bass.ds(n * B, B)]).then_inc(S["steps"].sem, 1)
                dve.wait_ge(S["rows"].sem, S["rows"].at(1) + n)
                dve.tensor_scalar(ohloT[:, :, :], p_lo[quarter % 2][:, :].rearrange("p (b q) -> p b q", b=B),
                                  iota_col[:, 0:1], None, ALU.is_equal).then_inc(S["turned"].sem, 1)
                for j in range(B):
                    ins = dve.scalar_tensor_tensor(same[:, j, :], p_key[quarter % 2][:, j * P:(j + 1) * P], g.k_f[:, bass.ds(n * B + j, 1)],
                                                   ones[:, :], ALU.is_equal, ALU.mult, accum_out=sel[:, quarter % 2, j, T:T + 1])
                ins.then_inc(S["rows_used"].sem, 1)

            def place(n, quarter, i):
                dve.wait_ge(S["looked"].sem, S["looked"].at(1) + n)
                dve.tensor_tensor(sel[:, quarter % 2, :, 0:T], p_look[:, :, 0:T], ohhi[:, quarter % 2, :, :], ALU.mult).then_inc(S["steps"].sem, 1)
                dve.wait_ge(S["steps"].sem, S["steps"].at(2) + n * D)
                dve.wait_ge(S["rows_used"].sem, S["rows_used"].at(1) + n)
                dve.tensor_reduce(found[:, quarter, :], sel[:, quarter % 2, :, :], X, ALU.add).then_inc(S["found"].sem, 1)
            if other is not None:
                other.start(dve)
            onehots(0, 0, 0)
            turns(dve, [before_in_column, ahead(onehots, 1), place], [lambda n, quarter, i: other.onehots(dve, n, quarter % 2)])

        @block.gpsimd
        def _(pool):
            limit = pool.to_reg(g.slots * P - 1)
            pool.wait_ge(blank.sem, blank.at(0))

            def scatter(n, quarter, i):
                pool.wait_ge(S["records"].sem, S["records"].at(1) + n)
                pool.sem_inc(gate.sem, 1)
                for j in range(B):
                    pool.indirect_dma_start(out=g.records, out_offset=bass.IndirectOffsetOnAxis(ap=idx[:, quarter, j:j + 1], axis=0),
                                            in_=rec[:, quarter, j, :], in_offset=None, bounds_check=limit,
                                            oob_is_err=False).then_inc(scat[quarter].sem, 16)
            turns(pool, [scatter], [])
            for quarter in range(Q):
                pool.wait_ge(scat[quarter].sem, scat[quarter].at(trips * B * 16))
        for name in S:
            extra = {"diag": 2, "rows": 1, "onehots": 1, "counts": 1, "tables": 1}.get(name, 0)
            S[name].base += Q * trips * (D if name == "steps" else 1) + extra
        for quarter in range(Q):
            scat[quarter].base += trips * B * 16
        gate.base += Q * trips


def read_sorted(nc, sig, sb, ps, g, C):
    ident = C["ident"]
    records, SLOTS, R = g.records, g.slots, g.rows
    prep = sig("sort_prepared")
    ld = sig("sort_loaded")
    with ExitStack() as c, nc.Block() as block:
        recs = sb("s_recs", [R, 4 * P, 4], F32, c)
        KT = sb("s_KT", [R, 4 * P], F32, c)
        ends = sb("s_ends", [R, 2], F32, c)
        KE = sb("s_KE", [8, 2, R], F32, c)
        pe_ = ps("s_pe", [8, 2, 256], F32, c)
        tr = sig("sort_turned")
        oi = sb("s_oi", [R, 2, 4 * P], I32, c)
        line = sb("s_line", [R, 3, 4 * P], BF16, c)
        fields = (1, 0, 3) if g.name == "by_src" else (1, 0)
        pl = [ps("s_pl", [P, 512], F32, c) for _ in fields]
        lst, lin = sig("lines_stored"), sig("lines_made")

        @block.sync
        def _(sp):
            sp.dma_start(recs[:, :, :], records.rearrange("(c q) f -> c q f", q=4 * P)).then_inc(ld.sem, 16)
            sp.wait_ge(lin.sem, lin.at(6))
            for k in range(3):
                sp.dma_start(g.lines[k].rearrange("(c q) -> c q", q=4 * P), line[:, k, :]).then_inc(lst.sem, 16)
            sp.wait_ge(lst.sem, lst.at(48))

        @block.scalar
        def _(act):
            act.wait_ge(tr.sem, tr.at(1))
            act.activation(g.klo[:, :].rearrange("p (c b) -> p b c", b=4), pl[0][:, 0:4 * R].rearrange("p (b c) -> p b c", b=4), ACT.Copy)
            if g.name == "by_src":
                act.activation(g.w[:, :].rearrange("p (c b) -> p b c", b=4), pl[2][:, 0:4 * R].rearrange("p (b c) -> p b c", b=4), ACT.Copy)

        @block.tensor
        def _(pe):
            pe.wait_ge(ld.sem, ld.at(16))
            for k, f in enumerate(fields):
                for b in range(4):
                    ins = pe.transpose(pl[k][:, b * R:(b + 1) * R], recs[:, b * P:(b + 1) * P, f], ident[0:R, 0:R])
            ins.then_inc(tr.sem, 1)
            pe.wait_ge(prep.sem, prep.at(4))
            for k in range(2):
                ins = pe.matmul(pe_[:, k, 0:R], ends[:, k:k + 1].to_broadcast([R, 8]), ident[0:R, 0:R], start=True, stop=True)
            ins.then_inc(tr.sem, 1)

        @block.vector
        def _(dve):
            n = [0]

            def link(ins):
                n[0] += 1
                ins.then_inc(prep.sem, 1)
                dve.wait_ge(prep.sem, prep.at(n[0]))

            def lowered(dst):
                link(dve.tensor_scalar(dst, dst, 1.0, -LOWEST, ALU.subtract, ALU.mult))

            dve.wait_ge(ld.sem, ld.at(16))
            link(dve.tensor_scalar(KT[:, :], recs[:, :, 1], 0.0, -1.0e5, ALU.is_lt, ALU.mult))
            link(dve.tensor_tensor(KT[:, :], KT[:, :], recs[:, :, 2], ALU.add))
            link(dve.tensor_copy(ends[:, 0:1], KT[:, 0:1]))
            link(dve.tensor_copy(ends[:, 1:2], KT[:, 4 * P - 1:4 * P]))
            dve.tensor_copy(line[:, 2, :], recs[:, :, 1]).then_inc(lin.sem, 1)
            dve.tensor_copy(oi[:, 0, :], recs[:, :, 0]).then_inc(lin.sem, 1)
            dve.wait_ge(lin.sem, lin.at(2))
            dve.tensor_scalar(oi[:, 1, :], oi[:, 0, :], 7, None, ALU.logical_shift_right).then_inc(lin.sem, 1)
            dve.wait_ge(lin.sem, lin.at(3))
            dve.tensor_copy(line[:, 1, :], oi[:, 1, :])
            dve.tensor_scalar(oi[:, 0, :], oi[:, 0, :], P - 1, None, ALU.bitwise_and).then_inc(lin.sem, 1)
            dve.wait_ge(lin.sem, lin.at(4))
            dve.tensor_copy(line[:, 0, :], oi[:, 0, :]).then_inc(lin.sem, 2)
            dve.memset(g.other[:, SLOTS:SLOTS + 16], 0)
            dve.wait_ge(tr.sem, tr.at(1))
            dve.tensor_copy(g.other[:, 0:SLOTS].rearrange("p (c b) -> p b c", b=4), pl[1][:, 0:4 * R].rearrange("p (b c) -> p b c", b=4))
            W = 4 * P
            link(dve.memset(g.negnew[:, 0:1], 0.0))
            link(dve.memset(g.negnewb[:, W - 1:W], 0.0))
            link(dve.tensor_tensor(g.negnew[:, 1:W], KT[:, 1:W], KT[:, 0:W - 1], ALU.is_equal))
            link(dve.tensor_tensor(g.negnewb[:, 0:W - 1], KT[:, 1:W], KT[:, 0:W - 1], ALU.is_equal))
            link(dve.tensor_scalar(g.negfirst[:, :], KT[:, :], ends[:, 0:1], None, ALU.is_equal))
            link(dve.tensor_scalar(g.neglast[:, :], KT[:, :], ends[:, 1:2], None, ALU.is_equal))
            for m in (g.negnew, g.negnewb, g.negfirst, g.neglast):
                lowered(m[:, :])
            dve.wait_ge(tr.sem, tr.at(2))
            link(dve.tensor_copy(KE[:, :, :], pe_[:, :, 0:R]))
            link(dve.memset(g.negcont[:, :], 0.0))
            link(dve.tensor_tensor(g.negcont[:, 1:R], KE[:, 0, 1:R], KE[:, 1, 0:R - 1], ALU.is_equal))
            link(dve.tensor_tensor(g.negthru[:, :], KE[:, 0, :], KE[:, 1, :], ALU.is_equal))
            link(dve.tensor_tensor(g.negthrub[:, :], g.negthru[:, :], g.negcont[:, 1:R + 1], ALU.mult))
            link(dve.tensor_tensor(g.negthru[:, :], g.negthru[:, :], g.negcont[:, 0:R], ALU.mult))
            for m in (g.negcont, g.negthru, g.negthrub):
                lowered(m[:, :])
            prep.base += n[0]
        tr.base += 2
        lin.base += 6
        lst.base += 48
        ld.base += 16


def gat_layer(nc, sig, sb, ps, A, K, n, g, convs, out):
    with ExitStack() as c:
        gat_layer_in(c, nc, sig, sb, ps, A, K, n, g, convs, out)


def gat_layer_in(lc, nc, sig, sb, ps, A, K, n, g, convs, out):
    N, T, NT, LAST = K["N"], K["T"], K["NT"], K["LAST"]
    xres, hres, ident, ones, iota_row = K["xres"], K["hres"], K["ident"], K["ones"], K["iota_row"]
    SLOTS = g.slots
    NC = len(convs)
    FEAT = NC * CH
    HS = sum(c[1] for c in convs)
    WALL = FEAT + 2 * HS
    nodes = sb('node_scores', [P, T, 2 * HS], F32, lc)
    heads0 = [sum(c[1] for c in convs[:k]) for k in range(NC)]
    AW = CH + max(c[1] for c in convs)
    acc0 = [k * AW for k in range(NC)]
    feats = nc.dram_tensor(f"feats{n}", [NT, FEAT], F32, kind="Internal").ap()

    steps, roots = sig("norm_steps"), sig("norm_roots")
    loaded = sig("x_loaded")
    wld, tr, trc = sig("weights_loaded"), sig("weights_turned"), sig("weights_copied")
    with ExitStack() as c:
        wall = sb("wall", [P, 2, WALL], F32, c)
        rstd = sb("n_rstd", [P, T], F32, c)
        shift = sb("n_shift", [P, T], F32, c)
        gb = sb("n_gb", [P, 2, 2], F32, c)
        with ExitStack() as c2, nc.Block() as block:
            total = sb("n_total", [P, T], F32, c2)
            nmean = sb("n_nmean", [P, T], F32, c2)
            ss = sb("n_ss", [P, T], F32, c2)
            var = sb("n_var", [P, T], F32, c2)
            std = sb("n_std", [P, T], F32, c2)
            squared = sig("norm_squared")
            CHUNK = 5
            sq = sb("n_sq", [P, CHUNK, CH], F32, c2)
            NORM = 2 * (T // CHUNK) + 3
            woi = sb("w_oi", [P, 2, CH], F32, c2)
            attb = sb("w_att", [P, 2, 2 * HS], F32, c2)
            pw = ps("w_ps", [P, 2, CH], F32, c2)
            pf = ps("w_pf", [P, 2, 256], F32, c2)
            n_sqrt = 2 if n == 3 else 1
            n_dma = [(4 if cv[3] == "head_in_out" else 1) + 2 * cv[1] for cv in convs]
            gbl = sig("gamma_loaded")
            wz = sig("weights_zeroed")

            @block.sync
            def _(sp):
                if n == 3:
                    for k in range(2):
                        for j, name in enumerate(("L3_gnn_gamma", "L3_gnn_beta")):
                            sp.dma_start(gb[:, j, k:k + 1], A[name][k * P:(k + 1) * P].rearrange("(c a) -> c a", a=1)).then_inc(gbl.sem, 16)
                for k, (_, H, W, form, a_from, a_to) in enumerate(convs):
                    C = CH // H
                    sp.wait_ge(wz.sem, wz.at(k + 1))
                    if form == "out_in":
                        sp.dma_start(woi[:, :, :], W.rearrange("(k p) f -> p k f", p=P)).then_inc(wld.sem, 16)
                    elif form == "in_out":
                        sp.dma_start(wall[:, :, k * CH:(k + 1) * CH], W.rearrange("(k p) f -> p k f", p=P)).then_inc(wld.sem, 16)
                    else:
                        for h in range(H):
                            sp.dma_start(wall[:, :, h * C:(h + 1) * C], W[h].rearrange("(k p) o -> p k o", p=P)).then_inc(wld.sem, 16)
                    for h in range(H):
                        r0, kk = (h * C) % P, (h * C) // P
                        for side, a in enumerate((a_from, a_to)):
                            col = side * HS + heads0[k] + h
                            sp.dma_start(attb[r0:r0 + C, kk, col:col + 1], a[h].rearrange("(c a) -> c a", a=1)).then_inc(wld.sem, 16)
                sp.wait_ge(wld.sem, wld.at(16 * sum(n_dma)))
                if n == 3:
                    sp.wait_ge(gbl.sem, gbl.at(64))

            @block.tensor
            def _(pe):
                for k, (_, H, W, form, _, _) in enumerate(convs):
                    pe.wait_ge(wld.sem, wld.at(16 * sum(n_dma[:k + 1])))
                    for a in range(2):
                        for b in range(2):
                            src = woi[:, a, b * P:(b + 1) * P] if form == "out_in" else wall[:, a, k * CH + b * P:k * CH + (b + 1) * P]
                            ins = pe.transpose(pw[:, b, a * P:(a + 1) * P], src, ident[:, :])
                    ins.then_inc(tr.sem, 1)
                    pe.wait_ge(trc.sem, trc.at(2 * k + 1))
                    hs = slice(heads0[k], heads0[k] + H)
                    for m in range(2):
                        for side in range(2):
                            col = side * HS + heads0[k]
                            for kk in range(2):
                                ins = pe.matmul(pf[:, m, col:col + H], woi[:, kk, m * P:(m + 1) * P],
                                                attb[:, kk, col:col + H], start=kk == 0, stop=kk == 1)
                    ins.then_inc(tr.sem, 1)

            @block.scalar
            def _(act):
                act.activation(attb[:, :, :], ident[:, 0:4 * HS].rearrange("p (k h) -> p k h", k=2), ACT.Copy, scale=0.0).then_inc(wz.sem, 1)
                CHUNKS = T // CHUNK
                for r in range(n_sqrt):
                    src = hres if r else xres
                    base = steps.at(2 if r == 0 else NORM + 1)
                    if r:
                        act.wait_ge(steps.sem, base)
                    with act.Fori(0, CHUNKS) as i:
                        if r == 0:
                            act.wait_ge(steps.sem, base + i * 2)
                        act.wait_ge(squared.sem, squared.at(2 * CHUNKS * r) + i)
                        for j in range(CHUNK):
                            t = i * CHUNK + j
                            ins = act.activation(sq[:, j, :], src[:, bass.ds(t, 1), :].rearrange("p a f -> p (a f)"), ACT.Square,
                                                 bias=nmean[:, bass.ds(t, 1)], accum_out=ss[:, bass.ds(t, 1)])
                        ins.then_inc(squared.sem, 1)
                    act.wait_ge(steps.sem, steps.at(2 * CHUNKS + 1 if r == 0 else NORM + 2))
                    act.activation(std[:, :], var[:, :], ACT.Sqrt).then_inc(roots.sem, 1)
                    if n == 3 and r == 0:
                        act.wait_ge(steps.sem, steps.at(NORM))
                        with act.Fori(0, CHUNKS) as i:
                            for j in range(CHUNK):
                                t = i * CHUNK + j
                                ins = act.activation(hres[:, bass.ds(t, 1), :].rearrange("p a f -> p (a f)"),
                                                     xres[:, bass.ds(t, 1), :].rearrange("p a f -> p (a f)"), ACT.Relu,
                                                     bias=shift[:, bass.ds(t, 1)], scale=rstd[:, bass.ds(t, 1)], accum_out=total[:, bass.ds(t, 1)])
                            ins.then_inc(squared.sem, 1)
                for k, (_, H, W, form, _, _) in enumerate(convs):
                    act.wait_ge(tr.sem, tr.at(2 * k + 1))
                    dst = wall[:, :, k * CH:(k + 1) * CH] if form == "out_in" else woi[:, :, :]
                    act.activation(dst, pw[:, :, :], ACT.Copy).then_inc(trc.sem, 1)
                    act.wait_ge(tr.sem, tr.at(2 * k + 2))
                    for side in range(2):
                        col = side * HS + heads0[k]
                        ins = act.activation(wall[:, :, FEAT + col:FEAT + col + H], pf[:, :, col:col + H], ACT.Copy)
                    ins.then_inc(trc.sem, 1)
                    if k + 1 < NC:
                        act.wait_ge(trc.sem, trc.at(2 * k + 2))
                        act.sem_inc(wz.sem, 1)

            @block.vector
            def _(dve):
                m = [0]
                CHUNKS = T // CHUNK

                def link(ins):
                    m[0] += 1
                    ins.then_inc(steps.sem, 1)
                    dve.wait_ge(steps.sem, steps.at(m[0]))

                def deviation(r, seen):
                    dve.wait_ge(squared.sem, squared.at(seen))
                    link(dve.tensor_scalar(var[:, :], ss[:, :], 1.0 / CH, EPS, ALU.mult, ALU.add))
                    dve.wait_ge(roots.sem, roots.at(r + 1))
                    link(dve.reciprocal(rstd[:, :], std[:, :]))
                    link(dve.tensor_tensor(shift[:, :], nmean[:, :], rstd[:, :], ALU.mult))

                if n == 0:
                    dve.wait_ge(loaded.sem, loaded.at(32))
                for i in range(CHUNKS):
                    ts = slice(i * CHUNK, (i + 1) * CHUNK)
                    link(dve.tensor_reduce(total[:, ts], xres[:, ts, :], X, ALU.add))
                    link(dve.tensor_scalar(nmean[:, ts], total[:, ts], -1.0 / CH, None, ALU.mult))
                deviation(0, CHUNKS)
                if n == 3:
                    dve.wait_ge(squared.sem, squared.at(2 * CHUNKS))
                    link(dve.tensor_scalar(nmean[:, :], total[:, :], -1.0 / CH, None, ALU.mult))
                    deviation(1, 3 * CHUNKS)
                steps.base += m[0]
            squared.base += (3 if n == 3 else 1) * (T // CHUNK)
            wld.base += 16 * sum(n_dma)
            tr.base += 2 * NC
            trc.base += 2 * NC
            wz.base += NC
            roots.base += n_sqrt
            if n == 3:
                gbl.base += 64

        hs_, ht, hc, hm, he = sig("tile_staged"), sig("tile_turned"), sig("tile_copied"), sig("tile_product"), sig("tile_evacuated")
        st = [sig(f"tile_stored{j}") for j in range(2)]
        with ExitStack() as c2, nc.Block() as block:
            hst = sb("t_st", [P, 2, CH], F32, c2)
            hT = sb("t_T", [P, 2, 2, P], F32, c2)
            row = sb("t_row", [P, 2, FEAT], F32, c2)
            pT = [ps(f"t_pT{j}", [P, 2, 256], F32, c2) for j in range(2)]
            pm = [ps(f"t_pm{j}", [P, 512], F32, c2) for j in range(2)]
            pn = [ps(f"t_pn{j}", [P, 512], F32, c2) for j in range(2)]
            MAIN = min(WALL, 512)

            @block.scalar
            def _(act):
                def stage(t, par):
                    act.wait_ge(ht.sem, ht.at(1) + t)
                    src = (hres if n == 3 else xres)[:, bass.ds(t, 1), :].rearrange("p a f -> p (a f)")
                    how = dict(bias=shift[:, bass.ds(t, 1)], scale=rstd[:, bass.ds(t, 1)])
                    act.activation(hst[:, par, :], src, ACT.Identity if n == 3 else ACT.Relu, **how).then_inc(hs_.sem, 1)
                    if n == 0:
                        act.activation(hres[:, bass.ds(t, 1), :].rearrange("p a f -> p (a f)"), src, ACT.Relu, **how)

                def turned(t, par):
                    act.wait_ge(ht.sem, ht.at(3) + t)
                    act.wait_ge(hm.sem, hm.at(1) + t)
                    if n == 3:
                        for k in range(2):
                            ins = act.activation(hT[:, par, k, :], pT[par][:, k, 0:P], ACT.Identity, bias=gb[:, 1, k:k + 1], scale=gb[:, 0, k:k + 1])
                    else:
                        ins = act.activation(hT[:, par, :, :], pT[par][:, :, 0:P], ACT.Copy)
                    ins.then_inc(hc.sem, 1)
                staggered(act, T, [(1, stage), (0, turned)])

            @block.tensor
            def _(pe):
                for j in range(2):
                    pe.matmul(pT[j][:, 0, 0:P], ident[:, :], ident[:, :], start=True, stop=True).then_inc(ht.sem, 1)
                for j in range(2):
                    pe.matmul(pm[j][:, 0:P], ident[:, :], ident[:, :], start=True, stop=True).then_inc(hm.sem, 1)

                def turn(t, par):
                    pe.wait_ge(hs_.sem, hs_.at(1) + t)
                    for k in range(2):
                        ins = pe.transpose(pT[par][:, k, 0:P], hst[:, par, k * P:(k + 1) * P], ident[:, :])
                    ins.then_inc(ht.sem, 1)

                def product(t, par):
                    pe.wait_ge(hc.sem, hc.at(1) + t)
                    pe.wait_ge(he.sem, he.at(1) + t)
                    for k in range(2):
                        ins = pe.matmul(pm[par][:, 0:MAIN], hT[:, par, k, :], wall[:, k, 0:MAIN], start=k == 0, stop=k == 1)
                    if WALL > MAIN:
                        for k in range(2):
                            ins = pe.matmul(pn[par][:, 0:WALL - MAIN], hT[:, par, k, :], wall[:, k, MAIN:WALL], start=k == 0, stop=k == 1)
                    ins.then_inc(hm.sem, 1)
                staggered(pe, T, [(1, turn), (0, product)])

            @block.vector
            def _(dve):
                for j in range(2):
                    dve.memset(row[:, j, :], 0.0).then_inc(he.sem, 1)

                def evacuate(t, par):
                    dve.wait_ge(hm.sem, hm.at(3) + t)
                    if later(t, 2):
                        dve.wait_ge(st[par].sem, st[par].at(-8 * par) + t * 8)
                    dve.tensor_copy(row[:, par, :], pm[par][:, 0:FEAT])
                    scores = pn[par][:, 0:WALL - MAIN] if WALL > MAIN else pm[par][:, FEAT:WALL]
                    dve.tensor_copy(nodes[:, bass.ds(t, 1), :].rearrange("p a f -> p (a f)"), scores).then_inc(he.sem, 1)
                staggered(dve, T, [(0, evacuate)])

            @block.sync
            def _(sp):
                def store(t, par):
                    sp.wait_ge(he.sem, he.at(3) + t)
                    sp.dma_start(feats[bass.ds(t * P, P), :], row[:, par, :]).then_inc(st[par].sem, 16)
                staggered(sp, T, [(0, store)])
                for j in range(2):
                    sp.wait_ge(st[j].sem, st[j].at(16 * (T // 2 + (1 - j) * (T % 2))))
            hs_.base += T
            ht.base += T + 2
            hc.base += T
            hm.base += T + 2
            he.base += T + 2
            for j in range(2):
                st[j].base += 16 * (T // 2 + (1 - j) * (T % 2))

    with ExitStack() as c:
        prob = sb("prob", [P, SLOTS, HS], F32, c)
        EARLY = SLOTS // 8 if NC == 1 else 0
        early = sb("early_rows", [P, EARLY, FEAT], F32, c) if EARLY else None
        edge_scores(nc, sig, sb, ps, K, n, g, nodes, prob, HS, feats, early, EARLY)
        if n == 1:
            softmax_global(nc, sig, sb, ps, g, prob, HS, K)
        else:
            for k, (_, H, *_r) in enumerate(convs):
                softmax_runs(nc, sig, sb, ps, g, prob, heads0[k], H, K)

        acc = sb("acc", [P, T, NC * AW], F32, c)
        gin = [sig(f"rows_in{j}") for j in range(16)]
        cp, gate, msg_ok, act_ok, mm, ac = (sig("row_index"), sig("row_gate"), sig("messages_ready"), sig("messages_ready_too"),
                                            sig("slot_product"), sig("slot_added"))
        with ExitStack() as c2, nc.Block() as block:
            idx = sb("m_idx", [P, 4, 4], I32, c2)
            rows = sb("m_rows", [P, 16, FEAT], F32, c2)
            msg = sb("m_msg", [P, 4, NC * AW], F32, c2)
            oh = sb("m_oh", [P, 8, P], F32, c2)
            opened = sb("m_opened", [P, 1], F32, c2)
            pp = [ps("m_p", [P, NC, 512], F32, c2) for j in range(4)]
            NI = SLOTS // 16
            NB = SLOTS // 4
            BY_ACT = [0] if NC == 2 else []
            ACT_SLOTS = {4: (1, 3), 8: (3,)}[HS] if NC == 1 else ()
            early_in = sig("early_rows_in")

            @block.gpsimd
            def _(pool):
                limit = pool.to_reg(NT - 1)
                with pool.Fori(0, NI) as i:
                    for par in range(4):
                        nb = i * 4 + par
                        pool.wait_ge(cp.sem, cp.at(1) + nb)
                        for j in range(4):
                            b = par * 4 + j
                            if EARLY and b % 8 == 0:
                                continue
                            pool.wait_ge(msg_ok.sem, msg_ok.at(1) + (nb * 4 + j))
                            pool.wait_ge(act_ok.sem, act_ok.at(1) + (nb * 4 + j))
                            pool.sem_inc(gate.sem, 1)
                            pool.indirect_dma_start(out=rows[:, b, :], out_offset=None, in_=feats,
                                                    in_offset=bass.IndirectOffsetOnAxis(ap=idx[:, par, j:j + 1], axis=0),
                                                    bounds_check=limit, oob_is_err=True).then_inc(gin[b].sem, 16)

            @block.scalar
            def _(act):
                act.wait_ge(ac.sem, ac.at(5))

                def indices(nb, par):
                    act.activation(idx[:, par, :], g.other[:, bass.ds(nb * 4, 4)], ACT.Copy).then_inc(cp.sem, 1)

                for nb in range(4):
                    indices(nb, nb)
                with act.Fori(0, NI) as i:
                    for b in range(16):
                        s = i * 16 + b
                        is_early = EARLY and b % 8 == 0
                        if not is_early:
                            act.wait_ge(gin[b].sem, gin[b].at(16) + i * 16)
                        if b % 4 == 3:
                            indices(i * 4 + b // 4 + 4, b // 4)
                        act.wait_ge(mm.sem, mm.at(1) + s)
                        for k, cv in enumerate(convs):
                            H = cv[1]
                            if k not in BY_ACT:
                                a = acc0[k] + CH
                                ins = act.activation(msg[:, b % 4, a:a + H],
                                                     prob[:, bass.ds(s, 1), heads0[k]:heads0[k] + H].rearrange("p a h -> p (a h)"), ACT.Copy)
                            if k in BY_ACT or b % 4 in ACT_SLOTS:
                                row = early[:, bass.ds(i * 2 + b // 8, 1), :].rearrange("p a f -> p (a f)") if is_early else rows[:, b, :]
                                for h in range(H):
                                    C = CH // H
                                    ins = act.activation(msg[:, b % 4, acc0[k] + h * C:acc0[k] + (h + 1) * C],
                                                         row[:, k * CH + h * C:k * CH + (h + 1) * C], ACT.Copy,
                                                         scale=prob[:, bass.ds(s, 1), heads0[k] + h:heads0[k] + h + 1].rearrange("p a h -> p (a h)"))
                        ins.then_inc(act_ok.sem, 1)

            @block.tensor
            def _(pe):
                for j in range(4):
                    for k in BY_ACT:
                        a = CH + convs[k][1]
                        pe.matmul(pp[j][:, k, a:AW], ident[:, :], ident[:, 0:AW - a], start=True, stop=True)
                    pe.matmul(pp[j][:, 0, 0:P], ident[:, :], ident[:, :], start=True, stop=True).then_inc(mm.sem, 1)
                with pe.Fori(0, NI) as i:
                    for b in range(16):
                        s = i * 16 + b
                        j = b % 4
                        pe.wait_ge(msg_ok.sem, msg_ok.at(17) + s)
                        pe.wait_ge(act_ok.sem, act_ok.at(17) + s)
                        pe.wait_ge(ac.sem, ac.at(2) + s)
                        for k, cv in enumerate(convs):
                            if k in BY_ACT:
                                pe.matmul(pp[j][:, k, 0:CH], oh[:, b % 8, :], msg[:, j, acc0[k]:acc0[k] + CH], start=True, stop=True)
                                ins = pe.matmul(pp[j][:, k, CH:CH + cv[1]], oh[:, b % 8, :],
                                                prob[:, bass.ds(s, 1), heads0[k]:heads0[k] + cv[1]].rearrange("p a h -> p (a h)"), start=True, stop=True)
                            else:
                                ins = pe.matmul(pp[j][:, k, 0:AW], oh[:, b % 8, :], msg[:, j, acc0[k]:acc0[k] + AW], start=True, stop=True)
                        ins.then_inc(mm.sem, 1)

            @block.vector
            def _(dve):
                dve.memset(acc[:, :, :], 0.0).then_inc(ac.sem, 4)
                dve.memset(msg[:, :, :], 0.0).then_inc(ac.sem, 1)
                dve.memset(oh[:, :, :], 0.0).then_inc(msg_ok.sem, 16)
                dve.wait_ge(ac.sem, ac.at(5))
                dve.memset(opened[:, :], 0.0).then_inc(act_ok.sem, 16)
                dve.wait_ge(msg_ok.sem, msg_ok.at(16))

                def tile_ids(word):
                    return four_tiles(dve, g, word, T)

                def message(i, b):
                    s = i * 16 + b
                    j = b % 4
                    if j == 0:
                        dve.wait_ge(mm.sem, mm.at(0) + s)
                        dve.tensor_tensor(oh[:, b % 8:b % 8 + 4, :], iota_row[:, :].unsqueeze(1).to_broadcast([P, 4, P]),
                                          g.klo[:, bass.ds(s, 4)].unsqueeze(2).to_broadcast([P, 4, P]), ALU.is_equal)
                    if j in ACT_SLOTS:
                        return
                    dve.wait_ge(mm.sem, mm.at(1) + s)
                    for k, cv in enumerate(convs):
                        H = cv[1]
                        C = CH // H
                        if k in BY_ACT:
                            continue
                        if EARLY and b % 8 == 0:
                            row = early[:, bass.ds(i * 2 + b // 8, 1), :].rearrange("p a f -> p (a f)")
                        else:
                            dve.wait_ge(gin[b].sem, gin[b].at(16) + i * 16)
                            row = rows[:, b, k * CH:(k + 1) * CH]
                        ins = dve.tensor_tensor(msg[:, j, acc0[k]:acc0[k] + CH].rearrange("p (h c) -> p h c", h=H),
                                                row.rearrange("p (h c) -> p h c", h=H),
                                                prob[:, bass.ds(s, 1), heads0[k]:heads0[k] + H].rearrange("p a h -> p (a h)").unsqueeze(2).to_broadcast([P, H, C]),
                                                ALU.mult)
                    ins.then_inc(msg_ok.sem, 2 if j + 1 in ACT_SLOTS else 1)

                def add(s, j, tile):
                    dve.wait_ge(mm.sem, mm.at(5) + s)
                    dve.wait_ge(ac.sem, ac.at(5) + s)
                    a = acc[:, bass.ds(tile, 1), :].rearrange("p a (k f) -> p (a k) f", k=NC)
                    dve.tensor_tensor(a, a, pp[j][:, :, 0:AW], ALU.add).then_inc(ac.sem, 1)

                if EARLY:
                    dve.wait_ge(early_in.sem, early_in.at(0))
                def four(i, batch):
                    nb = i * 4 + batch
                    ids = tile_ids(nb - 1)
                    for b in range(4):
                        message(i, 4 * batch + b)
                        add(nb * 4 - 4 + b, b, ids[b])

                for b in range(4):
                    message(0, b)
                for batch in range(1, 4):
                    four(0, batch)
                with dve.Fori(1, NI) as i:
                    for batch in range(4):
                        four(i, batch)
                ids = tile_ids(NB - 1)
                for b in range(4):
                    add(SLOTS - 4 + b, b, ids[b])
            cp.base += NB + 4
            gate.base += SLOTS - EARLY
            msg_ok.base += SLOTS + 16
            act_ok.base += SLOTS + 16
            mm.base += SLOTS + 4
            ac.base += SLOTS + 5
            for j in range(16):
                gin[j].base += 0 if EARLY and j % 8 == 0 else 16 * NI

        if n == 3:
            finish_last(nc, sig, sb, ps, A, K, convs, acc, acc0, out)
        else:
            finish_layer(nc, sig, sb, ps, A, K, n, convs, acc, acc0)


def edge_scores(nc, sig, sb, ps, K, n, g, nodes, prob, H, feats, early, EARLY):
    SLOTS, T = g.slots, K["T"]
    iota_row, iota_col = K["iota_row"], K["iota_col"]
    B = 8
    NB = SLOTS // B
    G = {4: 2, 8: 2, 12: 3}[H]
    PER = {4: 3, 8: 2, 12: 1}[H]
    BANKS = (B - G) // PER
    RING = BANKS if 2 * BANKS > 6 else 2 * BANKS
    assert PER * BANKS == B - G and PER * (T + 1) * H <= 512 and SLOTS % B == 0
    W = (T + 1) * H
    ldl = [sig(f"lines_in{j}") for j in range(2)]
    owned = sig("score_own_tiles")
    table_out, index_ok, own_ok, gused, gate = (sig("score_table_stored"), sig("score_index"), sig("score_own_picked"),
                                                sig("score_gathered_used"), sig("score_gate"))
    gin = [sig(f"scores_in{j}") for j in range(2)]
    early_in = sig("early_rows_in")
    table = nc.dram_tensor(f"scores{n}", [T * P, H], F32, kind="Internal").ap()
    hot, picked, used, lk = sig("score_onehots"), sig("scores_picked"), sig("scores_used"), sig("score_steps")
    with ExitStack() as c, nc.Block() as block:
        line = sb("e_line", [P, 2, (B + B - G) * P], BF16, c)
        lineh = sb("e_lineh", [T, 2, (B - G) * P], BF16, c)
        oh = sb("e_oh", [P, 2, (B + B - G) * P], BF16, c)
        ohh = sb("e_ohh", [T, 2, (B - G) * P], BF16, c)
        index = sb("e_index", [P, 2, G], I32, c)
        gathered = sb("e_gathered", [P, 2, G, H], F32, c)
        po = [ps("e_po", [P, 512], F32, c) for _ in range(2)]
        parts = [sb("e_parts", [P, 3, T, H], BF16, c) for _ in range(2)]
        rest = sb("e_rest", [P, T, H], F32, c)
        low1 = sb("e_low1", [T, T], F32, c)
        low = sb("e_low", [T, T, H], BF16, c)
        own_tile = sb("e_own_tile", [P, 2, B, 3, H], BF16, c)
        best = sb("e_best", [P, 2, BANKS, PER, H], F32, c)
        pb = [ps("e_pb", [P, 512], F32, c) for _ in range(RING)]

        def batches(eng, body, last=True):
            count = NB if last else NB - 1
            with eng.Fori(0, count // 2) as i:
                for par in range(2):
                    body(i * 2 + par, i, par)
            if count % 2:
                body(count - 1, count // 2, 0)

        @block.sync
        def _(sp):
            def body(nb, i, par):
                sp.wait_ge(hot.sem, hot.at(1) + nb)
                some = (B - G) * P
                for dst, src, first, rows in ((line[:, par, 0:B * P], g.lines[2], 0, P),
                                              (line[:, par, B * P:B * P + some], g.lines[0], G * P, P),
                                              (lineh[:, par, :], g.lines[1], G * P, T)):
                    size = B * P - first
                    sp.dma_start(dst, src[bass.ds(nb * (B * P) + first, size)].rearrange("(a f) -> a f", a=1).to_broadcast([rows, size])).then_inc(ldl[par].sem, 16)
            sp.dma_start(table.rearrange("(t p) h -> p t h", p=P), nodes[:, :, 0:H]).then_inc(table_out.sem, 16)
            batches(sp, body)
            sp.wait_ge(table_out.sem, table_out.at(16))

        @block.gpsimd
        def _(pool):
            limit = pool.to_reg(T * P - 1)
            pool.wait_ge(table_out.sem, table_out.at(16))

            def body(nb, i, par):
                pool.wait_ge(index_ok.sem, index_ok.at(1) + nb)
                pool.sem_inc(gate.sem, 1)
                if EARLY:
                    pool.indirect_dma_start(out=early[:, nb, :], out_offset=None, in_=feats,
                                            in_offset=bass.IndirectOffsetOnAxis(ap=g.other[:, nb * B:nb * B + 1], axis=0),
                                            bounds_check=limit, oob_is_err=True).then_inc(early_in.sem, 16)
                for j in range(G):
                    pool.indirect_dma_start(out=gathered[:, par, j, :], out_offset=None, in_=table,
                                            in_offset=bass.IndirectOffsetOnAxis(ap=index[:, par, j:j + 1], axis=0),
                                            bounds_check=limit, oob_is_err=True).then_inc(gin[par].sem, 16)
            if EARLY:
                for nb in range(NB):
                    body(nb, nb // 2, nb % 2)
            else:
                batches(pool, body)

        @block.tensor
        def _(pe):
            def body(nb, i, par):
                pe.wait_ge(hot.sem, hot.at(3) + nb)
                pe.wait_ge(owned.sem, owned.at(1) + nb)
                pe.wait_ge(gused.sem, gused.at(1) + nb)
                for j in range(G):
                    for k in range(3):
                        ins = pe.matmul(po[par][:, j * H:(j + 1) * H], oh[:, par, j * P:(j + 1) * P], own_tile[:, par, j, k, :],
                                        start=k == 0, stop=k == 2)
                ins.then_inc(own_ok.sem, 1)
                for j in range(G, B):
                    r = (j - G) // PER
                    bank = (par * BANKS + r) % RING
                    if (j - G) % PER == 0:
                        pe.wait_ge(used.sem, used.at(1) + nb * BANKS + r)
                    a = ((j - G) % PER) * W
                    own = slice(j * P, (j + 1) * P)
                    other = slice((B + j - G) * P, (B + j - G + 1) * P)
                    for k in range(3):
                        pe.matmul(pb[bank][:, a:a + T * H], oh[:, par, other], parts[0][:, k, :, :].rearrange("p t h -> p (t h)"),
                                  start=k == 0, stop=False)
                    pe.matmul(pb[bank][:, a:a + T * H], ohh[:, par, (j - G) * P:(j - G + 1) * P], low[:, :, :].rearrange("p t h -> p (t h)"),
                              start=False, stop=True)
                    for k in range(3):
                        ins = pe.matmul(pb[bank][:, a + T * H:a + W], oh[:, par, own],
                                        own_tile[:, par, j, k, :], start=k == 0, stop=k == 2)
                    if (j - G) % PER == PER - 1:
                        ins.then_inc(picked.sem, 1)
            batches(pe, body)

        @block.scalar
        def _(act):
            act.wait_ge(lk.sem, lk.at(10))

            def body(nb, i, par):
                act.wait_ge(picked.sem, picked.at(BANKS) + nb * BANKS)
                for j in range(B):
                    if j % 4 == 0:
                        ids = four_tiles(act, g, nb * 2 + j // 4, T)
                    ins = act.activation(own_tile[:, par, j, :, :],
                                         parts[1][:, :, bass.ds(ids[j % 4], 1), :].rearrange("p k a h -> p k (a h)"), ACT.Copy)
                ins.then_inc(owned.sem, 1)
                act.wait_ge(gused.sem, gused.at(1) + nb)
                act.activation(index[:, par, :], g.other[:, bass.ds(nb * B, G)], ACT.Copy).then_inc(index_ok.sem, 1)
            batches(act, body)

        @block.vector
        def _(dve):
            m = [0]

            def link(ins):
                m[0] += 1
                ins.then_inc(lk.sem, 1)
                dve.wait_ge(lk.sem, lk.at(m[0]))

            for side in range(2):
                src = nodes[:, :, side * H:(side + 1) * H]
                link(dve.tensor_copy(parts[side][:, 0, :, :], src))
                link(dve.tensor_tensor(rest[:, :, :], src, parts[side][:, 0, :, :], ALU.subtract))
                link(dve.tensor_copy(parts[side][:, 1, :, :], rest[:, :, :]))
                link(dve.tensor_tensor(rest[:, :, :], rest[:, :, :], parts[side][:, 1, :, :], ALU.subtract))
                link(dve.tensor_copy(parts[side][:, 2, :, :], rest[:, :, :]))
            link(dve.tensor_scalar(low1[:, :], iota_row[0:T, 0:T], iota_col[0:T, 0:1], LOWEST, ALU.not_equal, ALU.mult))
            link(dve.tensor_copy(low[:, :, :], low1[:, :].unsqueeze(2).to_broadcast([T, T, H])))
            link(dve.memset(best[:, :, :, :, :], 0.0))
            dve.memset(rest[:, 0, :], 0.0).then_inc(hot.sem, 2)
            dve.memset(rest[:, 1, :], 0.0).then_inc(used.sem, RING)
            dve.memset(rest[:, 2, :], 0.0).then_inc(picked.sem, 2 * BANKS)
            dve.memset(rest[:, 3, :], 0.0).then_inc(gused.sem, 2)

            def onehots(nb, i, par):
                dve.wait_ge(ldl[par].sem, ldl[par].at(48) + i * 48)
                dve.wait_ge(picked.sem, picked.at(BANKS) + nb * BANKS)
                dve.tensor_scalar(oh[:, par, :], line[:, par, :], iota_col[:, 0:1], None, ALU.is_equal)
                dve.tensor_scalar(ohh[:, par, :], lineh[:, par, :], iota_col[0:T, 0:1], None, ALU.is_equal).then_inc(hot.sem, 1)

            def bank_of(par, r):
                return pb[(par * BANKS + r) % RING][:, 0:PER * W].rearrange("p (s w) -> p s w", s=PER)

            def largest(nb, par, r):
                at = nb * BANKS + r
                dve.wait_ge(picked.sem, picked.at(2 * BANKS + 1) + at)
                dve.wait_ge(used.sem, used.at(RING - BANKS) + at)
                dve.tensor_reduce(best[:, par, r, :, :],
                                  bank_of(par, r)[:, :, 0:T * H].rearrange("p s (t h) -> p s h t", h=H), X, ALU.max).then_inc(lk.sem, 1)

            def own(nb, par, r):
                dve.wait_ge(lk.sem, lk.at(m[0] + 1) + nb * BANKS + r)
                dve.tensor_tensor(prob[:, bass.ds(nb * B + G + r * PER, PER), :], best[:, par, r, :, :],
                                  bank_of(par, r)[:, :, T * H:W], ALU.add).then_inc(used.sem, 1)

            AHEAD = BANKS > 2

            def scores(nb, par, last=False):
                if not AHEAD:
                    largest(nb, par, 0)
                for r in range(BANKS):
                    if r < BANKS - 1:
                        largest(nb, par, r + 1)
                    elif AHEAD and not last:
                        largest(nb + 1, 1 - par, 0)
                    own(nb, par, r)

            def add_gathered(nb, i, par):
                dve.wait_ge(own_ok.sem, own_ok.at(1) + nb)
                dve.wait_ge(gin[par].sem, gin[par].at(16 * G) + i * (16 * G))
                dve.tensor_tensor(prob[:, bass.ds(nb * B, G), :], gathered[:, par, :, :],
                                  po[par][:, 0:G * H].rearrange("p (s h) -> p s h", s=G), ALU.add).then_inc(gused.sem, 1)

            def body(nb, i, par):
                onehots(nb + 1, i + par, 1 - par)
                scores(nb, par)
                add_gathered(nb, i, par)

            onehots(0, 0, 0)
            if AHEAD:
                largest(0, 0, 0)
            batches(dve, body, last=False)
            scores(NB - 1, (NB - 1) % 2, last=True)
            add_gathered(NB - 1, (NB - 1) // 2, (NB - 1) % 2)
            total = m[0] + NB * BANKS
            m[0] = total
            dve.wait_ge(used.sem, used.at(RING + NB * BANKS))
            dve.wait_ge(gused.sem, gused.at(2 + NB))
            link(dve.scalar_tensor_tensor(prob[:, :, :], prob[:, :, :], 0.2, prob[:, :, :], ALU.mult, ALU.max))
            if n == 2:
                link(dve.tensor_tensor(prob[:, :, :], prob[:, :, :], g.w[:, :].unsqueeze(2).to_broadcast([P, SLOTS, H]), ALU.mult))
            lk.base += m[0]
        hot.base += NB + 2
        owned.base += NB
        picked.base += NB * BANKS + 2 * BANKS
        used.base += NB * BANKS + RING
        for j in range(2):
            ldl[j].base += 48 * (NB // 2 + (1 - j) * (NB % 2))
            gin[j].base += 16 * G * (NB // 2 + (1 - j) * (NB % 2))
        table_out.base += 16
        index_ok.base += NB
        own_ok.base += NB
        gused.base += NB + 2
        gate.base += NB
        early_in.base += 16 * EARLY


def softmax_global(nc, sig, sb, ps, g, prob, H, K):
    SLOTS = g.slots
    ident, ones = K["ident"], K["ones"]
    lk, tr = sig("softmax_steps"), sig("softmax_turned")
    with ExitStack() as c, nc.Block() as block:
        low = sb("x_low", [P, SLOTS], F32, c)
        top = sb("x_top", [P, H], F32, c)
        top1 = sb("x_top1", [H, 1], F32, c)
        diag = sb("x_diag", [H, H], F32, c)
        pt = ps("x_pt", [H, 512], F32, c)
        pb = ps("x_pb", [P, 512], F32, c)

        @block.vector
        def _(dve):
            m = [0]

            def link(ins):
                m[0] += 1
                ins.then_inc(lk.sem, 1)
                dve.wait_ge(lk.sem, lk.at(m[0]))
            link(dve.tensor_scalar(low[:, :], g.klo[:, :], 0.0, LOWEST, ALU.is_lt, ALU.mult))
            link(dve.tensor_tensor(prob[:, :, :], prob[:, :, :], low[:, :].unsqueeze(2).to_broadcast([P, SLOTS, H]), ALU.add))
            link(dve.tensor_reduce(top[:, :], prob[:, :, :].rearrange("p s h -> p h s"), X, ALU.max))
            dve.wait_ge(tr.sem, tr.at(1))
            link(dve.tensor_reduce(top1[:, :], pt[:, 0:P], X, ALU.max))
            link(dve.tensor_scalar(diag[:, :], ident[0:H, 0:H], top1[:, 0:1], None, ALU.mult))
            dve.wait_ge(tr.sem, tr.at(2))
            link(dve.tensor_copy(top[:, :], pb[:, 0:H]))
            link(dve.tensor_tensor(prob[:, :, :], prob[:, :, :], top[:, :].unsqueeze(1).to_broadcast([P, SLOTS, H]), ALU.subtract))

        @block.tensor
        def _(pe):
            pe.wait_ge(lk.sem, lk.at(3))
            pe.transpose(pt[:, 0:P], top[:, :], ident[:, :]).then_inc(tr.sem, 1)
            pe.wait_ge(lk.sem, lk.at(5))
            pe.matmul(pb[:, 0:H], ones[0:H, :], diag[:, :], start=True, stop=True).then_inc(tr.sem, 1)

        @block.scalar
        def _(act):
            act.wait_ge(lk.sem, lk.at(7))
            act.activation(prob[:, :, :], prob[:, :, :], ACT.Exp)
        lk.base += 7
        tr.base += 2


def softmax_runs(nc, sig, sb, ps, g, prob, h0, H, K):
    SLOTS, R = g.slots, g.rows
    W = 4 * P
    ident = K["ident"]
    lk, tr, ev, ex, back, bk = (sig("softmax_steps"), sig("softmax_turned"), sig("softmax_copied"),
                                sig("softmax_exps"), sig("softmax_back"), sig("softmax_done"))
    with ExitStack() as c, nc.Block() as block:
        sc = sb("y_sc", [R, H, W], F32, c)
        top = sb("y_top", [R, H, W], F32, c)
        tmp = sb("y_tmp", [R, W], F32, c)
        ends = sb("y_ends", [R, 2, H], F32, c)
        endT = sb("y_endT", [H, 2, R], F32, c)
        run = sb("y_run", [H, 2, R], F32, c)
        carry = sb("y_carry", [H, 2, R], F32, c)
        carryT = sb("y_carryT", [R, 2, H], F32, c)
        pt = [ps(f"y_pt{j}", [P, W], F32, c) for j in range(2)]
        pe1 = ps("y_pe", [H, 2, 256], F32, c)
        pe2 = ps("y_pf", [R, 2, 256], F32, c)
        pb = [ps(f"y_pb{j}", [P, W], F32, c) for j in range(2)]

        @block.tensor
        def _(pe):
            for h in range(H):
                if h >= 2:
                    pe.wait_ge(ev.sem, ev.at(h - 1))
                for b in range(4):
                    ins = pe.transpose(pt[h % 2][0:R, b * P:(b + 1) * P], prob[:, b:SLOTS:4, h0 + h], ident[:, :])
                ins.then_inc(tr.sem, 1)
            pe.wait_ge(lk.sem, lk.at(3 * H + 2))
            for k in range(2):
                ins = pe.transpose(pe1[:, k, 0:R], ends[:, k, :], ident[0:R, 0:R])
            ins.then_inc(tr.sem, 1)
            pe.wait_ge(lk.sem, lk.at(3 * H + 9))
            for k in range(2):
                ins = pe.transpose(pe2[:, k, 0:H], carry[:, k, :], ident[0:H, 0:H])
            ins.then_inc(tr.sem, 1)
            for h in range(H):
                pe.wait_ge(ex.sem, ex.at(h + 1))
                if h >= 2:
                    pe.wait_ge(bk.sem, bk.at(h - 1))
                for b in range(4):
                    ins = pe.transpose(pb[h % 2][:, b * R:(b + 1) * R], sc[:, h, b * P:(b + 1) * P], ident[0:R, 0:R])
                ins.then_inc(back.sem, 1)

        @block.scalar
        def _(act):
            for h in range(H):
                act.wait_ge(tr.sem, tr.at(h + 1))
                act.activation(sc[:, h, :], pt[h % 2][0:R, :], ACT.Copy).then_inc(ev.sem, 1)

            def turn_back(h):
                act.wait_ge(back.sem, back.at(h + 1))
                act.activation(prob[:, :, h0 + h].rearrange("p (c b) -> p b c", b=4),
                               pb[h % 2][:, 0:4 * R].rearrange("p (b c) -> p b c", b=4), ACT.Copy).then_inc(bk.sem, 1)
            for h in range(H):
                act.wait_ge(lk.sem, lk.at(3 * H + 10 + 3 * (h + 1)))
                act.activation(sc[:, h, :], sc[:, h, :], ACT.Exp).then_inc(ex.sem, 1)
                if h >= 1:
                    turn_back(h - 1)
            turn_back(H - 1)

        @block.vector
        def _(dve):
            m = [0]

            def link(ins):
                m[0] += 1
                ins.then_inc(lk.sem, 1)
                dve.wait_ge(lk.sem, lk.at(m[0]))
            for h in range(H):
                dve.wait_ge(ev.sem, ev.at(h + 1))
                link(dve.tensor_tensor_scan(top[:, h, :], g.negnew[:, :], sc[:, h, :], LOWEST, ALU.add, ALU.max))
                link(dve.tensor_tensor_scan(tmp[:, ::-1], g.negnewb[:, ::-1], sc[:, h, ::-1], LOWEST, ALU.add, ALU.max))
                link(dve.tensor_tensor(top[:, h, :], top[:, h, :], tmp[:, :], ALU.max))
            link(dve.tensor_copy(ends[:, 0, :], top[:, :, W - 1]))
            link(dve.tensor_copy(ends[:, 1, :], top[:, :, 0]))
            dve.wait_ge(tr.sem, tr.at(H + 1))
            link(dve.tensor_copy(endT[:, :, :], pe1[:, :, 0:R]))
            link(dve.tensor_tensor_scan(run[:, 0, :], g.negthru[0:H, :], endT[:, 0, :], LOWEST, ALU.add, ALU.max))
            link(dve.tensor_tensor_scan(run[:, 1, ::-1], g.negthrub[0:H, ::-1], endT[:, 1, ::-1], LOWEST, ALU.add, ALU.max))
            link(dve.memset(carry[:, 0, 0:1], LOWEST))
            link(dve.memset(carry[:, 1, R - 1:R], LOWEST))
            link(dve.tensor_tensor(carry[:, 0, 1:R], run[:, 0, 0:R - 1], g.negcont[0:H, 1:R], ALU.add))
            link(dve.tensor_tensor(carry[:, 1, 0:R - 1], run[:, 1, 1:R], g.negcont[0:H, 1:R], ALU.add))
            dve.wait_ge(tr.sem, tr.at(H + 2))
            link(dve.tensor_copy(carryT[:, :, :], pe2[:, :, 0:H]))
            for h in range(H):
                link(dve.scalar_tensor_tensor(top[:, h, :], g.negfirst[:, :], carryT[:, 0, h:h + 1], top[:, h, :], ALU.add, ALU.max))
                link(dve.scalar_tensor_tensor(top[:, h, :], g.neglast[:, :], carryT[:, 1, h:h + 1], top[:, h, :], ALU.add, ALU.max))
                link(dve.tensor_tensor(sc[:, h, :], sc[:, h, :], top[:, h, :], ALU.subtract))
        lk.base += 3 * H + 10 + 3 * H
        tr.base += H + 2
        ev.base += H
        ex.base += H
        back.base += H
        bk.base += H


def finish_layer(nc, sig, sb, ps, A, K, n, convs, acc, acc0):
    T, xres, hres = K["T"], K["xres"], K["hres"]
    lk, ld, ex, rs = sig("finish_steps"), sig("finish_loaded"), sig("finish_exps"), sig("residual_added")
    bias_in = {0: lambda: A["L0_gnn_bias"], 1: None, 2: lambda: A["L2_gnn_bias"].rearrange("h c -> (h c)")}[n]
    H = convs[0][1]
    CHUNK = 5
    chunks = [slice(t, t + CHUNK) for t in range(0, T, CHUNK)]
    waits = 1 if bias_in else 0
    with ExitStack() as c, nc.Block() as block:
        bias = sb("f_bias", [P, CH], F32, c)
        tmp = sb("f_tmp", [P, T, CH], F32, c) if n == 0 else None
        rden = sb("f_rden", [P, T, 8], F32, c)

        @block.sync
        def _(sp):
            if bias_in:
                sp.dma_start(bias[:, :], bias_in().rearrange("(a f) -> a f", a=1).to_broadcast([P, CH])).then_inc(ld.sem, 16)
                sp.wait_ge(ld.sem, ld.at(16))

        count, marks = [0], []

        @block.gpsimd
        def _(pool):
            if n == 0:
                for ts in chunks:
                    pool.tensor_tensor(xres[:, ts, :], xres[:, ts, :], hres[:, ts, :], ALU.add).then_inc(rs.sem, 1)

        @block.vector
        def _(dve):
            def link(ins):
                count[0] += 1
                ins.then_inc(lk.sem, 1)
                dve.wait_ge(lk.sem, lk.at(count[0]))

            if waits:
                dve.wait_ge(ld.sem, ld.at(16))
            z = acc[:, :, acc0[0]:acc0[0] + CH]
            den = acc[:, :, acc0[0] + CH:acc0[0] + CH + H]
            if n == 1:
                link(dve.tensor_scalar(den, den, 1e-6, None, ALU.max))
            elif n == 2:
                link(dve.tensor_scalar(den, den, 1e-30, None, ALU.max))
            else:
                link(dve.tensor_scalar(den, den, 1e-16, None, ALU.add))
            link(dve.reciprocal(rden[:, :, 0:H], den))
            for ts in chunks:
                z4 = z[:, ts, :].rearrange("p t (h c) -> p t h c", h=H)
                link(dve.tensor_tensor(z4, z4, rden[:, ts, 0:H].unsqueeze(3).to_broadcast([P, CHUNK, H, CH // H]), ALU.mult))
                if bias_in:
                    link(dve.tensor_tensor(z[:, ts, :], z[:, ts, :], bias[:, :].unsqueeze(1).to_broadcast([P, CHUNK, CH]), ALU.add))
                marks.append(count[0])
            for i, ts in enumerate(chunks):
                xt = xres[:, ts, :]
                if n == 0:
                    dve.wait_ge(rs.sem, rs.at(i + 1))
                    dve.wait_ge(ex.sem, ex.at(2 * i + 2))
                    link(dve.scalar_tensor_tensor(xt, tmp[:, ts, :], 1.0, xt, ALU.subtract, ALU.add))
                if n == 1:
                    link(dve.tensor_tensor(xt, xt, z[:, ts, :], ALU.add))
                else:
                    link(dve.scalar_tensor_tensor(xt, z[:, ts, :], 0.0, xt, ALU.max, ALU.add))

        @block.scalar
        def _(act):
            if n == 0:
                for i, ts in enumerate(chunks):
                    act.wait_ge(lk.sem, lk.at(marks[i]))
                    act.activation(tmp[:, ts, :], acc[:, ts, acc0[0]:acc0[0] + CH], ACT.Relu, scale=-1.0).then_inc(ex.sem, 1)
                    act.wait_ge(ex.sem, ex.at(2 * i + 1))
                    act.activation(tmp[:, ts, :], tmp[:, ts, :], ACT.Exp, scale=-1.0).then_inc(ex.sem, 1)

        lk.base += count[0]
        ld.base += 16 * waits
        if n == 0:
            ex.base += 2 * len(chunks)
            rs.base += len(chunks)


def finish_last(nc, sig, sb, ps, A, K, convs, acc, acc0, out):
    N, T, LAST = K["N"], K["T"], K["LAST"]
    xres, hres, ident = K["xres"], K["hres"], K["ident"]
    names = ("den", "divided", "biased", "relus", "exps", "joined", "turned", "copied", "product", "evacuated")
    den_, divided, biased, relus, exps, joined, turned, copied, product, evacuated = [sig("last_" + name) for name in names]
    ld, st, rs, gate = sig("finish_loaded"), sig("stored"), sig("residual_added"), sig("residual_gate")
    with ExitStack() as c, nc.Block() as block:
        bias = sb("f_bias", [P, 3, CH], F32, c)
        wu = sb("f_wu", [P, 4, CH], F32, c)
        rden = sb("f_rden", [P, T, 12], F32, c)
        z = sb("f_z", [P, 2, 2 * CH], F32, c)
        pos = sb("f_pos", [P, 2, 2 * CH], F32, c)
        neg = sb("f_neg", [P, 2, 2 * CH], F32, c)
        cat = sb("f_cat", [P, 2, 2 * CH], F32, c)
        catT = sb("f_catT", [P, 2, 4, P], F32, c)
        pT = [ps(f"f_pT{j}", [P, 512], F32, c) for j in range(2)]
        pm = [ps(f"f_pm{j}", [P, 512], F32, c) for j in range(2)]

        @block.sync
        def _(sp):
            for k, name in enumerate(("L3_gnn_b1", "L3_gnn_b2", "L3_gnn_bu")):
                sp.dma_start(bias[:, k, :], A[name].rearrange("(a f) -> a f", a=1).to_broadcast([P, CH])).then_inc(ld.sem, 16)
            sp.dma_start(wu[:, :, :], A["L3_gnn_Wu"].rearrange("(k p) f -> p k f", p=P)).then_inc(ld.sem, 16)
            sp.wait_ge(ld.sem, ld.at(64))
            for t in range(0, T - 1, 6):
                sp.wait_ge(evacuated.sem, evacuated.at(t + 6))
                sp.dma_start(out[t * P:(t + 6) * P, :].rearrange("(t p) f -> p t f", p=P), xres[:, t:t + 6, :]).then_inc(st.sem, 16)
            sp.wait_ge(evacuated.sem, evacuated.at(T))
            sp.dma_start(out[(T - 1) * P:N, :], xres[0:LAST, T - 1, :]).then_inc(st.sem, 16)
            sp.wait_ge(st.sem, st.at(16 * ((T - 1) // 6 + 1)))

        @block.gpsimd
        def _(pool):
            pool.wait_ge(ld.sem, ld.at(64))
            with pool.Fori(0, T) as t:
                xt = xres[:, bass.ds(t, 1), :].rearrange("p a f -> p (a f)")
                pool.tensor_tensor(xt, xt, hres[:, bass.ds(t, 1), :].rearrange("p a f -> p (a f)"), ALU.add).then_inc(rs.sem, 1)
                pool.wait_ge(rs.sem, rs.at(1) + t * 2)
                pool.sem_inc(gate.sem, 1)
                pool.tensor_tensor(xt, xt, bias[:, 2, :], ALU.add).then_inc(rs.sem, 1)

        @block.vector
        def _(dve):
            for k, cv in enumerate(convs):
                den = acc[:, :, acc0[k] + CH:acc0[k] + CH + cv[1]]
                dve.tensor_scalar(den, den, 1e-16, None, ALU.add).then_inc(den_.sem, 1)
            for k, cv in enumerate(convs):
                dve.wait_ge(den_.sem, den_.at(k + 1))
                dve.reciprocal(rden[:, :, 4 * k:4 * k + cv[1]], acc[:, :, acc0[k] + CH:acc0[k] + CH + cv[1]]).then_inc(den_.sem, 1)
            dve.wait_ge(den_.sem, den_.at(4))
            dve.wait_ge(ld.sem, ld.at(64))

            def divide(t, par):
                if later(t, 2):
                    dve.wait_ge(relus.sem, relus.at(-2) + t * 2)
                for k, cv in enumerate(convs):
                    H = cv[1]
                    ins = dve.tensor_tensor(z[:, par, k * CH:(k + 1) * CH].rearrange("p (h c) -> p h c", h=H),
                                            acc[:, bass.ds(t, 1), acc0[k]:acc0[k] + CH].rearrange("p a (h c) -> p (a h) c", h=H),
                                            rden[:, bass.ds(t, 1), 4 * k:4 * k + H].rearrange("p a h -> p (a h)").unsqueeze(2).to_broadcast([P, H, CH // H]),
                                            ALU.mult)
                ins.then_inc(divided.sem, 1)
                dve.wait_ge(divided.sem, divided.at(1) + t)
                dve.tensor_tensor(z[:, par, :], z[:, par, :], bias[:, 0:2, :].rearrange("p k f -> p (k f)"), ALU.add).then_inc(biased.sem, 1)

            def join(t, par):
                dve.wait_ge(exps.sem, exps.at(1) + t)
                if later(t, 2):
                    dve.wait_ge(turned.sem, turned.at(-1) + t)
                dve.scalar_tensor_tensor(cat[:, par, :], neg[:, par, :], 1.0, pos[:, par, :], ALU.subtract, ALU.add).then_inc(joined.sem, 1)

            def add(t, par):
                dve.wait_ge(rs.sem, rs.at(2) + t * 2)
                dve.wait_ge(product.sem, product.at(1) + t)
                xt = xres[:, bass.ds(t, 1), :].rearrange("p a f -> p (a f)")
                dve.tensor_tensor(xt, xt, pm[par][:, 0:CH], ALU.add).then_inc(evacuated.sem, 1)
            staggered(dve, T, [(0, join), (-2, add), (2, divide)])

        @block.scalar
        def _(act):
            def activations(t, par):
                act.wait_ge(biased.sem, biased.at(1) + t)
                if later(t, 2):
                    act.wait_ge(joined.sem, joined.at(-1) + t)
                act.activation(neg[:, par, :], z[:, par, :], ACT.Relu, scale=-1.0).then_inc(relus.sem, 1)
                act.activation(pos[:, par, :], z[:, par, :], ACT.Relu).then_inc(relus.sem, 1)
                act.wait_ge(relus.sem, relus.at(2) + t * 2)
                act.activation(neg[:, par, :], neg[:, par, :], ACT.Exp, scale=-1.0).then_inc(exps.sem, 1)

            def copy(t, par):
                act.wait_ge(turned.sem, turned.at(1) + t)
                if later(t, 2):
                    act.wait_ge(product.sem, product.at(-1) + t)
                act.activation(catT[:, par, :, :], pT[par][:, :].rearrange("p (k q) -> p k q", k=4), ACT.Copy).then_inc(copied.sem, 1)
            staggered(act, T, [(2, activations), (0, copy)])

        @block.tensor
        def _(pe):
            pe.wait_ge(ld.sem, ld.at(64))

            def turn(t, par):
                pe.wait_ge(joined.sem, joined.at(1) + t)
                for k in range(4):
                    ins = pe.transpose(pT[par][:, k * P:(k + 1) * P], cat[:, par, k * P:(k + 1) * P], ident[:, :])
                ins.then_inc(turned.sem, 1)

            def multiply(t, par):
                pe.wait_ge(copied.sem, copied.at(1) + t)
                if later(t, 2):
                    pe.wait_ge(evacuated.sem, evacuated.at(-1) + t)
                for k in range(4):
                    ins = pe.matmul(pm[par][:, 0:CH], catT[:, par, k, :], wu[:, k, :], start=k == 0, stop=k == 3)
                ins.then_inc(product.sem, 1)
            staggered(pe, T, [(0, turn), (-1, multiply)])


_INS = ['x', 'src', 'dst', 'edge_weight', 'L0_gnn_W', 'L0_gnn_att_src', 'L0_gnn_att_dst', 'L0_gnn_bias', 'L1_gnn_W',
        'L1_gnn_attn_l', 'L1_gnn_attn_r', 'L2_gnn_W', 'L2_gnn_a_self', 'L2_gnn_a_neigh', 'L2_gnn_bias', 'L3_gnn_gamma',
        'L3_gnn_beta', 'L3_gnn_W1', 'L3_gnn_a_src1', 'L3_gnn_a_dst1', 'L3_gnn_b1', 'L3_gnn_W2', 'L3_gnn_a_src2',
        'L3_gnn_a_dst2', 'L3_gnn_b2', 'L3_gnn_Wu', 'L3_gnn_bu']
_OUTS = [((3125, 256), 'float32')]


def kernel(**inputs):
    import numpy as _np
    import concourse.bacc as _bacc
    from concourse import mybir as _mybir
    from concourse.bass_utils import run_bass_kernel_spmd as _run

    nc = _bacc.Bacc("TRN2", target_bir_lowering=False, num_devices=1)
    arrays, args = {}, {}
    for name in _INS:
        a = _np.ascontiguousarray(inputs[name])
        arrays[f"in_{name}_dram"] = a
        args[name] = nc.dram_tensor(f"in_{name}_dram", a.shape, _mybir.dt.from_np(a.dtype), kind="ExternalInput").ap()
    outs = []
    for i, (shape, dtype) in enumerate(_OUTS):
        dt = _mybir.dt.from_np(_np.dtype(dtype))
        outs.append(nc.dram_tensor(f"out_{i}_dram", shape, dt, kind="ExternalOutput").ap())
    build(nc, args, *outs)
    r = _run(nc, [arrays], core_ids=[0])
    got = tuple(r.results[0][f"out_{i}_dram"] for i in range(len(_OUTS)))
    return got[0]
```
